# Optimizing a Trainium2 kernel written in Bass

```python
import numpy as np
import jax
import jax.numpy as jnp

def _softmax(x, axis=-1):
    return jax.nn.softmax(x, axis=axis)

def _gelu(x):
    return jax.nn.gelu(x, approximate=True)

def _silu(x):
    return jax.nn.silu(x)

def _sigmoid(x):
    return jax.nn.sigmoid(x)

def _layernorm(x, axis=-1, eps=1e-05):
    m = jnp.mean(x, axis=axis, keepdims=True)
    v = jnp.var(x, axis=axis, keepdims=True)
    return (x - m) / jnp.sqrt(v + eps)

def _scatter_add(tgt, idx, src, axis=0):
    return tgt.at[idx].add(src)

def _segment_sum(src, seg, n):
    return jax.ops.segment_sum(src, seg, n)
kernel_name = 'mk_prb_d2_jaxref_r8_4c230c'

def setup_inputs(seed: int=0):
    np.random.seed(seed)
    _w = jnp.asarray

    def _L0_attn_setup():
        import jax, jax.numpy as jnp
        import numpy as np
        H, DK, DV = (16, 64, 64)
        LN_EPS = 1e-05
        key = jax.random.key(seed)
        ks = jax.random.split(key, 5)
        B, N, D = (4, 512, 128)
        s = 1.0 / np.sqrt(D)
        return {'inputs': jax.random.normal(ks[0], (B, N, D), dtype=jnp.float32), 'W_Q': jax.random.normal(ks[1], (D, H * DK), dtype=jnp.float32) * s, 'W_K': jax.random.normal(ks[2], (D, H * DK), dtype=jnp.float32) * s, 'W_V': jax.random.normal(ks[3], (D, H * DV), dtype=jnp.float32) * s, 'W_fc': jax.random.normal(ks[4], (H * DV, D), dtype=jnp.float32) * s, 'gamma': jnp.ones((D,), dtype=jnp.float32), 'beta': jnp.zeros((D,), dtype=jnp.float32)}
    _L0_attn_in = _L0_attn_setup()

    def _L0_ffn_setup():
        import jax, jax.numpy as jnp
        import numpy as np
        H = 128
        I = 256
        E = 8
        B, S = (2, 128)

        def _swiglu(x, wg, wu, wd):
            return jax.nn.silu(x @ wg) * (x @ wu) @ wd
        key = jax.random.key(seed)
        ks = jax.random.split(key, 8)
        sc_h = 1.0 / np.sqrt(H)
        sc_i = 1.0 / np.sqrt(I)
        return {'hidden_states': jax.random.normal(ks[0], (B, S, H), jnp.float32), 'gate_w': jax.random.normal(ks[1], (H, E), jnp.float32) * sc_h, 'sh_gate': jax.random.normal(ks[2], (H, I), jnp.float32) * sc_h, 'sh_up': jax.random.normal(ks[3], (H, I), jnp.float32) * sc_h, 'sh_down': jax.random.normal(ks[4], (I, H), jnp.float32) * sc_i, 'rt_gate': jax.random.normal(ks[5], (E, H, I), jnp.float32) * sc_h, 'rt_up': jax.random.normal(ks[6], (E, H, I), jnp.float32) * sc_h, 'rt_down': jax.random.normal(ks[7], (E, I, H), jnp.float32) * sc_i}
    _L0_ffn_in = _L0_ffn_setup()

    def _L1_attn_setup():
        import jax, jax.numpy as jnp
        import numpy as np
        D = 128
        H = 16
        G = 4
        HD = D // H
        HPG = H // G
        THETA = 10000.0
        EPS = 1e-10

        def _l2_qk_norm(t):
            return t / (jnp.sqrt(jnp.sum(t * t, axis=-1, keepdims=True)) + EPS)

        def _rope(t):
            T = t.shape[1]
            half = HD // 2
            inv_freq = 1.0 / THETA ** (jnp.arange(half, dtype=jnp.float32) / half)
            ang = jnp.arange(T, dtype=jnp.float32)[:, None] * inv_freq[None, :]
            cos = jnp.cos(ang)[None, :, None, :]
            sin = jnp.sin(ang)[None, :, None, :]
            x1, x2 = (t[..., :half], t[..., half:])
            return jnp.concatenate([x1 * cos - x2 * sin, x2 * cos + x1 * sin], axis=-1)
        key = jax.random.key(seed)
        k1, k2, k3 = jax.random.split(key, 3)
        x = jax.random.normal(k1, (1, 512, D), jnp.float32)
        w_qkv = jax.random.normal(k2, (D, H * HD + 2 * G * HD), jnp.float32) * 0.02
        w_o = jax.random.normal(k3, (D, D), jnp.float32) * 0.02
        return {'x': x, 'w_qkv': w_qkv, 'w_o': w_o}
    _L1_attn_in = _L1_attn_setup()

    def _L1_ffn_setup():
        import jax, jax.numpy as jnp
        import numpy as np
        B, S, D = (4, 128, 128)
        E, K = (8, 2)
        H = 2 * D
        key = jax.random.key(seed)
        ks = jax.random.split(key, 5)
        x = jax.random.normal(ks[0], (B, S, D), dtype=jnp.float32)
        Wg = jax.random.normal(ks[1], (E, D), dtype=jnp.float32) * 0.02
        W1 = jax.random.normal(ks[2], (E, H, D), dtype=jnp.float32) * 0.02
        W2 = jax.random.normal(ks[3], (E, H, D), dtype=jnp.float32) * 0.02
        W3 = jax.random.normal(ks[4], (E, D, H), dtype=jnp.float32) * 0.02
        return {'x': x, 'Wg': Wg, 'W1': W1, 'W2': W2, 'W3': W3}
    _L1_ffn_in = _L1_ffn_setup()
    _d = {'L0_attn_inputs': _L0_attn_in['inputs'], 'L0_attn_W_Q': _L0_attn_in['W_Q'], 'L0_attn_W_K': _L0_attn_in['W_K'], 'L0_attn_W_V': _L0_attn_in['W_V'], 'L0_attn_W_fc': _L0_attn_in['W_fc'], 'L0_attn_gamma': _L0_attn_in['gamma'], 'L0_attn_beta': _L0_attn_in['beta'], 'L0_ffn_gate_w': _L0_ffn_in['gate_w'], 'L0_ffn_sh_gate': _L0_ffn_in['sh_gate'], 'L0_ffn_sh_up': _L0_ffn_in['sh_up'], 'L0_ffn_sh_down': _L0_ffn_in['sh_down'], 'L0_ffn_rt_gate': _L0_ffn_in['rt_gate'], 'L0_ffn_rt_up': _L0_ffn_in['rt_up'], 'L0_ffn_rt_down': _L0_ffn_in['rt_down'], 'L1_attn_w_qkv': _L1_attn_in['w_qkv'], 'L1_attn_w_o': _L1_attn_in['w_o'], 'L1_ffn_Wg': _L1_ffn_in['Wg'], 'L1_ffn_W1': _L1_ffn_in['W1'], 'L1_ffn_W2': _L1_ffn_in['W2'], 'L1_ffn_W3': _L1_ffn_in['W3']}
    _x0 = _d['L0_attn_inputs']
    _d['L0_attn_inputs'] = jax.random.normal(jax.random.fold_in(jax.random.key(seed), 1), (4, 512, 128), dtype=_x0.dtype)
    del _x0
    return _d

def reference(L0_attn_inputs, L0_attn_W_Q, L0_attn_W_K, L0_attn_W_V, L0_attn_W_fc, L0_attn_gamma, L0_attn_beta, L0_ffn_gate_w, L0_ffn_sh_gate, L0_ffn_sh_up, L0_ffn_sh_down, L0_ffn_rt_gate, L0_ffn_rt_up, L0_ffn_rt_down, L1_attn_w_qkv, L1_attn_w_o, L1_ffn_Wg, L1_ffn_W1, L1_ffn_W2, L1_ffn_W3):

    def _L0_attn_ref(inputs, W_Q, W_K, W_V, W_fc, gamma, beta):
        import jax, jax.numpy as jnp
        import numpy as np
        H, DK, DV = (16, 64, 64)
        LN_EPS = 1e-05
        B, N, D = inputs.shape
        Q = jax.nn.sigmoid((inputs @ W_Q).reshape(B, N, H, DK))
        K = jax.nn.sigmoid((inputs @ W_K).reshape(B, N, H, DK))
        V = (inputs @ W_V).reshape(B, N, H, DV)
        KV = jnp.einsum('bnhk,bnhv->bhkv', K, V)
        num = jnp.einsum('bnhk,bhkv->bnhv', Q, KV)
        k_sum = K.sum(axis=1)
        den = jnp.einsum('bnhk,bhk->bnh', Q, k_sum)[..., None] + 1e-08
        out = (num / den).reshape(B, N, H * DV) @ W_fc
        x = out + inputs
        mu = x.mean(axis=-1, keepdims=True)
        var = jnp.mean((x - mu) ** 2, axis=-1, keepdims=True)
        return (x - mu) * jax.lax.rsqrt(var + LN_EPS) * gamma + beta

    def _L0_ffn_ref(hidden_states, gate_w, sh_gate, sh_up, sh_down, rt_gate, rt_up, rt_down):
        import jax, jax.numpy as jnp
        import numpy as np
        H = 128
        I = 256
        E = 8
        B, S = (2, 128)

        def _swiglu(x, wg, wu, wd):
            return jax.nn.silu(x @ wg) * (x @ wu) @ wd
        b, s, h = hidden_states.shape
        x = hidden_states.reshape(-1, h)
        logits = x @ gate_w
        top_val = jnp.max(logits, axis=-1, keepdims=True)
        top_id = jnp.argmax(logits, axis=-1)
        score = jax.nn.sigmoid(top_val)
        xs = x * score
        g = jnp.einsum('th,ehi->eti', xs, rt_gate)
        u = jnp.einsum('th,ehi->eti', xs, rt_up)
        act = jax.nn.silu(g) * u
        y = jnp.einsum('eti,eih->eth', act, rt_down)
        onehot = jax.nn.one_hot(top_id, E, dtype=x.dtype)
        routed = jnp.einsum('eth,te->th', y, onehot)
        shared = _swiglu(x, sh_gate, sh_up, sh_down)
        return (shared + routed).reshape(b, s, h)

    def _L1_attn_ref(x, w_qkv, w_o):
        import jax, jax.numpy as jnp
        import numpy as np
        D = 128
        H = 16
        G = 4
        HD = D // H
        HPG = H // G
        THETA = 10000.0
        EPS = 1e-10

        def _l2_qk_norm(t):
            return t / (jnp.sqrt(jnp.sum(t * t, axis=-1, keepdims=True)) + EPS)

        def _rope(t):
            T = t.shape[1]
            half = HD // 2
            inv_freq = 1.0 / THETA ** (jnp.arange(half, dtype=jnp.float32) / half)
            ang = jnp.arange(T, dtype=jnp.float32)[:, None] * inv_freq[None, :]
            cos = jnp.cos(ang)[None, :, None, :]
            sin = jnp.sin(ang)[None, :, None, :]
            x1, x2 = (t[..., :half], t[..., half:])
            return jnp.concatenate([x1 * cos - x2 * sin, x2 * cos + x1 * sin], axis=-1)
        B, T, _ = x.shape
        qkv = x @ w_qkv
        q, k, v = jnp.split(qkv, [H * HD, H * HD + G * HD], axis=-1)
        q = q.reshape(B, T, H, HD)
        k = k.reshape(B, T, G, HD)
        v = v.reshape(B, T, G, HD)
        q = _l2_qk_norm(q)
        k = _l2_qk_norm(k)
        q = _rope(q)
        k = _rope(k)
        k = jnp.repeat(k, HPG, axis=2)
        v = jnp.repeat(v, HPG, axis=2)
        q = jnp.transpose(q, (0, 2, 1, 3))
        k = jnp.transpose(k, (0, 2, 1, 3))
        v = jnp.transpose(v, (0, 2, 1, 3))
        scale = 1.0 / np.sqrt(HD).astype(np.float32)
        scores = jnp.einsum('bhqd,bhkd->bhqk', q, k) * scale
        causal = jnp.tril(jnp.ones((T, T), dtype=bool))
        scores = jnp.where(causal[None, None], scores, jnp.float32(-1e+30))
        attn = jax.nn.softmax(scores, axis=-1)
        out = jnp.einsum('bhqk,bhkd->bhqd', attn, v)
        out = jnp.transpose(out, (0, 2, 1, 3)).reshape(B, T, H * HD)
        return out @ w_o

    def _L1_ffn_ref(x, Wg, W1, W2, W3):
        import jax, jax.numpy as jnp
        import numpy as np
        B, S, D = (4, 128, 128)
        E, K = (8, 2)
        H = 2 * D
        gate_out = jnp.einsum('bsd,ed->bse', x, Wg)
        top_v, top_i = jax.lax.top_k(gate_out, K)
        probs = jax.nn.softmax(top_v, axis=-1)
        out = jnp.zeros_like(x)
        for e in range(E):
            w_e = jnp.sum(probs * (top_i == e), axis=-1)
            h1 = jnp.einsum('bsd,hd->bsh', x, W1[e])
            h2 = jnp.einsum('bsd,hd->bsh', x, W2[e])
            g = h1 * jax.nn.sigmoid(h1) * h2
            y = jnp.einsum('bsh,dh->bsd', g, W3[e])
            out = out + y * w_e[..., None]
        return out
    x = L0_attn_inputs
    xn = _layernorm(x, axis=-1)
    x = x + _L0_attn_ref(xn, L0_attn_W_Q, L0_attn_W_K, L0_attn_W_V, L0_attn_W_fc, L0_attn_gamma, L0_attn_beta) + _L0_ffn_ref(xn, L0_ffn_gate_w, L0_ffn_sh_gate, L0_ffn_sh_up, L0_ffn_sh_down, L0_ffn_rt_gate, L0_ffn_rt_up, L0_ffn_rt_down)
    xn = _layernorm(x, axis=-1)
    x = x + _L1_attn_ref(xn, L1_attn_w_qkv, L1_attn_w_o) + _L1_ffn_ref(xn, L1_ffn_Wg, L1_ffn_W1, L1_ffn_W2, L1_ffn_W3)
    return x

_drawn_inputs = setup_inputs


def setup_inputs(seed=0):
    import zlib

    import numpy as np

    out = dict(_drawn_inputs(seed))
    spreads = {'L0_attn_gamma': (1.0, 0.2), 'L0_attn_beta': (0.0, 0.1)}
    factors = {'L0_attn_W_Q': 8.0,
     'L0_attn_W_K': 8.0,
     'L1_attn_w_qkv': 8.0,
     'L1_attn_w_o': 8.0,
     'L1_ffn_Wg': 8.0,
     'L1_ffn_W1': 8.0,
     'L1_ffn_W2': 8.0,
     'L1_ffn_W3': 8.0}
    for name, (base, spread) in spreads.items():
        noise = np.random.default_rng([zlib.crc32(name.encode()), seed]).standard_normal(out[name].shape)
        drawn = base * np.exp(spread * noise) if base else spread * noise
        out[name] = jnp.asarray(drawn.astype(out[name].dtype))
    for name, factor in factors.items():
        out[name] = (out[name] * factor).astype(out[name].dtype)
    return out
```

```python
import concourse.bass as bass
from concourse import mybir
from concourse.alu_op_type import AluOpType as ALU
from contextlib import ExitStack
import numpy as np

F32 = mybir.dt.float32
BF16 = mybir.dt.bfloat16
I32 = mybir.dt.int32
ACT = mybir.ActivationFunctionType
AX = mybir.AxisListType

P = 128
D = 128
B, N = 4, 512
CPB = N // P
C = B * CPB
E = 8
I = 256
LN_EPS = 1e-5

H0, DK = 16, 64
PAIRS = H0 * DK // P
DEN_EPS = 1e-8

H1, G1, HD = 16, 4, 8
HPG = H1 // G1
NQK = H1 + G1
NORM_EPS = 1e-10
TERMS = 8
VW = 32
MASKED = -1e30
EW = 2 * I + 2 * D

NB0 = C + E - 1
NB1 = 2 * C + E - 1
DEPTH = 4

K_ID, K_TRI, K_MASK, K_REV = 0, 128, 256, 384
K_M128 = K_REV + E
K_J = K_M128 + C
K_CC = K_J + NB1
K_SS = K_CC + CPB * NQK * HD
K_SEL = K_SS + CPB * NQK * HD
K_END = K_SEL + PAIRS * P


def constants():
    k = np.zeros((P, K_END), np.float32)
    i = np.arange(P)
    k[:, K_ID:K_ID + P] = i[:, None] == i[None, :]
    k[:, K_TRI:K_TRI + P] = i[:, None] < i[None, :]
    k[:, K_MASK:K_MASK + P] = np.where(i[:, None] > i[None, :], np.float32(MASKED), 0)
    for p in range(PAIRS):
        for half in range(2):
            for part in range(3):
                col = K_SEL + p * P + half * DK
                k[32 * part + 2 * p + half, col:col + DK] = 1
    k[:, K_REV:K_REV + E] = E - np.arange(E)
    k[:, K_M128:K_M128 + C] = P * np.arange(C)
    k[:, K_J:K_J + NB1] = np.arange(NB1)
    half = HD // 2
    inv = (np.float32(1) / np.float32(10000) ** (np.arange(half, dtype=np.float32) / np.float32(half))).astype(np.float32)
    chunk_of = [c for c in range(CPB) for _ in range(H1)] + [c for c in range(CPB) for _ in range(G1)]
    for n, c in enumerate(chunk_of):
        ang = (np.arange(c * P, (c + 1) * P, dtype=np.float32)[:, None] * inv).astype(np.float32)
        cos, sin = np.cos(ang), np.sin(ang)
        k[:, K_CC + n * HD:K_CC + (n + 1) * HD] = np.concatenate([cos, cos], 1)
        k[:, K_SS + n * HD:K_SS + (n + 1) * HD] = np.concatenate([-sin, sin], 1)
    return k


def build(nc, x_d, wq_d, wk_d, wvT_d, wfc_d, gamma_d, beta_d, gate_d, shg_d, shu_d, shd_d,
          experts0_d, wqkv_d, wo_d, wgT_d, experts1_d, const_d, out_d):
    ctx = ExitStack()

    def sb(name, shape, dt=F32):
        return ctx.enter_context(nc.sbuf_tensor(name, shape, dt))

    def sem(name):
        return ctx.enter_context(nc.semaphore(name))

    with ctx:
        const = sb("const", [P, K_SEL])
        ident = const[:, K_ID:K_ID + P]
        identb = sb("identb", [P, P], BF16)
        trib = sb("trib", [P, P], BF16)
        onesb = sb("onesb", [P, P], BF16)
        maskb = sb("maskb", [P, P], BF16)
        selb = sb("selb", [96, PAIRS, P], BF16)
        zero = sb("zero", [P, D])
        gamma = sb("gamma", [P, D])
        beta = sb("beta", [P, D])

        x = sb("x", [P, C, D])
        xn = sb("xn", [P, C, D + 1])
        xnT = sb("xnT", [P, B * N])
        xs = sb("xs", [P, C, D])
        experts = sb("experts", [P, E * EW])
        gate = sb("gate", [P, E])
        wg1 = sb("wg1", [P, E])
        shgu = sb("shgu", [P, 2, I])
        shdn = sb("shdn", [P, 2, D])
        wqkv = sb("wqkv", [P, 192])
        wo = sb("wo", [P, D])

        arenaA = sb("arenaA", [P, 12288])
        Ks = arenaA[:, 0:4096].rearrange("p (c k) -> p c k", c=CPB)
        QT = arenaA[:, 4096:12288].rearrange("p (t u n) -> p t u n", t=2, n=N)
        wvT = arenaA[:, 8192:9216].rearrange("p (u d) -> p u d", d=D)
        wfc = arenaA[:, 9216:10240].rearrange("p (u d) -> p u d", d=D)
        pT = arenaA[:, 0:4096].rearrange("p (r n) -> p r n", n=1024)
        qT = arenaA[:, 4096:8192].bitcast(BF16).rearrange("p (t u n) -> p t u n", t=2, n=N)
        kT = arenaA[:, 8192:10240].bitcast(BF16).rearrange("p (t g n) -> p t g n", t=2, n=N)
        yg2 = arenaA[:, 10240:12288].rearrange("p (c d) -> p c d", d=D)

        arenaB = sb("arenaB", [P, 7168])
        wq = arenaB[:, 0:1024]
        wk = arenaB[:, 1024:2048]
        wvf = arenaB[:, 2048:4096].rearrange("p (e u d) -> p e u d", e=2, d=D)
        xk = arenaB[:, 4096:5120].rearrange("p (u d) -> p u d", d=D)
        xkT = arenaB[:, 5120:6144]
        kvw = arenaB[:, 6144:7168].rearrange("p (u d) -> p u d", d=D)
        qk = arenaB[:, 0:640]
        tA = arenaB[:, 640:1280]
        tB = arenaB[:, 1280:1920]
        qpack = arenaB[:, 2048:4096].bitcast(BF16).rearrange("p (h t d) -> p h t d", t=TERMS, d=HD)
        kpack = arenaB[:, 4096:5120].bitcast(BF16).rearrange("p (h r t d) -> p h r t d", r=2, t=TERMS, d=HD)
        s1 = arenaB[:, 5120:5440].bitcast(BF16)
        s2 = arenaB[:, 5440:5760].bitcast(BF16)
        s3 = arenaB[:, 5760:6080].bitcast(BF16)
        ao = arenaB[:, 6144:6656].rearrange("p (c n) -> p c n", n=D)
        aoT = arenaB[:, 6656:7168]

        arenaC = sb("arenaC", [P, 3072])
        selector = arenaC[0:96, 0:PAIRS * P]
        shsg = arenaC[:, 0:1024].rearrange("p (a n) -> p a n", n=N)
        shact = arenaC[:, 1024:3072].rearrange("p (t a n) -> p t a n", t=2, n=N)
        v9 = arenaC[:, 0:2048].rearrange("p (c g w) -> p c g w", c=C, w=VW)
        osb = arenaC[:, 2048:3072].rearrange("p (t n) -> p t n", n=N)

        ksB = sb("ksB", [P, PAIRS * H0])
        dsb = sb("dsb", [H0, N])
        rr = sb("rr", [H0, N])
        mid = sb("mid", [H0, N], BF16)
        rd3 = sb("rd3", [96, N], BF16)
        zt = sb("zt", [P, CPB, D])

        xb = sb("xb", [P, DEPTH, D])
        xbT = sb("xbT", [P, 2, P])
        sg = sb("sg", [P, 2, I])
        act = sb("act", [P, 2, I])
        aT = sb("aT", [P, 2, I])
        yb = sb("yb", [P, DEPTH, D])

        st = sb("st", [P, C, 6])
        mv = sb("mv", [P, C, 2])
        nv = sb("nv", [P, 80])
        ny = sb("ny", [P, 80])
        nt = sb("nt", [P, 80])
        lg = sb("lg", [P, C, E])
        oh = [sb(f"oh{i}", [P, C, E]) for i in range(2)]
        ohb = sb("ohb", [P, C, E], BF16)
        ra = sb("ra", [P, C, E])
        rb = sb("rb", [P, C, E])
        tot = sb("tot", [P, C, E])
        pos = sb("pos", [P, C, E])
        top = [sb(f"top{i}", [P, C]) for i in range(2)]
        first = sb("first", [P, C])
        rsum = sb("rsum", [P, CPB * HPG])
        wide = sb("wide", [P, NB1 * E])
        nblk = sb("nblk", [P, E])
        bend = [sb(f"bend{i}", [P, E]) for i in range(2)]
        slotf = sb("slotf", [P, C])
        bef = sb("bef", [1, NB1])
        score = sb("score", [P, C])
        wts = [sb(f"wts{i}", [P, C]) for i in range(2)]
        slot = [sb(f"slot{i}", [P, C], I32) for i in range(3)]
        bexp = [sb(f"bexp{i}", [1, n], I32) for i, n in enumerate((NB0, NB1))]

        ps = ctx.enter_context(nc.psum_tensor("ps", [P, 8, 512], F32))

        def bank(i):
            return ps[:, i, :]

        def pair_banks(n):
            return ps[:, 2 * (n % 2):2 * (n % 2) + 2, :]

        NB = (NB0, NB1)
        xs_dr = [nc.dram_tensor(f"sorted_x{l}", [NB[l] * P, D], F32, kind="Internal").ap() for l in range(2)]
        y_dr = [nc.dram_tensor(f"sorted_y{l}", [NB[l] * P, D], F32, kind="Internal").ap() for l in range(2)]

        x_in = [sem(f"x_in{b}") for b in range(B)]
        const_in = sem("const_in")
        sel_in = sem("sel_in")
        gate_in = sem("gate_in")
        wvf_in = sem("wvf_in")
        wk_in = sem("wk_in")
        wq_in = sem("wq_in")
        affine_in = sem("affine_in")
        experts_in = [sem(f"experts_in{l}") for l in range(2)]
        shared_in = sem("shared_in")
        layer1_in = sem("layer1_in")
        zeroed = [sem(f"zeroed{l}") for l in range(2)]
        zero_set = sem("zero_set")
        pool_set = sem("pool_set")
        chain = sem("chain")
        casts = sem("casts")
        xn_done = [sem(f"xn_done{l}") for l in range(2)]
        xnT_ps = [sem(f"xnT_ps{l}") for l in range(2)]
        xnT_done = [sem(f"xnT_done{l}") for l in range(2)]
        logits = [sem(f"logits{l}") for l in range(2)]
        onehot = [sem(f"onehot{l}") for l in range(2)]
        ranks = [sem(f"ranks{l}") for l in range(2)]
        routed = [sem(f"routed{l}") for l in range(2)]
        top_set = sem("top_set")
        score_set = sem("score_set")
        xs_set = sem("xs_set")
        scattered = [sem(f"scattered{l}") for l in range(2)]
        gathered = [sem(f"gathered{l}") for l in range(2)]
        unit_ps = sem("unit_ps")
        unit_out = sem("unit_out")
        xk_ps, xk_out = sem("xk_ps"), sem("xk_out")
        xkT_ps, xkT_out = sem("xkT_ps"), sem("xkT_out")
        den_ps, rd3_set = sem("den_ps"), sem("rd3_set")
        kvw_ps, kvw_out = sem("kvw_ps"), sem("kvw_out")
        bc_ps, qs_set = sem("bc_ps"), sem("qs_set")
        y_ps, y_out = sem("y_ps"), sem("y_out")
        sh_ps, sh_sig, sh_act = sem("sh_ps"), sem("sh_sig"), sem("sh_act")
        shy_ps, shy_out = sem("shy_ps"), sem("shy_out")
        blk = [{n: sem(f"b{l}_{n}") for n in ("xT", "xbT", "gu", "sg", "m", "act", "aTp", "aT", "y", "yb")}
               | {n: [sem(f"b{l}_{n}{r}") for r in range(DEPTH)] for n in ("ld", "st")} for l in range(2)]
        qkv_ps, qkv_out = sem("qkv_ps"), sem("qkv_out")
        packed = sem("packed")
        tr_ps, tr_out = sem("tr_ps"), sem("tr_out")
        s_ps, p_set, pv_done = sem("s_ps"), sem("p_set"), sem("pv_done")
        o_out = sem("o_out")
        ot_ps, ao_set = sem("ot_ps"), sem("ao_set")
        aoT_ps, aoT_out = sem("aoT_ps"), sem("aoT_out")
        wo_ps, wo_out = sem("wo_ps"), sem("wo_out")
        fin, stored = sem("fin"), sem("stored")

        TILES = [
            [(0, 0, 0, 0), (1, 0, 1, 0)],
            [(2, 0, 0, 0), (3, 0, 1, 0)],
            [(0, 1, 0, 0), (0, 3, 0, 384), (1, 1, 1, 0), (1, 3, 1, 384)],
            [(2, 1, 0, 0), (2, 3, 0, 384), (3, 1, 1, 0), (3, 3, 1, 384)],
            [(0, 2, 0, 0), (2, 2, 0, 256), (1, 2, 1, 0), (3, 2, 1, 256)],
        ]
        NT = len(TILES)
        GROUPS = B * G1
        PIECES = {(0, 1): 0, (0, 3): 1, (2, 0): 2, (2, 2): 3, (2, 4): 4, (3, 0): 5, (3, 2): 6, (3, 3): 7}
        NPIECE = len(PIECES)
        BLOCKS_AFTER = 3 * G1

        def block_dmas(sp, l):
            s, n = blk[l], NB[l]

            def load(it, r):
                t = it * DEPTH + r
                sp.dma_start(xb[:, r % DEPTH, :], xs_dr[l][bass.ts(t, P), :]).then_inc(s["ld"][r % DEPTH], 16)

            def store(it, r):
                t = it * DEPTH + r
                sp.wait_ge(s["yb"], t + 3)
                sp.dma_start(y_dr[l][bass.ts(t, P), :], yb[:, r % DEPTH, :]).then_inc(s["st"][r % DEPTH], 16)

            for q in s["st"]:
                sp.sem_inc(q, 16)
            sp.wait_ge(scattered[l], 16 * C * (l + 1))
            for t in range(DEPTH):
                load(0, t)
            for k in range(3):
                sp.wait_ge(s["xT"], k + 1)
                load(1, k)
            with sp.Fori(0, (n - 7) // DEPTH) as it:
                for r in range(DEPTH):
                    sp.wait_ge(s["xT"], it * DEPTH + (4 + r))
                    load(it, 7 + r)
                    store(it, r)
            for t in range(n - 7, n):
                store(0, t)
            for r, q in enumerate(s["st"]):
                sp.wait_ge(q, 16 * (1 + len(range(r, n, DEPTH))))

        def o_evac(sc, gi):
            sc.wait_ge(pv_done, (gi + 1) * NT)
            if gi >= 2:
                sc.wait_ge(ot_ps, gi - 1)
            nc.scalar.activation(osb[:, gi % 2, :], bank(4 + gi % 2), ACT.Copy).then_inc(o_out, 1)

        def ao_evac(sc, b):
            sc.wait_ge(aoT_ps, b + 1)
            if b >= 1:
                sc.wait_ge(wo_ps, b)
            nc.scalar.activation(aoT, bank(6), ACT.Copy).then_inc(aoT_out, 1)

        def block_acts(sc, l):
            s, n = blk[l], NB[l]

            def x_evac(it, r):
                sc.wait_ge(s["xT"], it * DEPTH + (r + 1))
                nc.scalar.activation(xbT[:, r % 2, :], bank(r % 2)[:, 0:P], ACT.Copy).then_inc(s["xbT"], 1)

            def sigmoid(it, r):
                sc.wait_ge(s["gu"], it * DEPTH + (r + 1))
                nc.scalar.activation(sg[:, r % 2, :], bank(2 + r % 2)[:, 0:I], ACT.Sigmoid).then_inc(s["sg"], 1)

            def a_evac(it, r):
                sc.wait_ge(s["aTp"], it * DEPTH + (r + 1))
                nc.scalar.activation(aT[:, r % 2, :], bank(4 + r % 2)[:, 0:I], ACT.Copy).then_inc(s["aT"], 1)

            sc.sem_inc(s["aT"], 1)
            x_evac(0, 0)
            x_evac(0, 1)
            sigmoid(0, 0)
            x_evac(0, 2)
            sigmoid(0, 1)
            a_evac(0, 0)
            with sc.Fori(0, (n - 3) // DEPTH) as it:
                for r in range(DEPTH):
                    t = it * DEPTH + (2 + r)
                    sc.wait_ge(s["gu"], t)
                    x_evac(it, 3 + r)
                    sc.wait_ge(s["act"], t - 1)
                    sigmoid(it, 2 + r)
                    sc.wait_ge(s["y"], t - 1)
                    a_evac(it, 1 + r)
            t = n - 1
            sc.wait_ge(s["act"], t - 1)
            sigmoid(0, t)
            sc.wait_ge(s["y"], t - 1)
            a_evac(0, t - 1)
            sc.wait_ge(s["y"], t)
            a_evac(0, t)

        def block_matmuls(pe, l):
            s, n = blk[l], NB[l]

            at = {}

            def find_experts(t0):
                _, values = nc.values_load_multi_w_load_instructions(
                    bexp[l][0:1, t0:min(t0 + 4, n)], engines=(mybir.EngineType.PE,), min_val=0, max_val=(E - 1) * EW,
                    skip_runtime_bounds_check_because="route() counts at most E - 1 experts")
                for k, value in enumerate(values):
                    at[t0 + k] = value

            def x_transpose(t):
                pe.wait_ge(s["ld"][t % DEPTH], 16 * (t // DEPTH + 1))
                if t >= 2:
                    pe.wait_ge(s["xbT"], t - 1)
                nc.tensor.transpose(bank(t % 2)[:, 0:P], xb[:, t % DEPTH, :], ident).then_inc(s["xT"], 1)

            def gate_up(t):
                pe.wait_ge(s["xbT"], t + 1)
                if t >= 2:
                    pe.wait_ge(s["act"], t - 1)
                nc.tensor.matmul(bank(2 + t % 2), xbT[:, t % 2, :], experts[:, bass.ds(at[t], 2 * I)],
                                 start=True, stop=True).then_inc(s["gu"], 1)

            def a_transposes(t):
                pe.wait_ge(s["act"], t + 1)
                if t >= 2:
                    pe.wait_ge(s["aT"], t)
                for a in range(2):
                    last = nc.tensor.transpose(bank(4 + t % 2)[:, a * P:(a + 1) * P], act[:, t % 2, a * P:(a + 1) * P], ident)
                last.then_inc(s["aTp"], 1)

            def down(t):
                pe.wait_ge(s["aT"], t + 2)
                pe.wait_ge(s["yb"], t + 1)
                for a in range(2):
                    last = nc.tensor.matmul(bank(6 + t % 2)[:, 0:D], aT[:, t % 2, a * P:(a + 1) * P],
                                            experts[:, bass.ds(at[t] + (2 * I + a * D), D)],
                                            start=(a == 0), stop=(a == 1))
                last.then_inc(s["y"], 1)

            pe.wait_ge(experts_in[l], 16)
            pe.wait_ge(routed[l], 1)
            pe.sem_inc(s["y"], 1)
            find_experts(0)
            x_transpose(0)
            for t in range(n + 2):
                if t % 4 == 3 and t + 1 < n:
                    find_experts(t + 1)
                if t + 1 < n:
                    x_transpose(t + 1)
                if t < n:
                    gate_up(t)
                if t >= 2:
                    down(t - 2)
                if 1 <= t <= n:
                    a_transposes(t - 1)

        def shared_add(v, b):
            v.wait_ge(shy_ps, b + 1)
            xb4 = x[:, b * CPB:(b + 1) * CPB, :]
            nc.vector.tensor_tensor(xb4, xb4, bank(4 + b % 2).rearrange("p (c d) -> p c d", c=CPB),
                                    ALU.add).then_inc(shy_out, 1)

        def block_vectors(v, l):
            s, n = blk[l], NB[l]
            V = nc.vector

            def activate(it, r):
                t = it * DEPTH + r
                v.wait_ge(s["sg"], t + 1)
                gu = bank(2 + r % 2)
                V.tensor_tensor(act[:, r % 2, :], sg[:, r % 2, :], gu[:, 0:I], ALU.mult).then_inc(s["m"], 1)
                v.wait_ge(s["m"], t + 1)
                V.tensor_tensor(act[:, r % 2, :], act[:, r % 2, :], gu[:, I:2 * I], ALU.mult).then_inc(s["act"], 1)

            def take_y(it, r):
                t = it * DEPTH + r
                v.wait_ge(s["y"], t + 2)
                v.wait_ge(s["st"][r % DEPTH], (it + r // DEPTH + 1) * 16)
                V.tensor_copy(yb[:, r % DEPTH, :], bank(6 + r % 2)[:, 0:D]).then_inc(s["yb"], 1)

            activate(0, 0)
            activate(0, 1)
            with v.Fori(0, (n - 3) // DEPTH) as it:
                for r in range(DEPTH):
                    v.wait_ge(s["aTp"], it * DEPTH + (1 + r))
                    activate(it, 2 + r)
                    take_y(it, r)
            v.wait_ge(s["aTp"], n - 2)
            activate(0, n - 1)
            for t in range(n - 3, n):
                take_y(0, t)

        blkctx = ctx.enter_context(nc.Block())

        @blkctx.sync
        def _(sp):
            for b in range(B):
                sp.dma_start(x[:, b * CPB:(b + 1) * CPB, :],
                             x_d[b].rearrange("(c p) d -> p c d", p=P)).then_inc(x_in[b], 16)
            sp.dma_start(gate[:], gate_d).then_inc(gate_in, 16)
            sp.dma_start(wk, wk_d).then_inc(wk_in, 16)
            sp.dma_start(wq, wq_d).then_inc(wq_in, 16)
            sp.wait_ge(zero_set, 1)
            for l in range(2):
                sp.dma_start(xs_dr[l].rearrange("(n p) d -> p n d", p=P),
                             zero[:, :].rearrange("p (a d) -> p a d", a=1).broadcast_to([P, NB[l], D])
                             ).then_inc(zeroed[l], 16)
            sp.dma_start(experts[:], experts0_d).then_inc(experts_in[0], 16)
            sp.dma_start(shgu[:, 0, :], shg_d).then_inc(shared_in, 16)
            sp.dma_start(shgu[:, 1, :], shu_d).then_inc(shared_in, 16)
            sp.dma_start(shdn[:], shd_d.rearrange("(a p) d -> p a d", p=P)).then_inc(shared_in, 16)
            sp.dma_start(wqkv[:], wqkv_d).then_inc(layer1_in, 16)
            sp.dma_start(wo[:], wo_d).then_inc(layer1_in, 16)
            sp.dma_start(wg1[:], wgT_d).then_inc(layer1_in, 16)
            block_dmas(sp, 0)
            sp.wait_ge(blk[0]["y"], NB0 + 1)
            sp.dma_start(experts[:], experts1_d).then_inc(experts_in[1], 16)
            block_dmas(sp, 1)
            for b in range(B):
                sp.wait_ge(fin, b + 1)
                sp.dma_start(out_d[b].rearrange("(c p) d -> p c d", p=P),
                             x[:, b * CPB:(b + 1) * CPB, :]).then_inc(stored, 16)
            sp.wait_ge(stored, 16 * B)

        @blkctx.gpsimd
        def _(pool):
            nc.gpsimd.memset(zero[:], 0.0).then_inc(zero_set, 1)
            nc.gpsimd.memset(xn[:, :, D:D + 1], 1.0).then_inc(pool_set, 1)
            nc.gpsimd.memset(ksB[:], 0.0).then_inc(pool_set, 1)
            nc.gpsimd.memset(rd3[:], 0.0).then_inc(pool_set, 1)
            nc.gpsimd.memset(onesb[:], 1.0).then_inc(pool_set, 1)

            def scatter(l, k, src):
                for c in range(C):
                    pool.indirect_dma_start(
                        out=xs_dr[l][:, :], out_offset=bass.IndirectOffsetOnAxis(slot[l + k][:, c:c + 1], 0),
                        in_=src(c), in_offset=None).then_inc(scattered[l], 16)

            def gather(l, k, dst):
                for c in range(C):
                    pool.indirect_dma_start(
                        out=dst(c), out_offset=None, in_=y_dr[l][:, :],
                        in_offset=bass.IndirectOffsetOnAxis(slot[l + k][:, c:c + 1], 0)).then_inc(gathered[l], 16)

            def stored_blocks(l):
                for r, q in enumerate(blk[l]["st"]):
                    pool.wait_ge(q, 16 * (1 + len(range(r, NB[l], DEPTH))))

            pool.wait_ge(zeroed[0], 16)
            pool.wait_ge(routed[0], 1)
            pool.wait_ge(xs_set, 1)
            scatter(0, 0, lambda c: xs[:, c, :])
            pool.wait_ge(scattered[0], 16 * C)
            stored_blocks(0)
            gather(0, 0, lambda c: xs[:, c, :])
            pool.wait_ge(shy_ps, B)
            nc.gpsimd.memset(v9[:, :, :, HD:VW], 0.0).then_inc(pool_set, 1)
            pool.wait_ge(pool_set, 5)
            nc.gpsimd.memset(v9[:, :, :, HD:HD + 1], 1.0).then_inc(pool_set, 1)
            pool.wait_ge(zeroed[1], 16)
            pool.wait_ge(routed[1], 1)
            for k in range(2):
                scatter(1, k, lambda c: xn[:, c, 0:D])
            stored_blocks(1)
            gather(1, 0, lambda c: xs[:, c, :])
            gather(1, 1, lambda c: yg2[:, c, :])

        @blkctx.scalar
        def _(sc):
            sc.dma_start(const[:], const_d[:, 0:K_SEL]).then_inc(const_in, 16)
            sc.dma_start(selector, const_d[0:96, K_SEL:K_END]).then_inc(sel_in, 16)
            sc.dma_start(wvT, wvT_d.rearrange("(u q) d -> q u d", q=P)).then_inc(wvf_in, 16)
            sc.dma_start(wfc, wfc_d.rearrange("(u q) d -> q u d", q=P)).then_inc(wvf_in, 16)
            sc.dma_start(gamma[:], gamma_d.rearrange("(a d) -> a d", a=1).broadcast_to([P, D])).then_inc(affine_in, 16)
            sc.dma_start(beta[:], beta_d.rearrange("(a d) -> a d", a=1).broadcast_to([P, D])).then_inc(affine_in, 16)

            def xnT_evac(l):
                for b in range(B):
                    sc.wait_ge(xnT_ps[l], b + 1)
                    nc.scalar.activation(xnT[:, b * N:(b + 1) * N], bank(4 + b % 2), ACT.Copy).then_inc(xnT_done[l], 1)

            unit_n = [0]

            def unit(dst, fn):
                n = unit_n[0]
                unit_n[0] += 1
                sc.wait_ge(unit_ps, n + 1)
                nc.scalar.activation(dst, pair_banks(n), fn).then_inc(unit_out, 1)

            def proj_unit(b, i):
                if i < CPB:
                    unit(Ks[:, i, :].rearrange("p (a n) -> p a n", a=2), ACT.Sigmoid)
                else:
                    u = 2 * (i - CPB)
                    unit(QT[:, b % 2, u:u + 2, :], ACT.Sigmoid)

            xnT_evac(0)
            unit(wvf[:, 0].rearrange("p (a u) d -> p a (u d)", a=2), ACT.Copy)
            unit(wvf[:, 1].rearrange("p (a u) d -> p a (u d)", a=2), ACT.Copy)
            for i in range(8):
                proj_unit(0, i)
                if i == 3:
                    sc.wait_ge(top_set, 1)
                    nc.scalar.activation(score[:], top[0][:], ACT.Sigmoid).then_inc(score_set, 1)
            for b in range(B):
                more = b + 1 < B

                def units(lo, hi):
                    for i in range(lo, hi):
                        if more:
                            if i == 0:
                                sc.wait_ge(xk_ps, b + 1)
                            if i == CPB and b >= 1:
                                sc.wait_ge(y_ps, b)
                            proj_unit(b + 1, i)

                units(0, 2)
                sc.wait_ge(xkT_ps, b + 1)
                if b >= 1:
                    sc.wait_ge(kvw_ps, b)
                nc.scalar.activation(xkT.rearrange("p (a n) -> p a n", a=2), ps[:, 4:6, :], ACT.Copy).then_inc(xkT_out, 1)
                units(2, 3)
                sc.wait_ge(kvw_ps, b + 1)
                if b >= 1:
                    sc.wait_ge(y_ps, b)
                nc.scalar.activation(kvw.rearrange("p (a u) d -> p a (u d)", a=2), ps[:, 4:6, :], ACT.Copy).then_inc(kvw_out, 1)
                units(3, 8)

            block_acts(sc, 0)

            for n in range(2 * B):
                sc.wait_ge(sh_ps, n + 1)
                if n >= 2:
                    sc.wait_ge(sh_act, n - 1)
                nc.scalar.activation(shsg[:, n % 2, :], ps[:, 2 * (n % 2), :], ACT.Sigmoid).then_inc(sh_sig, 1)

            xnT_evac(1)
            sc.wait_ge(top_set, 2)
            nc.scalar.activation(wts[1][:], wts[1][:], ACT.Exp).then_inc(score_set, 1)

            for gi in range(GROUPS):
                b, g = divmod(gi, G1)
                if gi == BLOCKS_AFTER:
                    block_acts(sc, 1)
                for t in range(NT):
                    n = gi * NT + t
                    if gi >= 1 and t == 1 and gi != BLOCKS_AFTER:
                        o_evac(sc, gi - 1)
                    if gi >= 1 and g == 0 and t == 4:
                        ao_evac(sc, b - 1)
                    sc.wait_ge(s_ps, n + 1)
                    if n >= 4:
                        sc.wait_ge(pv_done, n - 3)
                    nc.scalar.activation(pT[:, n % 4, :].rearrange("p (a n) -> p a n", a=2), pair_banks(n),
                                         ACT.Exp, scale=float(1.0 / np.sqrt(np.float32(HD)))).then_inc(p_set, 1)
                if gi + 1 in (BLOCKS_AFTER, GROUPS):
                    o_evac(sc, gi)
            ao_evac(sc, B - 1)

        @blkctx.tensor
        def _(pe):
            def x_transposes(l):
                for b in range(B):
                    pe.wait_ge(xn_done[l], b + 1)
                    if b >= 2:
                        pe.wait_ge(xnT_done[l], b - 1)
                    for i in range(CPB):
                        last = nc.tensor.transpose(bank(4 + b % 2)[:, i * P:(i + 1) * P], xn[:, b * CPB + i, 0:D], ident)
                    last.then_inc(xnT_ps[l], 1)
                    if b >= 1:
                        router(l, b - 1)
                router(l, B - 1)

            def router(l, b):
                pe.wait_ge(xnT_done[l], b + 1)
                for c in range(b * CPB, (b + 1) * CPB):
                    last = nc.tensor.matmul(bank(6)[:, c * E:(c + 1) * E], xnT[:, c * P:(c + 1) * P],
                                            (gate, wg1)[l][:], start=True, stop=True)
                last.then_inc(logits[l], 1)

            def count_ranks(l):
                pe.wait_ge(onehot[l], 1)
                rhs = ohb[:].rearrange("p c e -> p (c e)")
                nc.tensor.matmul(bank(7)[:, 0:C * E], trib[:], rhs, start=True, stop=True)
                nc.tensor.matmul(bank(7)[:, C * E:2 * C * E], onesb[:], rhs, start=True, stop=True).then_inc(ranks[l], 1)

            unit_n = [0]

            def unit_begin():
                n = unit_n[0]
                if n >= 2:
                    pe.wait_ge(unit_out, n - 1)
                unit_n[0] += 1
                return pair_banks(n)

            def proj_unit(b, i):
                dst = unit_begin()
                if i < CPB:
                    c = b * CPB + i
                    for a in range(2):
                        last = nc.tensor.matmul(dst[:, a, :], xnT[:, c * P:(c + 1) * P], wk[:, a * 512:(a + 1) * 512],
                                                start=True, stop=True)
                else:
                    for a in range(2):
                        u = 2 * (i - CPB) + a
                        last = nc.tensor.matmul(dst[:, a, :], wq[:, u * P:(u + 1) * P], xnT[:, b * N:(b + 1) * N],
                                                start=True, stop=True)
                last.then_inc(unit_ps, 1)

            pe.wait_ge(const_in, 16)
            pe.wait_ge(gate_in, 16)
            x_transposes(0)
            pe.wait_ge(wvf_in, 32)
            for par in range(2):
                dst = unit_begin()
                rows = slice(DK * par, DK * par + DK)
                for u in range(PAIRS):
                    last = nc.tensor.matmul(dst[:, u // 4, (u % 4) * D:(u % 4 + 1) * D], wvT[rows, u, :], wfc[rows, u, :],
                                            start=True, stop=True)
                last.then_inc(unit_ps, 1)
            pe.wait_ge(wk_in, 16)
            pe.wait_ge(wq_in, 16)
            pe.wait_ge(casts, 1)
            pe.wait_ge(pool_set, 4)
            for i in range(8):
                proj_unit(0, i)
                if i == 1:
                    count_ranks(0)
            for b in range(B):
                more = b + 1 < B

                def units(lo, hi):
                    for i in range(lo, hi):
                        if more:
                            proj_unit(b + 1, i)

                pe.wait_ge(unit_out, 2 + 8 * b + CPB)
                if b >= 1:
                    pe.wait_ge(y_out, b)
                    pe.wait_ge(qs_set, 8 * b)
                else:
                    pe.wait_ge(xnT_done[0], B)
                    pe.wait_ge(onehot[0], 1)
                for u in range(PAIRS):
                    dst = ps[:, 4 + u // 3, (u % 3) * (D + 1):(u % 3 + 1) * (D + 1)]
                    for i in range(CPB):
                        last = nc.tensor.matmul(dst, Ks[:, i, u * P:(u + 1) * P], xn[:, b * CPB + i, :],
                                                start=(i == 0), stop=(i == CPB - 1))
                last.then_inc(xk_ps, 1)
                units(0, 2)
                pe.wait_ge(xk_out, b + 1)
                pe.wait_ge(unit_out, 2 + 8 * b + 8)
                if b == 0:
                    pe.wait_ge(routed[0], 1)
                for u in range(PAIRS):
                    last = nc.tensor.matmul(bank(7)[0:H0, :], ksB[:, u * H0:(u + 1) * H0], QT[:, b % 2, u, :],
                                            start=(u == 0), stop=(u == PAIRS - 1))
                last.then_inc(den_ps, 1)
                for u in range(PAIRS):
                    last = nc.tensor.transpose(ps[:, 4 + u // 4, (u % 4) * P:(u % 4 + 1) * P], xk[:, u, :], ident)
                last.then_inc(xkT_ps, 1)
                units(2, 3)
                pe.wait_ge(xkT_out, b + 1)
                for h in range(H0):
                    u, par = divmod(h, 2)
                    last = nc.tensor.matmul(ps[DK * par:DK * par + DK, 4 + u // 4, (u % 4) * D:(u % 4 + 1) * D],
                                            xkT[:, h * DK:(h + 1) * DK], wvf[:, par, u, :], start=True, stop=True)
                last.then_inc(kvw_ps, 1)
                units(3, 6)
                pe.wait_ge(rd3_set, b + 1)
                for u in range(PAIRS):
                    if u >= 2:
                        pe.wait_ge(qs_set, 8 * b + u - 1)
                    nc.tensor.matmul(bank(6 + u % 2), selb[:, u, :], rd3[:], start=True, stop=True).then_inc(bc_ps, 1)
                    if u == 3:
                        units(6, 7)
                units(7, 8)
                pe.wait_ge(kvw_out, b + 1)
                pe.wait_ge(qs_set, 8 * (b + 1))
                for i in range(CPB):
                    for u in range(PAIRS):
                        last = nc.tensor.matmul(bank(4)[:, i * D:(i + 1) * D], QT[:, b % 2, u, i * P:(i + 1) * P],
                                                kvw[:, u, :], start=(u == 0), stop=(u == PAIRS - 1))
                last.then_inc(y_ps, 1)

            pe.wait_ge(unit_out, 2 + 8 * B)
            pe.wait_ge(y_out, B)
            block_matmuls(pe, 0)

            pe.wait_ge(shared_in, 48)
            pe.wait_ge(blk[0]["xbT"], NB0)
            pe.wait_ge(blk[0]["act"], NB0)
            pe.wait_ge(blk[0]["aT"], NB0 + 1)

            def sh_down(b):
                pe.wait_ge(sh_act, 2 * b + 2)
                if b >= 2:
                    pe.wait_ge(shy_out, b - 1)
                for i in range(CPB):
                    for a in range(2):
                        last = nc.tensor.matmul(bank(4 + b % 2)[:, i * D:(i + 1) * D], shact[:, b % 2, a, i * P:(i + 1) * P],
                                                shdn[:, a, :], start=(a == 0), stop=(a == 1))
                last.then_inc(shy_ps, 1)

            for b in range(B):
                for a in range(2):
                    n = 2 * b + a
                    if n >= 2:
                        pe.wait_ge(sh_act, n - 1)
                    for k in range(2):
                        last = nc.tensor.matmul(pair_banks(n)[:, k, :], shgu[:, k, a * P:(a + 1) * P],
                                                xnT[:, b * N:(b + 1) * N], start=True, stop=True)
                    last.then_inc(sh_ps, 1)
                if b >= 1:
                    sh_down(b - 1)
            sh_down(B - 1)

            pe.wait_ge(layer1_in, 48)
            pe.wait_ge(shy_out, B)
            pe.wait_ge(blk[0]["yb"], NB0 + 2)
            x_transposes(1)
            count_ranks(1)

            def piece(b, i):
                if b == 0 and i == 0:
                    pe.wait_ge(routed[1], 1)
                if i < 2:
                    if b >= 1 or i == 1:
                        pe.wait_ge(qkv_out, 2 * b + i)
                    if b >= 1 and i == 0:
                        pe.wait_ge(tr_out, 6 * b)
                    for k in range(2):
                        c = b * CPB + 2 * i + k
                        last = nc.tensor.matmul(bank(7)[:, k * 192:(k + 1) * 192], xnT[:, c * P:(c + 1) * P], wqkv[:],
                                                start=True, stop=True)
                    last.then_inc(qkv_ps, 1)
                    return
                j = i - 2
                if j == 0:
                    pe.wait_ge(packed, b + 1)
                else:
                    pe.wait_ge(tr_out, 6 * b + j)
                dst = bank(7).bitcast(BF16)
                if j < CPB:
                    for u in range(H1 // 2):
                        last = nc.tensor.transpose(dst[:, u * P:(u + 1) * P],
                                                   qpack[:, j * H1 + 2 * u:j * H1 + 2 * u + 2].rearrange("p h t d -> p (h t d)"), identb[:])
                else:
                    for k in range(2):
                        for g in range(G1):
                            last = nc.tensor.transpose(dst[:, (k * G1 + g) * P:(k * G1 + g + 1) * P],
                                                       kpack[:, (2 * (j - CPB) + k) * G1 + g].rearrange("p r t d -> p (r t d)"),
                                                       identb[:])
                last.then_inc(tr_ps, 1)

            def score_tile(n):
                gi, t = divmod(n, NT)
                b, g = divmod(gi, G1)
                if t == 0 and g == 0:
                    pe.wait_ge(tr_out, 6 * (b + 1))
                if n >= 2:
                    pe.wait_ge(p_set, n - 1)
                for hh, kc, bk, col in TILES[t]:
                    h = g * HPG + hh
                    rows = slice(64 * (h % 2), 64 * (h % 2) + 64)
                    w = N - kc * P
                    dst = pair_banks(n)[:, bk, :]
                    nc.tensor.matmul(dst[:, col:col + w], kT[rows, b % 2, g, kc * P:(kc + 1) * P],
                                     qT[rows, b % 2, h // 2, kc * P:N], start=True, stop=False)
                    last = nc.tensor.matmul(dst[:, col:col + P], identb[:], maskb[:], start=False, stop=True)
                last.then_inc(s_ps, 1)

            def pv_tile(n):
                gi, t = divmod(n, NT)
                b, g = divmod(gi, G1)
                pe.wait_ge(p_set, n + 1)
                if t == 0 and gi >= 2:
                    pe.wait_ge(o_out, gi - 1)
                for hh, kc, bk, col in TILES[t]:
                    w = N - kc * P
                    last = nc.tensor.matmul(bank(4 + gi % 2)[VW * hh:VW * hh + VW, kc * P:N], v9[:, b * CPB + kc, g, :],
                                            pT[:, n % 4, bk * 512 + col:bk * 512 + col + w],
                                            start=(t < 2), stop=(t == NT - 1))
                last.then_inc(pv_done, 1)

            def o_transposes(gi):
                pe.wait_ge(o_out, gi + 1)
                if gi % G1 == 0 and gi >= G1:
                    pe.wait_ge(wo_out, gi // G1)
                elif gi >= 1:
                    pe.wait_ge(ao_set, gi)
                for i in range(CPB):
                    last = nc.tensor.transpose(bank(6)[:, i * P:(i + 1) * P], osb[:, gi % 2, i * P:(i + 1) * P], ident)
                last.then_inc(ot_ps, 1)

            def ao_transposes(b):
                pe.wait_ge(ao_set, (b + 1) * G1)
                for i in range(CPB):
                    last = nc.tensor.transpose(bank(6)[:, i * P:(i + 1) * P], ao[:, i, :], ident)
                last.then_inc(aoT_ps, 1)

            def wo_matmuls(b):
                pe.wait_ge(aoT_out, b + 1)
                for i in range(CPB):
                    last = nc.tensor.matmul(bank(6)[:, i * D:(i + 1) * D], aoT[:, i * P:(i + 1) * P], wo[:],
                                            start=True, stop=True)
                last.then_inc(wo_ps, 1)

            for i in range(NPIECE):
                piece(0, i)
            pe.wait_ge(pool_set, 6)
            score_tile(0)
            for gi in range(GROUPS):
                b, g = divmod(gi, G1)
                for t in range(NT):
                    n = gi * NT + t
                    if n + 1 < GROUPS * NT and (n + 1) % (BLOCKS_AFTER * NT) != 0:
                        score_tile(n + 1)
                    pv_tile(n)
                    if gi >= 1 and t == 1:
                        o_transposes(gi - 1)
                    if g == 0 and b >= 1 and t == 3:
                        ao_transposes(b - 1)
                    if g == 1 and b >= 1 and t == 0:
                        wo_matmuls(b - 1)
                    if b + 1 < B and (g, t) in PIECES:
                        piece(b + 1, PIECES[(g, t)])
                if gi + 1 == BLOCKS_AFTER:
                    pe.wait_ge(p_set, BLOCKS_AFTER * NT)
                    pe.wait_ge(o_out, BLOCKS_AFTER)
                    pe.wait_ge(ao_set, BLOCKS_AFTER - 1)
                    pe.wait_ge(tr_out, 6 * B)
                    block_matmuls(pe, 1)
                    pe.wait_ge(blk[1]["xbT"], NB1)
                    pe.wait_ge(blk[1]["act"], NB1)
                    pe.wait_ge(blk[1]["aT"], NB1 + 1)
                    pe.wait_ge(blk[1]["yb"], NB1 + 2)
                    score_tile(n + 1)
            o_transposes(GROUPS - 1)
            ao_transposes(B - 1)
            wo_matmuls(B - 1)

        @blkctx.vector
        def _(v):
            count = [0]

            def tick(ins):
                count[0] += 1
                ins.then_inc(chain, 1)

            def sync():
                v.wait_ge(chain, count[0])

            def link(ins):
                tick(ins)
                sync()

            V = nc.vector

            def rsqrt(n):
                a, y, t = nv[:, 0:n], ny[:, 0:n], nt[:, 0:n]
                link(V.tensor_scalar(t.bitcast(I32), a.bitcast(I32), 1, None, ALU.logical_shift_right))
                link(V.tensor_scalar(y.bitcast(I32), t.bitcast(I32), -1.0, float(0x5f3759df), ALU.mult, ALU.add))
                for _ in range(3):
                    link(V.scalar_tensor_tensor(out=t, in0=y, scalar=-0.5, in1=a, op0=ALU.mult, op1=ALU.mult))
                    link(V.tensor_tensor(t, t, y, ALU.mult))
                    link(V.scalar_tensor_tensor(out=y, in0=t, scalar=1.5, in1=y, op0=ALU.add, op1=ALU.mult))

            def normalise(src, dst, n, done=None):
                for i in range(n):
                    tick(V.bn_stats(st[:, i, :], src(i)))
                sync()
                for i in range(n):
                    tick(V.bn_aggr(mv[:, i, :], st[:, i, :]))
                sync()
                link(V.tensor_scalar(nv[:, 0:n], mv[:, 0:n, 1], LN_EPS, None, ALU.add))
                rsqrt(n)
                for i in range(n):
                    last = V.tensor_scalar(dst(i), src(i), mv[:, i, 0:1], ny[:, i:i + 1], ALU.subtract, ALU.mult)
                    if done is not None and i == n - 1:
                        last.then_inc(done, 1)
                    else:
                        tick(last)
                sync()

            CE = [P, C, E]

            def column(a):
                return a[:].rearrange("p (c o) -> p c o", o=1).broadcast_to(CE)

            rev = const[:, K_REV:K_REV + E].rearrange("p (o e) -> p o e", o=1).broadcast_to(CE)

            def best(src, k):
                link(V.tensor_reduce(top[k][:], src[:], AX.X, ALU.max))
                link(V.tensor_tensor(ra[:], src[:], column(top[k]), ALU.is_equal))
                link(V.tensor_tensor(ra[:], ra[:], rev, ALU.mult))
                link(V.tensor_reduce(first[:], ra[:], AX.X, ALU.max))
                link(V.tensor_tensor(oh[k][:], rev, column(first), ALU.is_equal))

            def route(l):
                choices = l + 1
                v.wait_ge(logits[l], B)
                link(V.tensor_copy(lg[:].rearrange("p c e -> p (c e)"), bank(6)[:, 0:C * E]))
                best(lg, 0)
                if l == 0:
                    V.tensor_copy(ohb[:], oh[0][:]).then_inc(onehot[0], 1)
                    V.tensor_copy(slotf[:], top[0][:]).then_inc(top_set, 1)
                else:
                    link(V.scalar_tensor_tensor(out=rb[:].rearrange("p c e -> p (c e)"), in0=oh[0][:].rearrange("p c e -> p (c e)"),
                                                scalar=-3e38, in1=lg[:].rearrange("p c e -> p (c e)"),
                                                op0=ALU.mult, op1=ALU.add))
                    best(rb, 1)
                    V.tensor_tensor(ohb[:], oh[0][:], oh[1][:], ALU.add).then_inc(onehot[1], 1)
                    V.tensor_tensor(wts[1][:], top[1][:], top[0][:], ALU.subtract).then_inc(top_set, 1)
                v.wait_ge(ranks[l], 1)
                link(V.tensor_copy(tot[:].rearrange("p c e -> p (c e)"), bank(7)[:, C * E:2 * C * E]))
                src, dst = tot, ra
                sh = 1
                while sh < C:
                    tick(V.tensor_copy(dst[:, 0:sh, :], src[:, 0:sh, :]))
                    link(V.tensor_tensor(dst[:, sh:C, :], src[:, sh:C, :], src[:, 0:C - sh, :], ALU.add))
                    src, dst = dst, (rb if dst is ra else ra)
                    sh *= 2
                cum, free = src, dst
                w16 = wide[:, 0:E * C].rearrange("p (e m) -> p e m", e=E)
                cnt = cum[:, C - 1, :].rearrange("p (e o) -> p e o", o=1).broadcast_to([P, E, C])
                m128 = const[:, K_M128:K_M128 + C].rearrange("p (o m) -> p o m", o=1).broadcast_to([P, E, C])
                link(V.tensor_tensor(w16, cnt, m128, ALU.is_gt))
                link(V.tensor_reduce(nblk[:], w16, AX.X, ALU.add))
                a, c = nblk, bend[0]
                for sh in (1, 2, 4):
                    tick(V.tensor_copy(c[:, 0:sh], a[:, 0:sh]))
                    link(V.tensor_tensor(c[:, sh:E], a[:, sh:E], a[:, 0:E - sh], ALU.add))
                    a, c = c, (bend[1] if c is bend[0] else bend[0])
                ends, starts = a, c
                link(V.tensor_tensor(starts[:], ends[:], nblk[:], ALU.subtract))
                link(V.tensor_scalar(starts[:], starts[:], float(P), None, ALU.mult))
                link(V.tensor_tensor(free[:], cum[:], tot[:], ALU.subtract))
                link(V.tensor_tensor(free[:], free[:], starts[:].rearrange("p (o e) -> p o e", o=1).broadcast_to(CE), ALU.add))
                link(V.tensor_tensor(pos[:].rearrange("p c e -> p (c e)"), bank(7)[:, 0:C * E],
                                     free[:].rearrange("p c e -> p (c e)"), ALU.add))
                nb = NB[l]
                wj = wide[0:1, 0:nb * (E - 1)].rearrange("p (j e) -> p j e", j=nb)
                jj = const[0:1, K_J:K_J + nb].rearrange("p (j o) -> p j o", o=1).broadcast_to([1, nb, E - 1])
                en = ends[0:1, 0:E - 1].rearrange("p (o e) -> p o e", o=1).broadcast_to([1, nb, E - 1])
                link(V.tensor_tensor(wj, jj, en, ALU.is_ge))
                link(V.tensor_reduce(bef[:, 0:nb], wj, AX.X, ALU.add))
                link(V.tensor_scalar(bexp[l][:], bef[:, 0:nb], float(EW), None, ALU.mult))
                if l == 0:
                    v.wait_ge(score_set, 1)
                for k in range(choices):
                    link(V.tensor_tensor(ra[:], oh[k][:], pos[:], ALU.mult))
                    link(V.tensor_reduce(first[:], ra[:], AX.X, ALU.add))
                    last = V.tensor_copy(slot[l + k][:], first[:])
                    if k < choices - 1:
                        link(last)
                last.then_inc(routed[l], 1)

            v.wait_ge(const_in, 16)
            tick(V.tensor_copy(identb[:], ident))
            tick(V.tensor_copy(trib[:], const[:, K_TRI:K_TRI + P]))
            tick(V.tensor_copy(maskb[:], const[:, K_MASK:K_MASK + P]))
            v.wait_ge(sel_in, 16)
            V.tensor_copy(selb[:].rearrange("p u d -> p (u d)"), selector).then_inc(casts, 1)
            for l in range(2):
                v.sem_inc(blk[l]["yb"], 2)

            for b in range(B):
                v.wait_ge(x_in[b], 16)
                normalise(lambda i: x[:, b * CPB + i, :], lambda i: xn[:, b * CPB + i, 0:D], CPB, xn_done[0])
            route(0)
            v.wait_ge(xn_done[0], B)
            V.tensor_tensor(xs[:], xn[:, :, 0:D], score[:].rearrange("p (c o) -> p c o", o=1).broadcast_to([P, C, D]),
                            ALU.mult).then_inc(xs_set, 1)

            v.wait_ge(pool_set, 3)
            for b in range(B):
                v.wait_ge(xk_ps, b + 1)
                if b >= 1:
                    v.wait_ge(den_ps, b)
                    v.wait_ge(xkT_ps, b)
                for k in range(3):
                    u0, m = 3 * k, min(3, PAIRS - 3 * k)
                    src = bank(4 + k)[:, 0:m * (D + 1)].rearrange("p (u n) -> p u n", u=m)
                    for par in range(2):
                        rows = slice(DK * par, DK * par + DK)
                        c0 = u0 * (H0 + 2) + par
                        tick(V.tensor_copy(ksB[rows, c0:c0 + (m - 1) * (H0 + 2) + 1:H0 + 2], src[rows, :, D]))
                    last = V.tensor_copy(xk[:, u0:u0 + m, :], src[:, :, 0:D])
                    if k < 2:
                        tick(last)
                last.then_inc(xk_out, 1)
                sync()
                v.wait_ge(den_ps, b + 1)
                link(V.tensor_scalar(dsb[:], bank(7)[0:H0, :], DEN_EPS, None, ALU.add))
                link(V.reciprocal(rr[:], dsb[:]))
                if b >= 1:
                    v.wait_ge(bc_ps, 8 * b)
                link(V.tensor_copy(rd3[0:H0, :], rr[:]))
                link(V.tensor_tensor(dsb[:], rr[:], rd3[0:H0, :], ALU.subtract))
                link(V.tensor_copy(mid[:], dsb[:]))
                tick(V.tensor_copy(rd3[32:32 + H0, :], mid[:]))
                link(V.tensor_tensor(rr[:], dsb[:], mid[:], ALU.subtract))
                V.tensor_copy(rd3[64:64 + H0, :], rr[:]).then_inc(rd3_set, 1)
                for u in range(PAIRS):
                    v.wait_ge(bc_ps, 8 * b + u + 1)
                    V.tensor_tensor(QT[:, b % 2, u, :], QT[:, b % 2, u, :], bank(6 + u % 2), ALU.mult).then_inc(qs_set, 1)
                v.wait_ge(y_ps, b + 1)
                V.tensor_tensor(zt[:], bank(4).rearrange("p (c d) -> p c d", c=CPB),
                                xn[:, b * CPB:(b + 1) * CPB, 0:D], ALU.add).then_inc(y_out, 1)
                v.wait_ge(y_out, b + 1)
                normalise(lambda i: zt[:, i, :], lambda i: zt[:, i, :], CPB)
                if b == 0:
                    v.wait_ge(affine_in, 32)
                g4 = gamma[:].rearrange("p (o d) -> p o d", o=1).broadcast_to([P, CPB, D])
                b4 = beta[:].rearrange("p (o d) -> p o d", o=1).broadcast_to([P, CPB, D])
                xb4 = x[:, b * CPB:(b + 1) * CPB, :]
                link(V.tensor_tensor(zt[:], zt[:], g4, ALU.mult))
                tick(V.tensor_tensor(xb4, xb4, b4, ALU.add))
                sync()
                link(V.tensor_tensor(xb4, xb4, zt[:], ALU.add))

            block_vectors(v, 0)

            for n in range(2 * B):
                b, a = divmod(n, 2)
                v.wait_ge(sh_sig, n + 1)
                if b >= 2:
                    v.wait_ge(shy_ps, b - 1)
                link(V.tensor_tensor(shact[:, b % 2, a, :], shsg[:, a, :], pair_banks(n)[:, 0, :], ALU.mult))
                V.tensor_tensor(shact[:, b % 2, a, :], shact[:, b % 2, a, :], pair_banks(n)[:, 1, :],
                                ALU.mult).then_inc(sh_act, 1)
                if a == 1 and b >= 1:
                    shared_add(v, b - 1)
            shared_add(v, B - 1)
            v.wait_ge(shy_out, B)

            v.wait_ge(gathered[0], 16 * C)
            for b in range(B):
                xb4 = x[:, b * CPB:(b + 1) * CPB, :]
                link(V.tensor_tensor(xb4, xb4, xs[:, b * CPB:(b + 1) * CPB, :], ALU.add))
                normalise(lambda i: x[:, b * CPB + i, :], lambda i: xn[:, b * CPB + i, 0:D], CPB, xn_done[1])
            route(1)

            def take_qkv(b, i):
                v.wait_ge(qkv_ps, 2 * b + i + 1)
                src = bank(7)[:, 0:2 * 192].rearrange("p (c n) -> p c n", c=2)
                tick(V.tensor_copy(qk[:, i * 256:(i + 1) * 256].rearrange("p (c n) -> p c n", c=2), src[:, :, 0:128]))
                tick(V.tensor_copy(qk[:, 512 + i * 64:512 + (i + 1) * 64].rearrange("p (c n) -> p c n", c=2),
                                   src[:, :, 128:160]))
                c0 = b * CPB + 2 * i
                for k in range(2):
                    last = V.tensor_copy(v9[:, c0 + k, :, 0:HD], src[:, k, 160:192].rearrange("p (g d) -> p g d", g=G1))
                    if k == 0:
                        tick(last)
                last.then_inc(qkv_out, 1)

            def heads(a):
                return a.rearrange("p (h d) -> p h d", d=HD)

            def pack(b):
                sync()
                nn = CPB * NQK
                link(V.tensor_tensor(tA, qk, qk, ALU.mult))
                link(V.tensor_reduce(nv[:, 0:nn], heads(tA), AX.X, ALU.add))
                rsqrt(nn)
                link(V.tensor_tensor(nt[:, 0:nn], nv[:, 0:nn], ny[:, 0:nn], ALU.mult))
                link(V.tensor_scalar(nt[:, 0:nn], nt[:, 0:nn], NORM_EPS, None, ALU.add))
                link(V.reciprocal(ny[:, 0:nn], nt[:, 0:nn]))
                link(V.tensor_tensor(heads(qk), heads(qk),
                                     ny[:, 0:nn].rearrange("p (h o) -> p h o", o=1).broadcast_to([P, nn, HD]), ALU.mult))
                cc, ss = const[:, K_CC:K_CC + nn * HD], const[:, K_SS:K_SS + nn * HD]
                hf = HD // 2
                tick(V.tensor_tensor(tA, qk, cc, ALU.mult))
                tick(V.tensor_tensor(heads(tB)[:, :, 0:hf], heads(qk)[:, :, hf:HD], heads(ss)[:, :, 0:hf], ALU.mult))
                link(V.tensor_tensor(heads(tB)[:, :, hf:HD], heads(qk)[:, :, 0:hf], heads(ss)[:, :, hf:HD], ALU.mult))
                link(V.tensor_tensor(tA, tA, tB, ALU.add))
                link(V.tensor_copy(s1, tA))
                link(V.tensor_tensor(tB, tA, s1, ALU.subtract))
                link(V.tensor_copy(s2, tB))
                link(V.tensor_tensor(tA, tB, s2, ALU.subtract))
                link(V.tensor_copy(s3, tA))
                nq = CPB * H1
                if b >= 1:
                    v.wait_ge(tr_ps, 6 * b)
                for part, t0, t1 in ((s1, 0, 3), (s2, 3, 6), (s3, 6, 8)):
                    src = part[:, 0:nq * HD].rearrange("p (h o d) -> p h o d", o=1, d=HD).broadcast_to([P, nq, t1 - t0, HD])
                    tick(V.tensor_copy(qpack[:, :, t0:t1, :], src))
                for j, part in enumerate((s1, s2, s3)):
                    src = part[:, nq * HD:].rearrange("p (h o d) -> p h o d", o=1, d=HD)
                    m = len(range(j, TERMS, 3))
                    tick(V.tensor_copy(kpack[:, :, 0, j:TERMS:3, :], src.broadcast_to([P, CPB * G1, m, HD])))
                sync()
                V.tensor_copy(kpack[:, :, 1].rearrange("p h t d -> p h (t d)"),
                              kpack[:, :, 0].rearrange("p h t d -> p h (t d)")).then_inc(packed, 1)

            def take_transposed(b, j):
                v.wait_ge(tr_ps, 6 * b + j + 1)
                if j == 0 and b >= 2:
                    v.wait_ge(s_ps, (b - 1) * G1 * NT)
                src = bank(7).bitcast(BF16)
                if j < CPB:
                    V.tensor_copy(qT[:, b % 2, :, j * P:(j + 1) * P],
                                  src.rearrange("p (u n) -> p u n", n=P)).then_inc(tr_out, 1)
                else:
                    k = 2 * (j - CPB)
                    V.tensor_copy(kT[:, b % 2, :, k * P:(k + 2) * P].rearrange("p g (k n) -> p k g n", k=2),
                                  src.rearrange("p (k g n) -> p k g n", k=2, g=G1)).then_inc(tr_out, 1)

            def take_piece(b, i):
                if i < 2:
                    take_qkv(b, i)
                else:
                    take_transposed(b, i - 2)
                if i == 1:
                    pack(b)

            def divide(gi):
                b, g = divmod(gi, G1)
                v.wait_ge(ot_ps, gi + 1)
                if g == 0 and b >= 1:
                    v.wait_ge(aoT_ps, b)
                src = bank(6).rearrange("p (c h w) -> p c h w", c=CPB, w=VW)
                rs = rsum[:].rearrange("p (c h) -> p c h", c=CPB)
                link(V.reciprocal(rs, src[:, :, :, HD]))
                dst = ao.rearrange("p c (h d) -> p c h d", d=HD)[:, :, g * HPG:(g + 1) * HPG, :]
                V.tensor_tensor(dst, src[:, :, :, 0:HD],
                                rsum[:].rearrange("p (c h o) -> p c h o", c=CPB, o=1).broadcast_to([P, CPB, HPG, HD]),
                                ALU.mult).then_inc(ao_set, 1)

            def wo_add(b):
                v.wait_ge(wo_ps, b + 1)
                xb4 = x[:, b * CPB:(b + 1) * CPB, :]
                return V.tensor_tensor(xb4, xb4, bank(6).rearrange("p (c d) -> p c d", c=CPB), ALU.add)

            def add_experts():
                v.wait_ge(score_set, 2)
                link(V.tensor_scalar(slotf[:], wts[1][:], 1.0, None, ALU.add))
                link(V.reciprocal(wts[0][:], slotf[:]))
                link(V.tensor_tensor(wts[1][:], wts[1][:], wts[0][:], ALU.mult))
                v.wait_ge(gathered[1], 16 * 2 * C)
                v.wait_ge(wo_out, B - 1)
                for k, src in enumerate((xs, yg2)):
                    for c in range(C):
                        last = V.scalar_tensor_tensor(out=x[:, c, :], in0=src[:, c, :], scalar=wts[k][:, c:c + 1],
                                                      in1=x[:, c, :], op0=ALU.mult, op1=ALU.add)
                        if k == 1 and c % CPB == CPB - 1 and c < C - 1:
                            last.then_inc(fin, 1)
                        else:
                            tick(last)
                    sync()

            for i in range(NPIECE):
                take_piece(0, i)
            for gi in range(GROUPS):
                b, g = divmod(gi, G1)
                if gi == BLOCKS_AFTER:
                    block_vectors(v, 1)
                for t in range(NT):
                    if gi >= 1 and t == 1:
                        divide(gi - 1)
                    if g == 1 and b >= 1 and t == 0:
                        wo_add(b - 1).then_inc(wo_out, 1)
                    if b + 1 < B and (g, t) in PIECES:
                        take_piece(b + 1, PIECES[(g, t)])
            add_experts()
            divide(GROUPS - 1)
            wo_add(B - 1).then_inc(fin, 1)

_INS = ["x", "wq", "wk", "wvT", "wfc", "gamma", "beta", "gate", "shg", "shu", "shd", "experts0",
        "wqkv", "wo", "wgT", "experts1", "const"]


def expert_columns(gate, up, down):
    down = down.reshape(E, 2, P, D).transpose(2, 0, 1, 3).reshape(P, E, 2 * D)
    return np.ascontiguousarray(np.concatenate([gate.transpose(1, 0, 2), up.transpose(1, 0, 2), down], 2).reshape(P, E * EW))


def kernel(L0_attn_inputs, L0_attn_W_Q, L0_attn_W_K, L0_attn_W_V, L0_attn_W_fc, L0_attn_gamma, L0_attn_beta,
           L0_ffn_gate_w, L0_ffn_sh_gate, L0_ffn_sh_up, L0_ffn_sh_down, L0_ffn_rt_gate, L0_ffn_rt_up, L0_ffn_rt_down,
           L1_attn_w_qkv, L1_attn_w_o, L1_ffn_Wg, L1_ffn_W1, L1_ffn_W2, L1_ffn_W3):
    import concourse.bacc as bacc
    from concourse.bass_utils import run_bass_kernel_spmd

    t, a = np.ascontiguousarray, np.asarray
    values = [
        t(L0_attn_inputs), t(L0_attn_W_Q), t(L0_attn_W_K), t(np.asarray(L0_attn_W_V).T), t(L0_attn_W_fc),
        t(L0_attn_gamma), t(L0_attn_beta), t(L0_ffn_gate_w), t(L0_ffn_sh_gate), t(L0_ffn_sh_up), t(L0_ffn_sh_down),
        expert_columns(a(L0_ffn_rt_gate), a(L0_ffn_rt_up), a(L0_ffn_rt_down)), t(L1_attn_w_qkv), t(L1_attn_w_o),
        t(a(L1_ffn_Wg).T), expert_columns(*(a(w).transpose(0, 2, 1) for w in (L1_ffn_W1, L1_ffn_W2, L1_ffn_W3))),
        constants(),
    ]
    nc = bacc.Bacc("TRN2", target_bir_lowering=False, num_devices=1)
    arrays, args = {}, []
    for name, a in zip(_INS, values):
        arrays[f"in_{name}"] = a
        args.append(nc.dram_tensor(f"in_{name}", a.shape, mybir.dt.from_np(a.dtype), kind="ExternalInput").ap())
    args.append(nc.dram_tensor("out_x", (B, N, D), F32, kind="ExternalOutput").ap())
    build(nc, *args)
    r = run_bass_kernel_spmd(nc, [arrays], core_ids=[0])
    return r.results[0]["out_x"]
```

```python
import concourse.bass as bass
from concourse import mybir
from concourse.alu_op_type import AluOpType as ALU
from contextlib import ExitStack
import numpy as np

F32 = mybir.dt.float32
BF16 = mybir.dt.bfloat16
I32 = mybir.dt.int32
ACT = mybir.ActivationFunctionType
AX = mybir.AxisListType

P = 128
D = 128
B, N = 4, 512
CPB = N // P
C = B * CPB
E = 8
I = 256
LN_EPS = 1e-5

H0, DK = 16, 64
PAIRS = H0 * DK // P
DEN_EPS = 1e-8

H1, G1, HD = 16, 4, 8
HPG = H1 // G1
NQK = H1 + G1
NORM_EPS = 1e-10
TERMS = 8
VW = 32
MASKED = -1e30
EW = 2 * I + 2 * D

NB0 = C + E - 1
NB1 = 2 * C + E - 1
DEPTH = 4

K_ID, K_TRI, K_MASK, K_REV = 0, 128, 256, 384
K_M128 = K_REV + E
K_J = K_M128 + C
K_CC = K_J + NB1
K_SS = K_CC + CPB * NQK * HD
K_PART = K_SS + CPB * NQK * HD
K_SEL = K_PART + 2
K_END = K_SEL + PAIRS * P


def den_row(pair, half, part):
    return 32 * (pair % 4) + 4 * part + 2 * (pair // 4) + half


def constants():
    k = np.zeros((P, K_END), np.float32)
    i = np.arange(P)
    k[:, K_ID:K_ID + P] = i[:, None] == i[None, :]
    k[:, K_TRI:K_TRI + P] = i[:, None] < i[None, :]
    k[:, K_MASK:K_MASK + P] = np.where(i[:, None] > i[None, :], np.float32(MASKED), 0)
    for p in range(PAIRS):
        for half in range(2):
            for part in range(3):
                col = K_SEL + p * P + half * DK
                k[den_row(p, half, part), col:col + DK] = 1
    k[:, K_PART] = -(i % 32 // 4 >= 1).astype(np.float32)
    k[:, K_PART + 1] = -(i % 32 // 4 == 2).astype(np.float32)
    k[:, K_REV:K_REV + E] = E - np.arange(E)
    k[:, K_M128:K_M128 + C] = P * np.arange(C)
    k[:, K_J:K_J + NB1] = np.arange(NB1)
    half = HD // 2
    inv = (np.float32(1) / np.float32(10000) ** (np.arange(half, dtype=np.float32) / np.float32(half))).astype(np.float32)
    chunk_of = [c for c in range(CPB) for _ in range(H1)] + [c for c in range(CPB) for _ in range(G1)]
    for n, c in enumerate(chunk_of):
        ang = (np.arange(c * P, (c + 1) * P, dtype=np.float32)[:, None] * inv).astype(np.float32)
        cos, sin = np.cos(ang), np.sin(ang)
        k[:, K_CC + n * HD:K_CC + (n + 1) * HD] = np.concatenate([cos, cos], 1)
        k[:, K_SS + n * HD:K_SS + (n + 1) * HD] = np.concatenate([-sin, sin], 1)
    return k


def build(nc, x_d, wq_d, wk_d, wvT_d, wfc_d, gamma_d, beta_d, gate_d, shg_d, shu_d, shd_d,
          experts0_d, wqkv_d, wo_d, wgT_d, experts1_d, const_d, out_d):
    ctx = ExitStack()

    def sb(name, shape, dt=F32):
        return ctx.enter_context(nc.sbuf_tensor(name, shape, dt))

    def sem(name):
        return ctx.enter_context(nc.semaphore(name))

    with ctx:
        const = sb("const", [P, K_SEL])
        ident = const[:, K_ID:K_ID + P]
        identb = sb("identb", [P, P], BF16)
        trib = sb("trib", [P, P], BF16)
        onesb = sb("onesb", [P, P], BF16)
        maskb = sb("maskb", [P, P], BF16)
        selb = sb("selb", [P, PAIRS, P], BF16)
        zero = sb("zero", [P, D])
        gamma = sb("gamma", [P, D])
        beta = sb("beta", [P, D])

        x = sb("x", [P, C, D])
        xn = sb("xn", [P, C, D + 1])
        xnT = sb("xnT", [P, B * N])
        xs = sb("xs", [P, C, D])
        experts = sb("experts", [P, E * EW])
        gate = sb("gate", [P, E])
        wg1 = sb("wg1", [P, E])
        shgu = sb("shgu", [P, 2, I])
        shdn = sb("shdn", [P, 2, D])
        wqkv = sb("wqkv", [P, 192])
        wo = sb("wo", [P, D])

        arenaA = sb("arenaA", [P, 12288])
        Ks = arenaA[:, 0:4096].rearrange("p (c k) -> p c k", c=CPB)
        QT = arenaA[:, 4096:12288].rearrange("p (t u n) -> p t u n", t=2, n=N)
        wvT = arenaA[:, 8192:9216].rearrange("p (u d) -> p u d", d=D)
        wfc = arenaA[:, 9216:10240].rearrange("p (u d) -> p u d", d=D)
        shact = arenaA[:, 0:4096].rearrange("p (b a n) -> p b a n", b=B, n=N)
        pT = arenaA[:, 0:4096].rearrange("p (r n) -> p r n", n=1024)
        qT = arenaA[:, 4096:8192].bitcast(BF16).rearrange("p (t u n) -> p t u n", t=2, n=N)
        kT = arenaA[:, 8192:10240].bitcast(BF16).rearrange("p (t g n) -> p t g n", t=2, n=N)
        yg2 = arenaA[:, 10240:12288].rearrange("p (c d) -> p c d", d=D)

        arenaB = sb("arenaB", [P, 7168])
        wq = arenaB[:, 0:1024]
        wk = arenaB[:, 1024:2048]
        shgus = arenaB[:, 0:2048].rearrange("p (r a n) -> p r a n", r=2, n=N)
        wvf = arenaB[:, 2048:4096].rearrange("p (e u d) -> p e u d", e=2, d=D)
        xk = arenaB[:, 4096:5120].rearrange("p (u d) -> p u d", d=D)
        xkT = arenaB[:, 5120:6144]
        kvw = arenaB[:, 6144:7168].rearrange("p (u d) -> p u d", d=D)
        qk = arenaB[:, 0:640]
        tA = arenaB[:, 640:1280]
        tB = arenaB[:, 1280:1920]
        qpack = arenaB[:, 2048:4096].bitcast(BF16).rearrange("p (h t d) -> p h t d", t=TERMS, d=HD)
        kpack = arenaB[:, 4096:5120].bitcast(BF16).rearrange("p (h r t d) -> p h r t d", r=2, t=TERMS, d=HD)
        s1 = arenaB[:, 5120:5440].bitcast(BF16)
        s2 = arenaB[:, 5440:5760].bitcast(BF16)
        s3 = arenaB[:, 5760:6080].bitcast(BF16)
        ao = arenaB[:, 6144:6656].rearrange("p (c n) -> p c n", n=D)
        aoT = arenaB[:, 6656:7168]

        arenaC = sb("arenaC", [P, 3072])
        selector = arenaC[:, 0:PAIRS * P]
        shsg = arenaC[:, 0:1024].rearrange("p (a n) -> p a n", n=N)
        v9 = arenaC[:, 0:2048].rearrange("p (c g w) -> p c g w", c=C, w=VW)
        osb = arenaC[:, 2048:3072].rearrange("p (t n) -> p t n", n=N)

        ksB = sb("ksB", [P, PAIRS, 32])
        dsb = sb("dsb", [P, N])
        rr = sb("rr", [P, N])
        mid = sb("mid", [P, N], BF16)
        rd3 = sb("rd3", [P, N], BF16)
        zt = sb("zt", [P, CPB, D])

        xb = sb("xb", [P, DEPTH, D])
        xbT = sb("xbT", [P, 2, P])
        sg = sb("sg", [P, 2, I])
        act = sb("act", [P, 2, I])
        aT = sb("aT", [P, 2, I])
        yb = sb("yb", [P, DEPTH, D])

        st = sb("st", [P, C, 6])
        mv = sb("mv", [P, C, 2])
        nv = sb("nv", [P, 80])
        ny = sb("ny", [P, 80])
        nt = sb("nt", [P, 80])
        lg = sb("lg", [P, C, E])
        oh = [sb(f"oh{i}", [P, C, E]) for i in range(2)]
        ohb = sb("ohb", [P, C, E], BF16)
        ra = sb("ra", [P, C, E])
        rb = sb("rb", [P, C, E])
        tot = sb("tot", [P, C, E])
        pos = sb("pos", [P, C, E])
        top = [sb(f"top{i}", [P, C]) for i in range(2)]
        first = sb("first", [P, C])
        rsum = sb("rsum", [P, CPB * HPG])
        wide = sb("wide", [P, NB1 * E])
        nblk = sb("nblk", [P, E])
        bend = [sb(f"bend{i}", [P, E]) for i in range(2)]
        slotf = sb("slotf", [P, C])
        bef = sb("bef", [1, NB1])
        score = sb("score", [P, C])
        wts = [sb(f"wts{i}", [P, C]) for i in range(2)]
        slot = [sb(f"slot{i}", [P, C], I32) for i in range(3)]
        bexp = [sb(f"bexp{i}", [1, n], I32) for i, n in enumerate((NB0, NB1))]

        ps = ctx.enter_context(nc.psum_tensor("ps", [P, 8, 512], F32))

        def bank(i):
            return ps[:, i, :]

        def pair_banks(n):
            return ps[:, 2 * (n % 2):2 * (n % 2) + 2, :]

        NB = (NB0, NB1)
        xs_dr = [nc.dram_tensor(f"sorted_x{l}", [NB[l] * P, D], F32, kind="Internal").ap() for l in range(2)]
        y_dr = [nc.dram_tensor(f"sorted_y{l}", [NB[l] * P, D], F32, kind="Internal").ap() for l in range(2)]

        x_in = [sem(f"x_in{b}") for b in range(B)]
        const_in = sem("const_in")
        sel_in = sem("sel_in")
        gate_in = sem("gate_in")
        wvf_in = sem("wvf_in")
        wk_in = sem("wk_in")
        wq_in = sem("wq_in")
        affine_in = sem("affine_in")
        experts_in = [sem(f"experts_in{l}") for l in range(2)]
        shared_in = sem("shared_in")
        layer1_in = sem("layer1_in")
        zeroed = [sem(f"zeroed{l}") for l in range(2)]
        zero_set = sem("zero_set")
        pool_set = sem("pool_set")
        chain = sem("chain")
        casts = sem("casts")
        xn_done = [sem(f"xn_done{l}") for l in range(2)]
        xnT_ps = sem("xnT_ps")
        xnT_done = sem("xnT_done")
        logits = sem("logits")
        onehot = [sem(f"onehot{l}") for l in range(2)]
        ranks = sem("ranks")
        routed = [sem(f"routed{l}") for l in range(2)]
        top_set = sem("top_set")
        score_set = sem("score_set")
        xs_set = sem("xs_set")
        scattered = [sem(f"scattered{l}") for l in range(2)]
        gathered = [[sem(f"gathered0_{b}") for b in range(B)],
                    [sem(f"gathered1_{k}") for k in range(2)]]
        unit_ps = sem("unit_ps")
        unit_out = sem("unit_out")
        xk_ps, xk_out = sem("xk_ps"), sem("xk_out")
        xkT_ps, xkT_out = sem("xkT_ps"), sem("xkT_out")
        den_ps, rd3_set = sem("den_ps"), sem("rd3_set")
        kvw_ps, kvw_out = sem("kvw_ps"), sem("kvw_out")
        bc_ps, qs_set = sem("bc_ps"), sem("qs_set")
        y_ps, y_out = sem("y_ps"), sem("y_out")
        sh_sig, sh_m, sh_act = sem("sh_sig"), sem("sh_m"), sem("sh_act")
        shy_ps, shy_out = sem("shy_ps"), sem("shy_out")
        blk = [{n: sem(f"b{l}_{n}") for n in ("xT", "xbT", "gu", "sg", "m", "act", "aTp", "aT", "y", "yb")}
               | {n: [sem(f"b{l}_{n}{r}") for r in range(DEPTH)] for n in ("ld", "st")} for l in range(2)]
        piece_ps, piece_out = sem("piece_ps"), sem("piece_out")
        packed = sem("packed")
        s_ps, p_set, pv_done = sem("s_ps"), sem("p_set"), sem("pv_done")
        o_out = sem("o_out")
        ot_ps, ao_set = sem("ot_ps"), sem("ao_set")
        aoT_ps, aoT_out = sem("aoT_ps"), sem("aoT_out")
        wo_ps, wo_out = sem("wo_ps"), sem("wo_out")
        fin, stored = sem("fin"), sem("stored")

        TILES = [
            [(0, 0, 0, 0), (1, 0, 1, 0)],
            [(2, 0, 0, 0), (3, 0, 1, 0)],
            [(0, 1, 0, 0), (0, 3, 0, 384), (1, 1, 1, 0), (1, 3, 1, 384)],
            [(2, 1, 0, 0), (2, 3, 0, 384), (3, 1, 1, 0), (3, 3, 1, 384)],
            [(0, 2, 0, 0), (2, 2, 0, 256), (1, 2, 1, 0), (3, 2, 1, 256)],
        ]
        NT = len(TILES)
        GROUPS = B * G1
        PV_STEPS = [(0, 1, 0, 0, N // 2), (0, 1, 0, N // 2, N), (2, 3, 1, P, N), (2, 3, 3, 3 * P, N), (4, 4, 2, 2 * P, N)]
        PV_DONE = [2, 2, 4, 4, 5]
        FIRST = [("x", 0), ("qkv", 0, 0), ("qkv", 0, 1)] + [("tr", 0, j) for j in range(6)]
        BEHIND = {
            (0, 1): ("x", 1), (0, 2): ("qkv", 1, 0), (0, 3): ("qkv", 1, 1), (0, 4): ("x", 2), (1, 1): ("x", 3),
            (1, 3): ("logits",), (2, 1): ("tr", 1, 0), (2, 2): ("ranks",), (2, 3): ("tr", 1, 1), (2, 4): ("tr", 1, 2),
            (3, 0): ("tr", 1, 3), (3, 2): ("tr", 1, 4), (3, 3): ("tr", 1, 5), (3, 4): ("qkv", 2, 0),
            (4, 0): ("qkv", 2, 1), (6, 0): ("qkv", 3, 0), (6, 1): ("tr", 2, 0), (6, 2): ("qkv", 3, 1),
            (6, 3): ("tr", 2, 1), (6, 4): ("tr", 2, 2), (7, 0): ("tr", 2, 3), (7, 2): ("tr", 2, 4), (7, 3): ("tr", 2, 5),
            (8, 1): ("tr", 3, 0), (8, 4): ("tr", 3, 1), (9, 2): ("tr", 3, 2), (10, 0): ("tr", 3, 3),
            (10, 3): ("tr", 3, 4), (11, 1): ("tr", 3, 5),
        }
        PIECES = FIRST + [BEHIND[at] for at in sorted(BEHIND)]
        PACK = {(0, 4): (1, 0), (1, 0): (1, 1), (1, 1): (1, 2), (1, 2): (1, 3),
                (4, 0): (2, 0), (4, 4): (2, 1), (5, 0): (2, 2), (5, 1): (2, 3),
                (6, 2): (3, 0), (6, 4): (3, 1), (7, 0): (3, 2), (7, 4): (3, 3)}
        BLOCKS_AFTER = 2 * G1

        def piece_bank(n):
            return 7 if n > len(FIRST) or n % 2 else 6

        def piece_no(*piece):
            return PIECES.index(piece) + 1

        SHARED_UNITS = 2 + 8 * B

        def block_dmas(sp, l):
            s, n = blk[l], NB[l]

            def load(it, r):
                t = it * DEPTH + r
                sp.dma_start(xb[:, r % DEPTH, :], xs_dr[l][bass.ts(t, P), :]).then_inc(s["ld"][r % DEPTH], 16)

            def store(it, r):
                t = it * DEPTH + r
                sp.wait_ge(s["yb"], t + 3)
                sp.dma_start(y_dr[l][bass.ts(t, P), :], yb[:, r % DEPTH, :]).then_inc(s["st"][r % DEPTH], 16)

            for q in s["st"]:
                sp.sem_inc(q, 16)
            sp.wait_ge(scattered[l], 16 * C * (l + 1))
            for t in range(DEPTH):
                load(0, t)
            for k in range(3):
                sp.wait_ge(s["xT"], k + 1)
                load(1, k)
            with sp.Fori(0, (n - 7) // DEPTH) as it:
                for r in range(DEPTH):
                    sp.wait_ge(s["xT"], it * DEPTH + (4 + r))
                    load(it, 7 + r)
                    store(it, r)
            for t in range(n - 7, n):
                store(0, t)
            for r, q in enumerate(s["st"]):
                sp.wait_ge(q, 16 * (1 + len(range(r, n, DEPTH))))

        def o_evac(sc, gi):
            sc.wait_ge(pv_done, (gi + 1) * NT)
            if gi >= 2:
                sc.wait_ge(ot_ps, gi - 1)
            nc.scalar.activation(osb[:, gi % 2, :], bank(4 + gi % 2), ACT.Copy).then_inc(o_out, 1)

        def ao_evac(sc, b):
            sc.wait_ge(aoT_ps, b + 1)
            if b >= 1:
                sc.wait_ge(wo_ps, b)
            nc.scalar.activation(aoT, bank(6), ACT.Copy).then_inc(aoT_out, 1)

        def block_acts(sc, l):
            s, n = blk[l], NB[l]

            def x_evac(it, r):
                sc.wait_ge(s["xT"], it * DEPTH + (r + 1))
                nc.scalar.activation(xbT[:, r % 2, :], bank(r % 2)[:, 0:P], ACT.Copy).then_inc(s["xbT"], 1)

            def sigmoid(it, r):
                sc.wait_ge(s["gu"], it * DEPTH + (r + 1))
                nc.scalar.activation(sg[:, r % 2, :], bank(2 + r % 2)[:, 0:I], ACT.Sigmoid).then_inc(s["sg"], 1)

            def a_evac(it, r):
                sc.wait_ge(s["aTp"], it * DEPTH + (r + 1))
                nc.scalar.activation(aT[:, r % 2, :], bank(4 + r % 2)[:, 0:I], ACT.Copy).then_inc(s["aT"], 1)

            sc.sem_inc(s["aT"], 1)
            x_evac(0, 0)
            x_evac(0, 1)
            sigmoid(0, 0)
            x_evac(0, 2)
            sigmoid(0, 1)
            a_evac(0, 0)
            with sc.Fori(0, (n - 3) // DEPTH) as it:
                for r in range(DEPTH):
                    t = it * DEPTH + (2 + r)
                    sc.wait_ge(s["gu"], t)
                    x_evac(it, 3 + r)
                    sc.wait_ge(s["act"], t - 1)
                    sigmoid(it, 2 + r)
                    sc.wait_ge(s["y"], t - 1)
                    a_evac(it, 1 + r)
            t = n - 1
            sc.wait_ge(s["act"], t - 1)
            sigmoid(0, t)
            sc.wait_ge(s["y"], t - 1)
            a_evac(0, t - 1)
            sc.wait_ge(s["y"], t)
            a_evac(0, t)

        def block_matmuls(pe, l):
            s, n = blk[l], NB[l]

            at = {}

            def find_experts(t0):
                _, values = nc.values_load_multi_w_load_instructions(
                    bexp[l][0:1, t0:min(t0 + 4, n)], engines=(mybir.EngineType.PE,), min_val=0, max_val=(E - 1) * EW,
                    skip_runtime_bounds_check_because="route() counts at most E - 1 experts")
                for k, value in enumerate(values):
                    at[t0 + k] = value

            def x_transpose(t):
                pe.wait_ge(s["ld"][t % DEPTH], 16 * (t // DEPTH + 1))
                if t >= 2:
                    pe.wait_ge(s["xbT"], t - 1)
                nc.tensor.transpose(bank(t % 2)[:, 0:P], xb[:, t % DEPTH, :], ident).then_inc(s["xT"], 1)

            def gate_up(t):
                pe.wait_ge(s["xbT"], t + 1)
                if t >= 2:
                    pe.wait_ge(s["act"], t - 1)
                nc.tensor.matmul(bank(2 + t % 2), xbT[:, t % 2, :], experts[:, bass.ds(at[t], 2 * I)],
                                 start=True, stop=True).then_inc(s["gu"], 1)

            def a_transposes(t):
                pe.wait_ge(s["act"], t + 1)
                if t >= 2:
                    pe.wait_ge(s["aT"], t)
                for a in range(2):
                    last = nc.tensor.transpose(bank(4 + t % 2)[:, a * P:(a + 1) * P], act[:, t % 2, a * P:(a + 1) * P], ident)
                last.then_inc(s["aTp"], 1)

            def down(t):
                pe.wait_ge(s["aT"], t + 2)
                pe.wait_ge(s["yb"], t + 1)
                for a in range(2):
                    last = nc.tensor.matmul(bank(6 + t % 2)[:, 0:D], aT[:, t % 2, a * P:(a + 1) * P],
                                            experts[:, bass.ds(at[t] + (2 * I + a * D), D)],
                                            start=(a == 0), stop=(a == 1))
                last.then_inc(s["y"], 1)

            pe.wait_ge(experts_in[l], 16)
            pe.wait_ge(routed[l], 1)
            pe.sem_inc(s["y"], 1)
            find_experts(0)
            x_transpose(0)
            for t in range(n + 2):
                if t % 4 == 3 and t + 1 < n:
                    find_experts(t + 1)
                if t + 1 < n:
                    x_transpose(t + 1)
                if t < n:
                    gate_up(t)
                if t >= 2:
                    down(t - 2)
                if 1 <= t <= n:
                    a_transposes(t - 1)

        def shared_add(v, b):
            v.wait_ge(shy_ps, b + 1)
            xb4 = x[:, b * CPB:(b + 1) * CPB, :]
            nc.vector.tensor_tensor(xb4, xb4, bank(4 + b % 2).rearrange("p (c d) -> p c d", c=CPB),
                                    ALU.add).then_inc(shy_out, 1)

        def block_vectors(v, l):
            s, n = blk[l], NB[l]
            V = nc.vector

            def activate(it, r):
                t = it * DEPTH + r
                v.wait_ge(s["sg"], t + 1)
                gu = bank(2 + r % 2)
                V.tensor_tensor(act[:, r % 2, :], sg[:, r % 2, :], gu[:, 0:I], ALU.mult).then_inc(s["m"], 1)
                v.wait_ge(s["m"], t + 1)
                V.tensor_tensor(act[:, r % 2, :], act[:, r % 2, :], gu[:, I:2 * I], ALU.mult).then_inc(s["act"], 1)

            def take_y(it, r):
                t = it * DEPTH + r
                v.wait_ge(s["y"], t + 2)
                v.wait_ge(s["st"][r % DEPTH], (it + r // DEPTH + 1) * 16)
                V.tensor_copy(yb[:, r % DEPTH, :], bank(6 + r % 2)[:, 0:D]).then_inc(s["yb"], 1)

            activate(0, 0)
            activate(0, 1)
            with v.Fori(0, (n - 3) // DEPTH) as it:
                for r in range(DEPTH):
                    v.wait_ge(s["aTp"], it * DEPTH + (1 + r))
                    activate(it, 2 + r)
                    take_y(it, r)
            v.wait_ge(s["aTp"], n - 2)
            activate(0, n - 1)
            for t in range(n - 3, n):
                take_y(0, t)

        blkctx = ctx.enter_context(nc.Block())

        @blkctx.sync
        def _(sp):
            for b in range(B):
                sp.dma_start(x[:, b * CPB:(b + 1) * CPB, :],
                             x_d[b].rearrange("(c p) d -> p c d", p=P)).then_inc(x_in[b], 16)
            sp.dma_start(gate[:], gate_d).then_inc(gate_in, 16)
            sp.dma_start(wk, wk_d).then_inc(wk_in, 16)
            sp.dma_start(wq, wq_d).then_inc(wq_in, 16)
            sp.wait_ge(zero_set, 1)
            for l in range(2):
                sp.dma_start(xs_dr[l].rearrange("(n p) d -> p n d", p=P),
                             zero[:, :].rearrange("p (a d) -> p a d", a=1).broadcast_to([P, NB[l], D])
                             ).then_inc(zeroed[l], 16)
            sp.dma_start(experts[:], experts0_d).then_inc(experts_in[0], 16)
            sp.dma_start(shgu[:, 0, :], shg_d).then_inc(shared_in, 16)
            sp.dma_start(shgu[:, 1, :], shu_d).then_inc(shared_in, 16)
            sp.dma_start(shdn[:], shd_d.rearrange("(a p) d -> p a d", p=P)).then_inc(shared_in, 16)
            sp.dma_start(wqkv[:], wqkv_d).then_inc(layer1_in, 16)
            sp.dma_start(wo[:], wo_d).then_inc(layer1_in, 16)
            sp.dma_start(wg1[:], wgT_d).then_inc(layer1_in, 16)
            block_dmas(sp, 0)
            sp.wait_ge(blk[0]["y"], NB0 + 1)
            sp.dma_start(experts[:], experts1_d).then_inc(experts_in[1], 16)
            block_dmas(sp, 1)
            for b in range(B):
                sp.wait_ge(fin, b + 1)
                sp.dma_start(out_d[b].rearrange("(c p) d -> p c d", p=P),
                             x[:, b * CPB:(b + 1) * CPB, :]).then_inc(stored, 16)
            sp.wait_ge(stored, 16 * B)

        @blkctx.gpsimd
        def _(pool):
            nc.gpsimd.memset(zero[:], 0.0).then_inc(zero_set, 1)
            nc.gpsimd.memset(xn[:, :, D:D + 1], 1.0).then_inc(pool_set, 1)
            nc.gpsimd.memset(ksB[:], 0.0).then_inc(pool_set, 1)
            nc.gpsimd.memset(onesb[:], 1.0).then_inc(pool_set, 1)

            def scatter(l, k, src):
                for c in range(C):
                    pool.indirect_dma_start(
                        out=xs_dr[l][:, :], out_offset=bass.IndirectOffsetOnAxis(slot[l + k][:, c:c + 1], 0),
                        in_=src(c), in_offset=None).then_inc(scattered[l], 16)

            def gather(l, k, dst):
                for c in range(C):
                    pool.indirect_dma_start(
                        out=dst(c), out_offset=None, in_=y_dr[l][:, :],
                        in_offset=bass.IndirectOffsetOnAxis(slot[l + k][:, c:c + 1], 0)
                        ).then_inc(gathered[l][k if l else c // CPB], 16)

            def stored_blocks(l):
                for r, q in enumerate(blk[l]["st"]):
                    pool.wait_ge(q, 16 * (1 + len(range(r, NB[l], DEPTH))))

            pool.wait_ge(zeroed[0], 16)
            pool.wait_ge(routed[0], 1)
            pool.wait_ge(xs_set, 1)
            scatter(0, 0, lambda c: xs[:, c, :])
            pool.wait_ge(xk_ps, B)
            for i in range(2 * B):
                b, a = divmod(i, 2)
                pool.wait_ge(sh_sig, i + 1)
                pool.wait_ge(unit_out, SHARED_UNITS + i + 1)
                nc.gpsimd.tensor_tensor(shact[:, b, a, :], shsg[:, a, :], shgus[:, a, 0, :], ALU.mult).then_inc(sh_m, 1)
                pool.wait_ge(sh_m, i + 1)
                nc.gpsimd.tensor_tensor(shact[:, b, a, :], shact[:, b, a, :], shgus[:, a, 1, :],
                                        ALU.mult).then_inc(sh_act, 1)
            pool.wait_ge(scattered[0], 16 * C)
            stored_blocks(0)
            gather(0, 0, lambda c: xs[:, c, :])
            pool.wait_ge(sh_act, 2 * B)
            nc.gpsimd.memset(v9[:, :, :, HD:VW], 0.0).then_inc(pool_set, 1)
            pool.wait_ge(pool_set, 4)
            nc.gpsimd.memset(v9[:, :, :, HD:HD + 1], 1.0).then_inc(pool_set, 1)
            pool.wait_ge(zeroed[1], 16)
            pool.wait_ge(routed[1], 1)
            for k in range(2):
                scatter(1, k, lambda c: xn[:, c, 0:D])
            stored_blocks(1)
            gather(1, 0, lambda c: xs[:, c, :])
            gather(1, 1, lambda c: yg2[:, c, :])

        @blkctx.scalar
        def _(sc):
            sc.dma_start(const[:], const_d[:, 0:K_SEL]).then_inc(const_in, 16)
            sc.dma_start(selector, const_d[:, K_SEL:K_END]).then_inc(sel_in, 16)
            sc.dma_start(wvT, wvT_d.rearrange("(u q) d -> q u d", q=P)).then_inc(wvf_in, 16)
            sc.dma_start(wfc, wfc_d.rearrange("(u q) d -> q u d", q=P)).then_inc(wvf_in, 16)
            sc.dma_start(gamma[:], gamma_d.rearrange("(a d) -> a d", a=1).broadcast_to([P, D])).then_inc(affine_in, 16)
            sc.dma_start(beta[:], beta_d.rearrange("(a d) -> a d", a=1).broadcast_to([P, D])).then_inc(affine_in, 16)

            def take_piece(piece):
                if piece[0] not in ("x", "tr"):
                    return
                sc.wait_ge(piece_ps, piece_no(*piece))
                b = piece[1]
                if piece[0] == "x":
                    nc.scalar.activation(xnT[:, b * N:(b + 1) * N], bank(piece_bank(piece_no(*piece))),
                                         ACT.Copy).then_inc(piece_out, 1)
                    return
                j = piece[2]
                if j == 0 and b >= 2:
                    sc.wait_ge(s_ps, (b - 1) * G1 * NT)
                src = bank(piece_bank(piece_no(*piece))).bitcast(BF16)
                if j < CPB:
                    nc.scalar.activation(qT[:, b % 2, :, j * P:(j + 1) * P],
                                         src.rearrange("p (u n) -> p u n", n=P), ACT.Copy).then_inc(piece_out, 1)
                else:
                    k = 2 * (j - CPB)
                    nc.scalar.activation(kT[:, b % 2, :, k * P:(k + 2) * P].rearrange("p g (k n) -> p k g n", k=2),
                                         src.rearrange("p (k g n) -> p k g n", k=2, g=G1), ACT.Copy).then_inc(piece_out, 1)

            unit_n = [0]

            def unit(dst, fn):
                n = unit_n[0]
                unit_n[0] += 1
                sc.wait_ge(unit_ps, n + 1)
                nc.scalar.activation(dst, pair_banks(n), fn).then_inc(unit_out, 1)

            def proj_unit(b, i):
                if i < CPB:
                    unit(Ks[:, i, :].rearrange("p (a n) -> p a n", a=2), ACT.Sigmoid)
                else:
                    u = 2 * (i - CPB)
                    unit(QT[:, b % 2, u:u + 2, :], ACT.Sigmoid)

            for b in range(B):
                sc.wait_ge(xnT_ps, b + 1)
                nc.scalar.activation(xnT[:, b * N:(b + 1) * N], bank(4 + b % 2), ACT.Copy).then_inc(xnT_done, 1)
            unit(wvf[:, 0].rearrange("p (a u) d -> p a (u d)", a=2), ACT.Copy)
            unit(wvf[:, 1].rearrange("p (a u) d -> p a (u d)", a=2), ACT.Copy)
            for i in range(8):
                proj_unit(0, i)
                if i == 3:
                    sc.wait_ge(top_set, 1)
                    nc.scalar.activation(score[:], top[0][:], ACT.Sigmoid).then_inc(score_set, 1)
            for b in range(B):
                more = b + 1 < B

                def units(lo, hi):
                    for i in range(lo, hi):
                        if not more:
                            sc.wait_ge(unit_ps, SHARED_UNITS + i + 1)
                            if i >= 2:
                                sc.wait_ge(sh_act, i - 1)
                            banks = pair_banks(SHARED_UNITS + i)
                            nc.scalar.activation(shsg[:, i % 2, :], banks[:, 0, :], ACT.Sigmoid).then_inc(sh_sig, 1)
                            nc.scalar.activation(shgus[:, i % 2], banks, ACT.Copy).then_inc(unit_out, 1)
                        else:
                            if i == 0:
                                sc.wait_ge(xk_ps, b + 1)
                            if i == CPB and b >= 1:
                                sc.wait_ge(y_ps, b)
                            proj_unit(b + 1, i)

                units(0, 2)
                sc.wait_ge(xkT_ps, b + 1)
                if b >= 1:
                    sc.wait_ge(kvw_ps, b)
                nc.scalar.activation(xkT.rearrange("p (a n) -> p a n", a=2), ps[:, 4:6, :], ACT.Copy).then_inc(xkT_out, 1)
                units(2, 3)
                sc.wait_ge(kvw_ps, b + 1)
                if b >= 1:
                    sc.wait_ge(y_ps, b)
                nc.scalar.activation(kvw.rearrange("p (a u) d -> p a (u d)", a=2), ps[:, 4:6, :], ACT.Copy).then_inc(kvw_out, 1)
                units(3, 8)

            block_acts(sc, 0)

            sc.wait_ge(shy_ps, B)
            for piece in FIRST:
                take_piece(piece)

            for gi in range(GROUPS):
                b, g = divmod(gi, G1)
                if gi == BLOCKS_AFTER:
                    block_acts(sc, 1)
                for t in range(NT):
                    n = gi * NT + t
                    if gi >= 1 and t == 2 and gi != BLOCKS_AFTER:
                        o_evac(sc, gi - 1)
                    sc.wait_ge(s_ps, n + 1)
                    if n >= 4:
                        sc.wait_ge(pv_done, (n - 4) // NT * NT + PV_DONE[(n - 4) % NT])
                    nc.scalar.activation(pT[:, n % 4, :].rearrange("p (a n) -> p a n", a=2), pair_banks(n),
                                         ACT.Exp, scale=float(1.0 / np.sqrt(np.float32(HD)))).then_inc(p_set, 1)
                    if b >= 1 and g == 1 and t == 1:
                        ao_evac(sc, b - 1)
                    before = divmod(n - 1, NT)
                    if before in BEHIND and t > 0:
                        take_piece(BEHIND[before])
                if (gi, NT - 1) in BEHIND:
                    take_piece(BEHIND[gi, NT - 1])
                if gi == G1 - 1:
                    sc.wait_ge(top_set, 2)
                    nc.scalar.activation(wts[1][:], wts[1][:], ACT.Exp).then_inc(score_set, 1)
                if gi + 1 in (BLOCKS_AFTER, GROUPS):
                    o_evac(sc, gi)
            ao_evac(sc, B - 1)

        @blkctx.tensor
        def _(pe):
            def router(dst, weights, chunks):
                for c in chunks:
                    last = nc.tensor.matmul(dst[:, c * E:(c + 1) * E], xnT[:, c * P:(c + 1) * P], weights[:],
                                            start=True, stop=True)
                return last

            def count_ranks():
                rhs = ohb[:].rearrange("p c e -> p (c e)")
                nc.tensor.matmul(bank(7)[:, 0:C * E], trib[:], rhs, start=True, stop=True)
                return nc.tensor.matmul(bank(7)[:, C * E:2 * C * E], onesb[:], rhs, start=True, stop=True)

            unit_n = [0]

            def unit_begin():
                n = unit_n[0]
                if n >= 2:
                    pe.wait_ge(unit_out, n - 1)
                unit_n[0] += 1
                return pair_banks(n)

            def shared_unit(i):
                b, a = divmod(i, 2)
                dst = unit_begin()
                for k in range(2):
                    last = nc.tensor.matmul(dst[:, k, :], shgu[:, k, a * P:(a + 1) * P], xnT[:, b * N:(b + 1) * N],
                                            start=True, stop=True)
                last.then_inc(unit_ps, 1)

            def proj_unit(b, i):
                dst = unit_begin()
                if i < CPB:
                    c = b * CPB + i
                    for a in range(2):
                        last = nc.tensor.matmul(dst[:, a, :], xnT[:, c * P:(c + 1) * P], wk[:, a * 512:(a + 1) * 512],
                                                start=True, stop=True)
                else:
                    for a in range(2):
                        u = 2 * (i - CPB) + a
                        last = nc.tensor.matmul(dst[:, a, :], wq[:, u * P:(u + 1) * P], xnT[:, b * N:(b + 1) * N],
                                                start=True, stop=True)
                last.then_inc(unit_ps, 1)

            pe.wait_ge(const_in, 16)
            pe.wait_ge(gate_in, 16)
            for b in range(B + 1):
                if b < B:
                    pe.wait_ge(xn_done[0], b + 1)
                    if b >= 2:
                        pe.wait_ge(xnT_done, b - 1)
                    for i in range(CPB):
                        last = nc.tensor.transpose(bank(4 + b % 2)[:, i * P:(i + 1) * P], xn[:, b * CPB + i, 0:D], ident)
                    last.then_inc(xnT_ps, 1)
                if b >= 1:
                    pe.wait_ge(xnT_done, b)
                    router(bank(6), gate, range((b - 1) * CPB, b * CPB)).then_inc(logits, 1)
            pe.wait_ge(wvf_in, 32)
            for par in range(2):
                dst = unit_begin()
                rows = slice(DK * par, DK * par + DK)
                for u in range(PAIRS):
                    last = nc.tensor.matmul(dst[:, u // 4, (u % 4) * D:(u % 4 + 1) * D], wvT[rows, u, :], wfc[rows, u, :],
                                            start=True, stop=True)
                last.then_inc(unit_ps, 1)
            pe.wait_ge(wk_in, 16)
            pe.wait_ge(wq_in, 16)
            pe.wait_ge(casts, 1)
            pe.wait_ge(pool_set, 3)
            for i in range(8):
                proj_unit(0, i)
                if i == 1:
                    pe.wait_ge(onehot[0], 1)
                    count_ranks().then_inc(ranks, 1)
            for b in range(B):
                more = b + 1 < B

                def units(lo, hi):
                    for i in range(lo, hi):
                        if more:
                            proj_unit(b + 1, i)
                        else:
                            if i == 0:
                                pe.wait_ge(shared_in, 48)
                            shared_unit(i)

                pe.wait_ge(unit_out, 2 + 8 * b + CPB)
                if b >= 1:
                    pe.wait_ge(y_out, b)
                    pe.wait_ge(qs_set, 8 * b)
                else:
                    pe.wait_ge(xnT_done, B)
                    pe.wait_ge(onehot[0], 1)
                for u in range(PAIRS):
                    dst = ps[:, 4 + u // 3, (u % 3) * (D + 1):(u % 3 + 1) * (D + 1)]
                    for i in range(CPB):
                        last = nc.tensor.matmul(dst, Ks[:, i, u * P:(u + 1) * P], xn[:, b * CPB + i, :],
                                                start=(i == 0), stop=(i == CPB - 1))
                last.then_inc(xk_ps, 1)
                units(0, 2)
                pe.wait_ge(xk_out, b + 1)
                pe.wait_ge(unit_out, 2 + 8 * b + 8)
                if b == 0:
                    pe.wait_ge(routed[0], 1)
                for u in range(PAIRS):
                    rows = slice(32 * (u % 4), 32 * (u % 4) + 32)
                    last = nc.tensor.matmul(bank(7)[rows, :], ksB[:, u, :], QT[:, b % 2, u, :],
                                            start=(u < 4), stop=(u >= 4))
                last.then_inc(den_ps, 1)
                for u in range(PAIRS):
                    last = nc.tensor.transpose(ps[:, 4 + u // 4, (u % 4) * P:(u % 4 + 1) * P], xk[:, u, :], ident)
                last.then_inc(xkT_ps, 1)
                units(2, 3)
                pe.wait_ge(xkT_out, b + 1)
                for h in range(H0):
                    u, par = divmod(h, 2)
                    last = nc.tensor.matmul(ps[DK * par:DK * par + DK, 4 + u // 4, (u % 4) * D:(u % 4 + 1) * D],
                                            xkT[:, h * DK:(h + 1) * DK], wvf[:, par, u, :], start=True, stop=True)
                last.then_inc(kvw_ps, 1)
                units(3, 6)
                pe.wait_ge(rd3_set, b + 1)
                for u in range(PAIRS):
                    if u >= 2:
                        pe.wait_ge(qs_set, 8 * b + u - 1)
                    nc.tensor.matmul(bank(6 + u % 2), selb[:, u, :], rd3[:], start=True, stop=True).then_inc(bc_ps, 1)
                    if u == 3:
                        units(6, 7)
                units(7, 8)
                pe.wait_ge(kvw_out, b + 1)
                pe.wait_ge(qs_set, 8 * (b + 1))
                for i in range(CPB):
                    for u in range(PAIRS):
                        last = nc.tensor.matmul(bank(4)[:, i * D:(i + 1) * D], QT[:, b % 2, u, i * P:(i + 1) * P],
                                                kvw[:, u, :], start=(u == 0), stop=(u == PAIRS - 1))
                last.then_inc(y_ps, 1)

            pe.wait_ge(unit_out, SHARED_UNITS + 2 * B)
            pe.wait_ge(y_out, B)
            block_matmuls(pe, 0)

            pe.wait_ge(blk[0]["xbT"], NB0)
            pe.wait_ge(blk[0]["act"], NB0)
            pe.wait_ge(blk[0]["aT"], NB0 + 1)
            pe.wait_ge(sh_act, 2 * B)
            for b in range(B):
                if b >= 2:
                    pe.wait_ge(shy_out, b - 1)
                for i in range(CPB):
                    for a in range(2):
                        last = nc.tensor.matmul(bank(4 + b % 2)[:, i * D:(i + 1) * D], shact[:, b, a, i * P:(i + 1) * P],
                                                shdn[:, a, :], start=(a == 0), stop=(a == 1))
                last.then_inc(shy_ps, 1)

            pe.wait_ge(layer1_in, 48)
            pe.wait_ge(shy_out, B)
            pe.wait_ge(blk[0]["yb"], NB0 + 2)
            def fill_piece(piece):
                n = piece_no(*piece)
                before = n - 1 if n > len(FIRST) else n - 2
                if before > 0:
                    pe.wait_ge(piece_out, before)
                dst = bank(piece_bank(n))
                if piece[0] == "x":
                    b = piece[1]
                    pe.wait_ge(xn_done[1], b + 1)
                    for i in range(CPB):
                        last = nc.tensor.transpose(dst[:, i * P:(i + 1) * P], xn[:, b * CPB + i, 0:D], ident)
                elif piece[0] == "logits":
                    last = router(dst, wg1, range(C))
                elif piece[0] == "ranks":
                    pe.wait_ge(onehot[1], 1)
                    last = count_ranks()
                elif piece[0] == "qkv":
                    _, b, i = piece
                    pe.wait_ge(piece_out, piece_no("x", b))
                    for k in range(2):
                        c = b * CPB + 2 * i + k
                        last = nc.tensor.matmul(dst[:, k * 192:(k + 1) * 192], xnT[:, c * P:(c + 1) * P], wqkv[:],
                                                start=True, stop=True)
                else:
                    _, b, j = piece
                    if j == 0:
                        pe.wait_ge(packed, b + 1)
                    dst = dst.bitcast(BF16)
                    if j < CPB:
                        for u in range(H1 // 2):
                            two = qpack[:, j * H1 + 2 * u:j * H1 + 2 * u + 2].rearrange("p h t d -> p (h t d)")
                            last = nc.tensor.transpose(dst[:, u * P:(u + 1) * P], two, identb[:])
                    else:
                        for k in range(2):
                            for g in range(G1):
                                two = kpack[:, (2 * (j - CPB) + k) * G1 + g].rearrange("p r t d -> p (r t d)")
                                last = nc.tensor.transpose(dst[:, (k * G1 + g) * P:(k * G1 + g + 1) * P], two, identb[:])
                last.then_inc(piece_ps, 1)

            def score_tile(n):
                gi, t = divmod(n, NT)
                b, g = divmod(gi, G1)
                if t == 0 and g == 0:
                    pe.wait_ge(piece_out, piece_no("tr", b, 5))
                if n >= 2:
                    pe.wait_ge(p_set, n - 1)
                for hh, kc, bk, col in TILES[t]:
                    h = g * HPG + hh
                    rows = slice(64 * (h % 2), 64 * (h % 2) + 64)
                    w = N - kc * P
                    dst = pair_banks(n)[:, bk, :]
                    nc.tensor.matmul(dst[:, col:col + w], kT[rows, b % 2, g, kc * P:(kc + 1) * P],
                                     qT[rows, b % 2, h // 2, kc * P:N], start=True, stop=False)
                    last = nc.tensor.matmul(dst[:, col:col + P], identb[:], maskb[:], start=False, stop=True)
                last.then_inc(s_ps, 1)

            def pv_step(gi, k):
                b, g = divmod(gi, G1)
                t0, t2, kc, q0, q1 = PV_STEPS[k]
                if k == 0 and gi >= 2:
                    pe.wait_ge(o_out, gi - 1)
                pe.wait_ge(p_set, gi * NT + t2 + 1)
                for hh in range(HPG):
                    t = t2 if hh >= 2 else t0
                    for head, key, bk, col in TILES[t]:
                        if (head, key) == (hh, kc):
                            c0 = bk * 512 + col + q0 - kc * P
                    last = nc.tensor.matmul(bank(4 + gi % 2)[VW * hh:VW * hh + VW, q0:q1], v9[:, b * CPB + kc, g, :],
                                            pT[:, (gi * NT + t) % 4, c0:c0 + q1 - q0],
                                            start=(k == 0), stop=(k == len(PV_STEPS) - 1))
                last.then_inc(pv_done, 1)

            def o_transposes(gi):
                pe.wait_ge(o_out, gi + 1)
                if gi % G1 == 0 and gi >= G1:
                    pe.wait_ge(wo_out, gi // G1)
                elif gi >= 1:
                    pe.wait_ge(ao_set, gi)
                for i in range(CPB):
                    last = nc.tensor.transpose(bank(6)[:, i * P:(i + 1) * P], osb[:, gi % 2, i * P:(i + 1) * P], ident)
                last.then_inc(ot_ps, 1)

            def ao_transposes(b):
                pe.wait_ge(ao_set, (b + 1) * G1)
                for i in range(CPB):
                    last = nc.tensor.transpose(bank(6)[:, i * P:(i + 1) * P], ao[:, i, :], ident)
                last.then_inc(aoT_ps, 1)

            def wo_matmuls(b):
                pe.wait_ge(aoT_out, b + 1)
                for i in range(CPB):
                    last = nc.tensor.matmul(bank(6)[:, i * D:(i + 1) * D], aoT[:, i * P:(i + 1) * P], wo[:],
                                            start=True, stop=True)
                last.then_inc(wo_ps, 1)

            for piece in FIRST:
                fill_piece(piece)
            pe.wait_ge(pool_set, 5)
            score_tile(0)
            for gi in range(GROUPS):
                b, g = divmod(gi, G1)
                for t in range(NT):
                    n = gi * NT + t
                    stop = gi + 1 in (BLOCKS_AFTER, GROUPS) and t == NT - 1
                    if t == 3:
                        pv_step(gi, 1)
                    if t == 0 and gi not in (0, BLOCKS_AFTER):
                        pv_step(gi - 1, 3)
                    if not stop:
                        score_tile(n + 1)
                    if t == 0 and gi not in (0, BLOCKS_AFTER):
                        pv_step(gi - 1, 4)
                    if t == 2:
                        pv_step(gi, 0)
                    if t == 4:
                        pv_step(gi, 2)
                    if stop:
                        pv_step(gi, 3)
                        pv_step(gi, 4)
                    if gi >= 1 and t == 3:
                        o_transposes(gi - 1)
                    if g == 1 and b >= 1 and t == 0:
                        ao_transposes(b - 1)
                    if g == 1 and b >= 1 and t == 2:
                        wo_matmuls(b - 1)
                    if (gi, t) in BEHIND:
                        fill_piece(BEHIND[gi, t])
                if gi + 1 == BLOCKS_AFTER:
                    pe.wait_ge(p_set, BLOCKS_AFTER * NT)
                    pe.wait_ge(o_out, BLOCKS_AFTER)
                    pe.wait_ge(ao_set, BLOCKS_AFTER - 1)
                    pe.wait_ge(piece_out, piece_no("tr", BLOCKS_AFTER // G1, 5))
                    block_matmuls(pe, 1)
                    pe.wait_ge(blk[1]["xbT"], NB1)
                    pe.wait_ge(blk[1]["act"], NB1)
                    pe.wait_ge(blk[1]["aT"], NB1 + 1)
                    pe.wait_ge(blk[1]["yb"], NB1 + 2)
                    score_tile(n + 1)
            o_transposes(GROUPS - 1)
            ao_transposes(B - 1)
            wo_matmuls(B - 1)

        @blkctx.vector
        def _(v):
            count = [0]

            def tick(ins):
                count[0] += 1
                ins.then_inc(chain, 1)

            def sync():
                v.wait_ge(chain, count[0])

            def link(ins):
                tick(ins)
                sync()

            V = nc.vector

            def rsqrt(n):
                a, y, t = nv[:, 0:n], ny[:, 0:n], nt[:, 0:n]
                link(V.tensor_scalar(t.bitcast(I32), a.bitcast(I32), 1, None, ALU.logical_shift_right))
                link(V.tensor_scalar(y.bitcast(I32), t.bitcast(I32), -1.0, float(0x5f3759df), ALU.mult, ALU.add))
                for _ in range(3):
                    link(V.scalar_tensor_tensor(out=t, in0=y, scalar=-0.5, in1=a, op0=ALU.mult, op1=ALU.mult))
                    link(V.tensor_tensor(t, t, y, ALU.mult))
                    link(V.scalar_tensor_tensor(out=y, in0=t, scalar=1.5, in1=y, op0=ALU.add, op1=ALU.mult))

            def normalise(src, dst, n, done=None, times=1):
                for i in range(n):
                    tick(V.bn_stats(st[:, i, :], src(i)))
                sync()
                for i in range(n):
                    tick(V.bn_aggr(mv[:, i, :], st[:, i, :]))
                sync()
                link(V.tensor_scalar(nv[:, 0:n], mv[:, 0:n, 1], LN_EPS, None, ALU.add))
                rsqrt(n)
                for i in range(n):
                    last = V.tensor_scalar(dst(i), src(i), mv[:, i, 0:1], ny[:, i:i + 1], ALU.subtract, ALU.mult)
                    if done is not None and i == n - 1:
                        last.then_inc(done, times)
                    else:
                        tick(last)
                sync()

            CE = [P, C, E]

            def column(a):
                return a[:].rearrange("p (c o) -> p c o", o=1).broadcast_to(CE)

            rev = const[:, K_REV:K_REV + E].rearrange("p (o e) -> p o e", o=1).broadcast_to(CE)

            def best(src, k):
                link(V.tensor_reduce(top[k][:], src[:], AX.X, ALU.max))
                link(V.tensor_tensor(ra[:], src[:], column(top[k]), ALU.is_equal))
                link(V.tensor_tensor(ra[:], ra[:], rev, ALU.mult))
                link(V.tensor_reduce(first[:], ra[:], AX.X, ALU.max))
                link(V.tensor_tensor(oh[k][:], rev, column(first), ALU.is_equal))

            def choose(l):
                best(lg, 0)
                if l == 0:
                    V.tensor_copy(ohb[:], oh[0][:]).then_inc(onehot[0], 1)
                    V.tensor_copy(slotf[:], top[0][:]).then_inc(top_set, 1)
                else:
                    link(V.scalar_tensor_tensor(out=rb[:].rearrange("p c e -> p (c e)"), in0=oh[0][:].rearrange("p c e -> p (c e)"),
                                                scalar=-3e38, in1=lg[:].rearrange("p c e -> p (c e)"),
                                                op0=ALU.mult, op1=ALU.add))
                    best(rb, 1)
                    V.tensor_tensor(ohb[:], oh[0][:], oh[1][:], ALU.add).then_inc(onehot[1], 1)
                    V.tensor_tensor(wts[1][:], top[1][:], top[0][:], ALU.subtract).then_inc(top_set, 1)

            def take_ranks():
                tick(V.tensor_copy(tot[:].rearrange("p c e -> p (c e)"), bank(7)[:, C * E:2 * C * E]))
                return V.tensor_copy(pos[:].rearrange("p c e -> p (c e)"), bank(7)[:, 0:C * E])

            def place(l):
                choices = l + 1
                src, dst = tot, ra
                sh = 1
                while sh < C:
                    tick(V.tensor_copy(dst[:, 0:sh, :], src[:, 0:sh, :]))
                    link(V.tensor_tensor(dst[:, sh:C, :], src[:, sh:C, :], src[:, 0:C - sh, :], ALU.add))
                    src, dst = dst, (rb if dst is ra else ra)
                    sh *= 2
                cum, free = src, dst
                w16 = wide[:, 0:E * C].rearrange("p (e m) -> p e m", e=E)
                cnt = cum[:, C - 1, :].rearrange("p (e o) -> p e o", o=1).broadcast_to([P, E, C])
                m128 = const[:, K_M128:K_M128 + C].rearrange("p (o m) -> p o m", o=1).broadcast_to([P, E, C])
                link(V.tensor_tensor(w16, cnt, m128, ALU.is_gt))
                link(V.tensor_reduce(nblk[:], w16, AX.X, ALU.add))
                a, c = nblk, bend[0]
                for sh in (1, 2, 4):
                    tick(V.tensor_copy(c[:, 0:sh], a[:, 0:sh]))
                    link(V.tensor_tensor(c[:, sh:E], a[:, sh:E], a[:, 0:E - sh], ALU.add))
                    a, c = c, (bend[1] if c is bend[0] else bend[0])
                ends, starts = a, c
                link(V.tensor_tensor(starts[:], ends[:], nblk[:], ALU.subtract))
                link(V.tensor_scalar(starts[:], starts[:], float(P), None, ALU.mult))
                link(V.tensor_tensor(free[:], cum[:], tot[:], ALU.subtract))
                link(V.tensor_tensor(free[:], free[:], starts[:].rearrange("p (o e) -> p o e", o=1).broadcast_to(CE), ALU.add))
                link(V.tensor_tensor(pos[:], pos[:], free[:], ALU.add))
                nb = NB[l]
                wj = wide[0:1, 0:nb * (E - 1)].rearrange("p (j e) -> p j e", j=nb)
                jj = const[0:1, K_J:K_J + nb].rearrange("p (j o) -> p j o", o=1).broadcast_to([1, nb, E - 1])
                en = ends[0:1, 0:E - 1].rearrange("p (o e) -> p o e", o=1).broadcast_to([1, nb, E - 1])
                link(V.tensor_tensor(wj, jj, en, ALU.is_ge))
                link(V.tensor_reduce(bef[:, 0:nb], wj, AX.X, ALU.add))
                link(V.tensor_scalar(bexp[l][:], bef[:, 0:nb], float(EW), None, ALU.mult))
                if l == 0:
                    v.wait_ge(score_set, 1)
                for k in range(choices):
                    link(V.tensor_tensor(ra[:], oh[k][:], pos[:], ALU.mult))
                    link(V.tensor_reduce(first[:], ra[:], AX.X, ALU.add))
                    last = V.tensor_copy(slot[l + k][:], first[:])
                    if k < choices - 1:
                        link(last)
                last.then_inc(routed[l], 1)

            v.wait_ge(const_in, 16)
            tick(V.tensor_copy(identb[:], ident))
            tick(V.tensor_copy(trib[:], const[:, K_TRI:K_TRI + P]))
            tick(V.tensor_copy(maskb[:], const[:, K_MASK:K_MASK + P]))
            v.wait_ge(sel_in, 16)
            V.tensor_copy(selb[:].rearrange("p u d -> p (u d)"), selector).then_inc(casts, 1)
            for l in range(2):
                v.sem_inc(blk[l]["yb"], 2)

            for b in range(B):
                v.wait_ge(x_in[b], 16)
                normalise(lambda i: x[:, b * CPB + i, :], lambda i: xn[:, b * CPB + i, 0:D], CPB, xn_done[0])
            v.wait_ge(logits, B)
            link(V.tensor_copy(lg[:].rearrange("p c e -> p (c e)"), bank(6)[:, 0:C * E]))
            choose(0)
            v.wait_ge(ranks, 1)
            link(take_ranks())
            place(0)
            v.wait_ge(xn_done[0], B)
            V.tensor_tensor(xs[:], xn[:, :, 0:D], score[:].rearrange("p (c o) -> p c o", o=1).broadcast_to([P, C, D]),
                            ALU.mult).then_inc(xs_set, 1)

            v.wait_ge(pool_set, 2)
            for b in range(B):
                v.wait_ge(xk_ps, b + 1)
                if b >= 1:
                    v.wait_ge(den_ps, b)
                    v.wait_ge(xkT_ps, b)
                for k in range(3):
                    u0, m = 3 * k, min(3, PAIRS - 3 * k)
                    src = bank(4 + k)[:, 0:m * (D + 1)].rearrange("p (u n) -> p u n", u=m)
                    for par in range(2):
                        rows = slice(DK * par, DK * par + DK)
                        for first4 in (True, False):
                            us = [u for u in range(u0, u0 + m) if (u < 4) == first4]
                            if us:
                                c0 = den_row(us[0], par, 0) % 32
                                sums = src[rows, us[0] - u0:us[-1] - u0 + 1, D:D + 1].broadcast_to([DK, len(us), 3])
                                tick(V.tensor_copy(ksB[rows, us[0]:us[-1] + 1, c0:c0 + 9:4], sums))
                    last = V.tensor_copy(xk[:, u0:u0 + m, :], src[:, :, 0:D])
                    if k < 2:
                        tick(last)
                last.then_inc(xk_out, 1)
                sync()
                v.wait_ge(den_ps, b + 1)
                link(V.tensor_scalar(dsb[:], bank(7), DEN_EPS, None, ALU.add))
                link(V.reciprocal(rr[:], dsb[:]))
                part = const[:, K_PART:K_PART + 2]
                link(V.tensor_copy(mid[:], rr[:]))
                link(V.scalar_tensor_tensor(out=dsb[:], in0=mid[:], scalar=part[:, 0:1], in1=rr[:],
                                            op0=ALU.mult, op1=ALU.add))
                link(V.tensor_copy(mid[:], dsb[:]))
                link(V.scalar_tensor_tensor(out=rr[:], in0=mid[:], scalar=part[:, 1:2], in1=dsb[:],
                                            op0=ALU.mult, op1=ALU.add))
                if b >= 1:
                    v.wait_ge(bc_ps, 8 * b)
                V.tensor_copy(rd3[:], rr[:]).then_inc(rd3_set, 1)
                for u in range(PAIRS):
                    v.wait_ge(bc_ps, 8 * b + u + 1)
                    V.tensor_tensor(QT[:, b % 2, u, :], QT[:, b % 2, u, :], bank(6 + u % 2), ALU.mult).then_inc(qs_set, 1)
                v.wait_ge(y_ps, b + 1)
                V.tensor_tensor(zt[:], bank(4).rearrange("p (c d) -> p c d", c=CPB),
                                xn[:, b * CPB:(b + 1) * CPB, 0:D], ALU.add).then_inc(y_out, 1)
                v.wait_ge(y_out, b + 1)
                normalise(lambda i: zt[:, i, :], lambda i: zt[:, i, :], CPB)
                if b == 0:
                    v.wait_ge(affine_in, 32)
                g4 = gamma[:].rearrange("p (o d) -> p o d", o=1).broadcast_to([P, CPB, D])
                b4 = beta[:].rearrange("p (o d) -> p o d", o=1).broadcast_to([P, CPB, D])
                xb4 = x[:, b * CPB:(b + 1) * CPB, :]
                link(V.tensor_tensor(zt[:], zt[:], g4, ALU.mult))
                tick(V.tensor_tensor(xb4, xb4, b4, ALU.add))
                sync()
                link(V.tensor_tensor(xb4, xb4, zt[:], ALU.add))

            block_vectors(v, 0)

            for b in range(B):
                shared_add(v, b)
            v.wait_ge(shy_out, B)

            def layer_norm1(b, m):
                for q in range(b, b + m):
                    v.wait_ge(gathered[0][q], 16 * CPB)
                xm = x[:, b * CPB:(b + m) * CPB, :]
                link(V.tensor_tensor(xm, xm, xs[:, b * CPB:(b + m) * CPB, :], ALU.add))
                normalise(lambda i: x[:, b * CPB + i, :], lambda i: xn[:, b * CPB + i, 0:D], m * CPB, xn_done[1], m)

            def take_qkv(b, i):
                src = bank(piece_bank(piece_no("qkv", b, i)))[:, 0:2 * 192].rearrange("p (c n) -> p c n", c=2)
                tick(V.tensor_copy(qk[:, i * 256:(i + 1) * 256].rearrange("p (c n) -> p c n", c=2), src[:, :, 0:128]))
                tick(V.tensor_copy(qk[:, 512 + i * 64:512 + (i + 1) * 64].rearrange("p (c n) -> p c n", c=2),
                                   src[:, :, 128:160]))
                c0 = b * CPB + 2 * i
                for k in range(2):
                    last = V.tensor_copy(v9[:, c0 + k, :, 0:HD], src[:, k, 160:192].rearrange("p (g d) -> p g d", g=G1))
                    if k == 0:
                        tick(last)
                last.then_inc(piece_out, 1)

            def heads(a):
                return a.rearrange("p (h d) -> p h d", d=HD)

            nn, nq = CPB * NQK, CPB * H1

            def pack_norm(b):
                sync()
                link(V.tensor_tensor(tA, qk, qk, ALU.mult))
                link(V.tensor_reduce(nv[:, 0:nn], heads(tA), AX.X, ALU.add))
                rsqrt(nn)
                link(V.tensor_tensor(nt[:, 0:nn], nv[:, 0:nn], ny[:, 0:nn], ALU.mult))
                link(V.tensor_scalar(nt[:, 0:nn], nt[:, 0:nn], NORM_EPS, None, ALU.add))
                link(V.reciprocal(ny[:, 0:nn], nt[:, 0:nn]))
                link(V.tensor_tensor(heads(qk), heads(qk),
                                     ny[:, 0:nn].rearrange("p (h o) -> p h o", o=1).broadcast_to([P, nn, HD]), ALU.mult))

            def pack_rotate(b):
                cc, ss = const[:, K_CC:K_CC + nn * HD], const[:, K_SS:K_SS + nn * HD]
                hf = HD // 2
                tick(V.tensor_tensor(tA, qk, cc, ALU.mult))
                tick(V.tensor_tensor(heads(tB)[:, :, 0:hf], heads(qk)[:, :, hf:HD], heads(ss)[:, :, 0:hf], ALU.mult))
                link(V.tensor_tensor(heads(tB)[:, :, hf:HD], heads(qk)[:, :, 0:hf], heads(ss)[:, :, hf:HD], ALU.mult))
                link(V.tensor_tensor(tA, tA, tB, ALU.add))

            def pack_split(b):
                link(V.tensor_copy(s1, tA))
                link(V.tensor_tensor(tB, tA, s1, ALU.subtract))
                link(V.tensor_copy(s2, tB))
                link(V.tensor_tensor(tA, tB, s2, ALU.subtract))
                link(V.tensor_copy(s3, tA))

            def pack_lay(b):
                if b >= 1:
                    v.wait_ge(piece_ps, piece_no("tr", b - 1, 5))
                for part, t0, t1 in ((s1, 0, 3), (s2, 3, 6), (s3, 6, 8)):
                    src = part[:, 0:nq * HD].rearrange("p (h o d) -> p h o d", o=1, d=HD).broadcast_to([P, nq, t1 - t0, HD])
                    tick(V.tensor_copy(qpack[:, :, t0:t1, :], src))
                for j, part in enumerate((s1, s2, s3)):
                    src = part[:, nq * HD:].rearrange("p (h o d) -> p h o d", o=1, d=HD)
                    m = len(range(j, TERMS, 3))
                    tick(V.tensor_copy(kpack[:, :, 0, j:TERMS:3, :], src.broadcast_to([P, CPB * G1, m, HD])))
                sync()
                V.tensor_copy(kpack[:, :, 1].rearrange("p h t d -> p h (t d)"),
                              kpack[:, :, 0].rearrange("p h t d -> p h (t d)")).then_inc(packed, 1)

            def take_piece(piece):
                if piece[0] in ("x", "tr"):
                    return
                v.wait_ge(piece_ps, piece_no(*piece))
                if piece[0] == "logits":
                    V.tensor_copy(lg[:].rearrange("p c e -> p (c e)"), bank(7)[:, 0:C * E]).then_inc(piece_out, 1)
                    v.wait_ge(piece_out, piece_no(*piece))
                    choose(1)
                elif piece[0] == "ranks":
                    take_ranks().then_inc(piece_out, 1)
                    v.wait_ge(piece_out, piece_no(*piece))
                    sync()
                else:
                    take_qkv(piece[1], piece[2])

            pack_steps = (pack_norm, pack_rotate, pack_split, pack_lay)

            def divide(gi):
                b, g = divmod(gi, G1)
                v.wait_ge(ot_ps, gi + 1)
                if g == 0 and b >= 1:
                    v.wait_ge(aoT_ps, b)
                src = bank(6).rearrange("p (c h w) -> p c h w", c=CPB, w=VW)
                rs = rsum[:].rearrange("p (c h) -> p c h", c=CPB)
                link(V.reciprocal(rs, src[:, :, :, HD]))
                dst = ao.rearrange("p c (h d) -> p c h d", d=HD)[:, :, g * HPG:(g + 1) * HPG, :]
                V.tensor_tensor(dst, src[:, :, :, 0:HD],
                                rsum[:].rearrange("p (c h o) -> p c h o", c=CPB, o=1).broadcast_to([P, CPB, HPG, HD]),
                                ALU.mult).then_inc(ao_set, 1)

            def wo_add(b):
                v.wait_ge(wo_ps, b + 1)
                xb4 = x[:, b * CPB:(b + 1) * CPB, :]
                return V.tensor_tensor(xb4, xb4, bank(6).rearrange("p (c d) -> p c d", c=CPB), ALU.add)

            def add_experts():
                v.wait_ge(score_set, 2)
                link(V.tensor_scalar(slotf[:], wts[1][:], 1.0, None, ALU.add))
                link(V.reciprocal(wts[0][:], slotf[:]))
                link(V.tensor_tensor(wts[1][:], wts[1][:], wts[0][:], ALU.mult))
                v.wait_ge(wo_out, B - 1)
                for k, src in enumerate((xs, yg2)):
                    v.wait_ge(gathered[1][k], 16 * C)
                    for c in range(C):
                        last = V.scalar_tensor_tensor(out=x[:, c, :], in0=src[:, c, :], scalar=wts[k][:, c:c + 1],
                                                      in1=x[:, c, :], op0=ALU.mult, op1=ALU.add)
                        if k == 1 and c % CPB == CPB - 1 and c < C - 1:
                            last.then_inc(fin, 1)
                        else:
                            tick(last)
                    sync()

            layer_norm1(0, 1)
            for piece in FIRST:
                take_piece(piece)
            for step in pack_steps:
                step(0)
            layer_norm1(1, 3)
            for gi in range(GROUPS):
                b, g = divmod(gi, G1)
                if gi == BLOCKS_AFTER:
                    block_vectors(v, 1)
                if gi == GROUPS - 2:
                    add_experts()
                for t in range(NT):
                    if gi >= 1 and t == 3:
                        divide(gi - 1)
                    if g == 1 and b >= 1 and t == 2:
                        wo_add(b - 1).then_inc(wo_out, 1)
                    if (gi, t) in BEHIND:
                        take_piece(BEHIND[gi, t])
                    if (gi, t) in PACK:
                        q, step = PACK[gi, t]
                        pack_steps[step](q)
                    if (gi, t) == (2, 4):
                        place(1)
            divide(GROUPS - 1)
            wo_add(B - 1).then_inc(fin, 1)

_INS = ["x", "wq", "wk", "wvT", "wfc", "gamma", "beta", "gate", "shg", "shu", "shd", "experts0",
        "wqkv", "wo", "wgT", "experts1", "const"]


def expert_columns(gate, up, down):
    down = down.reshape(E, 2, P, D).transpose(2, 0, 1, 3).reshape(P, E, 2 * D)
    return np.ascontiguousarray(np.concatenate([gate.transpose(1, 0, 2), up.transpose(1, 0, 2), down], 2).reshape(P, E * EW))


def kernel(L0_attn_inputs, L0_attn_W_Q, L0_attn_W_K, L0_attn_W_V, L0_attn_W_fc, L0_attn_gamma, L0_attn_beta,
           L0_ffn_gate_w, L0_ffn_sh_gate, L0_ffn_sh_up, L0_ffn_sh_down, L0_ffn_rt_gate, L0_ffn_rt_up, L0_ffn_rt_down,
           L1_attn_w_qkv, L1_attn_w_o, L1_ffn_Wg, L1_ffn_W1, L1_ffn_W2, L1_ffn_W3):
    import concourse.bacc as bacc
    from concourse.bass_utils import run_bass_kernel_spmd

    t, a = np.ascontiguousarray, np.asarray
    values = [
        t(L0_attn_inputs), t(L0_attn_W_Q), t(L0_attn_W_K), t(np.asarray(L0_attn_W_V).T), t(L0_attn_W_fc),
        t(L0_attn_gamma), t(L0_attn_beta), t(L0_ffn_gate_w), t(L0_ffn_sh_gate), t(L0_ffn_sh_up), t(L0_ffn_sh_down),
        expert_columns(a(L0_ffn_rt_gate), a(L0_ffn_rt_up), a(L0_ffn_rt_down)), t(L1_attn_w_qkv), t(L1_attn_w_o),
        t(a(L1_ffn_Wg).T), expert_columns(*(a(w).transpose(0, 2, 1) for w in (L1_ffn_W1, L1_ffn_W2, L1_ffn_W3))),
        constants(),
    ]
    nc = bacc.Bacc("TRN2", target_bir_lowering=False, num_devices=1)
    arrays, args = {}, []
    for name, a in zip(_INS, values):
        arrays[f"in_{name}"] = a
        args.append(nc.dram_tensor(f"in_{name}", a.shape, mybir.dt.from_np(a.dtype), kind="ExternalInput").ap())
    args.append(nc.dram_tensor("out_x", (B, N, D), F32, kind="ExternalOutput").ap())
    build(nc, *args)
    r = run_bass_kernel_spmd(nc, [arrays], core_ids=[0])
    return r.results[0]["out_x"]
```

```python
import concourse.bass as bass
from concourse import mybir
from concourse.alu_op_type import AluOpType as ALU
from contextlib import ExitStack
import numpy as np

F32 = mybir.dt.float32
BF16 = mybir.dt.bfloat16
F32R = mybir.dt.float32r
I32 = mybir.dt.int32
ACT = mybir.ActivationFunctionType
AX = mybir.AxisListType

P = 128
D = 128
B, N = 4, 512
CPB = N // P
C = B * CPB
E = 8
I = 256
LN_EPS = 1e-5

H0, DK = 16, 64
PAIRS = H0 * DK // P
DEN_EPS = 1e-8

H1, G1, HD = 16, 4, 8
HPG = H1 // G1
NQK = H1 + G1
NORM_EPS = 1e-10
TERMS = 8
VW = 32
MASKED = -1e30
GU = 2 * I
EW = (GU + 2 * D, GU)

NB0 = C + E - 1
NB1 = 2 * C + E - 1
DEPTH = 4

K_ID, K_TRI, K_MASK, K_REV = 0, 128, 256, 384
K_M128 = K_REV + E
K_J = K_M128 + C
K_PART = K_J + NB1
K_CC = K_PART + 2
K_SS = K_CC + CPB * NQK * HD
K_SEL = K_SS + CPB * NQK * HD
K_END = K_SEL + PAIRS * P


def den_row(pair, half, part):
    return 32 * (pair % 4) + 4 * part + 2 * (pair // 4) + half


def constants():
    k = np.zeros((P, K_END), np.float32)
    i = np.arange(P)
    k[:, K_ID:K_ID + P] = i[:, None] == i[None, :]
    k[:, K_TRI:K_TRI + P] = i[:, None] < i[None, :]
    k[:, K_MASK:K_MASK + P] = np.where(i[:, None] > i[None, :], np.float32(MASKED), 0)
    for p in range(PAIRS):
        for half in range(2):
            for part in range(3):
                col = K_SEL + p * P + half * DK
                k[den_row(p, half, part), col:col + DK] = 1
    k[:, K_PART] = -(i % 32 // 4 >= 1).astype(np.float32)
    k[:, K_PART + 1] = -(i % 32 // 4 == 2).astype(np.float32)
    k[:, K_REV:K_REV + E] = E - np.arange(E)
    k[:, K_M128:K_M128 + C] = P * np.arange(C)
    k[:, K_J:K_J + NB1] = np.arange(NB1)
    half = HD // 2
    inv = (np.float32(1) / np.float32(10000) ** (np.arange(half, dtype=np.float32) / np.float32(half))).astype(np.float32)
    chunk_of = [c for c in range(CPB) for _ in range(H1)] + [c for c in range(CPB) for _ in range(G1)]
    for n, c in enumerate(chunk_of):
        ang = (np.arange(c * P, (c + 1) * P, dtype=np.float32)[:, None] * inv).astype(np.float32)
        cos, sin = np.cos(ang), np.sin(ang)
        k[:, K_CC + n * HD:K_CC + (n + 1) * HD] = np.concatenate([cos, cos], 1)
        k[:, K_SS + n * HD:K_SS + (n + 1) * HD] = np.concatenate([-sin, sin], 1)
    return k


def build(nc, x_d, wq_d, wk_d, wvT_d, wfc_d, gamma_d, beta_d, gate_d, shg_d, shu_d, shd_d,
          experts0_d, wqkv_d, wo_d, wgT_d, experts1_d, const_d, out_d):
    ctx = ExitStack()

    def sb(name, shape, dt=F32):
        return ctx.enter_context(nc.sbuf_tensor(name, shape, dt))

    def sem(name):
        return ctx.enter_context(nc.semaphore(name))

    with ctx:
        const = sb("const", [P, K_SEL])
        ident = const[:, K_ID:K_ID + P]
        identb = sb("identb", [P, P], BF16)
        trib = sb("trib", [P, P], BF16)
        onesb = sb("onesb", [P, P], BF16)
        maskb = sb("maskb", [P, P], BF16)
        selb = sb("selb", [P, PAIRS, P], BF16)
        zero = sb("zero", [P, D])
        gamma = sb("gamma", [P, D])
        beta = sb("beta", [P, D])

        x = sb("x", [P, C, D])
        xn = sb("xn", [P, C, D + 1])
        xs = sb("xs", [P, C, D])
        experts = sb("experts", [P, E * (GU + 2 * D)])
        high, low = sb("high", [P, E * GU]), sb("low", [P, E * GU])
        assert E * GU == 2 * B * N == 4 * H0 * DK
        gate = sb("gate", [P, E])
        gate_parts = sb("gate_parts", [P, 2 * E])
        wg1 = sb("wg1", [P, E])
        xnT, xnT_low = high[:, 0:B * N], high[:, B * N:2 * B * N]
        wq_high, wq_low, wk_high, wk_low = (low[:, i * H0 * DK:(i + 1) * H0 * DK] for i in range(4))
        shgu_high, shgu_low = (w[:, 0:2 * I].rearrange("p (k n) -> p k n", k=2) for w in (wk_high, wk_low))
        shdn = sb("shdn", [P, 2, D])
        wqkv = sb("wqkv", [P, 192])
        wo = sb("wo", [P, D])

        arenaA = sb("arenaA", [P, 12288])
        Ks = arenaA[:, 0:4096].rearrange("p (c k) -> p c k", c=CPB)
        QT = arenaA[:, 4096:12288].rearrange("p (t u n) -> p t u n", t=2, n=N)
        wvT = arenaA[:, 8192:9216].rearrange("p (u d) -> p u d", d=D)
        wfc = arenaA[:, 9216:10240].rearrange("p (u d) -> p u d", d=D)
        shact = arenaA[:, 4096:8192].rearrange("p (b a n) -> p b a n", b=B, n=N)
        pT = arenaA[:, 0:4096].rearrange("p (r n) -> p r n", n=1024)
        qT = arenaA[:, 4096:8192].bitcast(BF16).rearrange("p (t u n) -> p t u n", t=2, n=N)
        kT = arenaA[:, 8192:10240].bitcast(BF16).rearrange("p (t g n) -> p t g n", t=2, n=N)
        xnT1 = arenaA[:, 10240:12288]
        yg2 = arenaA[:, 10240:12288].rearrange("p (c d) -> p c d", d=D)

        arenaB = sb("arenaB", [P, 7168])
        wq = arenaB[:, 0:1024]
        wk = arenaB[:, 1024:2048]
        shgus = arenaB[:, 0:2048].rearrange("p (r a n) -> p r a n", r=2, n=N)
        wvf = arenaB[:, 2048:4096].rearrange("p (e u d) -> p e u d", e=2, d=D)
        xk = arenaB[:, 4096:5120].rearrange("p (u d) -> p u d", d=D)
        xkT = arenaB[:, 5120:6144]
        kvw = arenaB[:, 6144:7168].rearrange("p (u d) -> p u d", d=D)
        qk = arenaB[:, 0:640]
        tA = arenaB[:, 640:1280]
        tB = arenaB[:, 1280:1920]
        qpack = arenaB[:, 2048:4096].bitcast(BF16).rearrange("p (h t d) -> p h t d", t=TERMS, d=HD)
        kpack = arenaB[:, 4096:5120].bitcast(BF16).rearrange("p (h r t d) -> p h r t d", r=2, t=TERMS, d=HD)
        s1 = arenaB[:, 5120:5440].bitcast(BF16)
        s2 = arenaB[:, 5440:5760].bitcast(BF16)
        s3 = arenaB[:, 5760:6080].bitcast(BF16)
        ao = arenaB[:, 6144:6656].rearrange("p (c n) -> p c n", n=D)
        aoT = arenaB[:, 6656:7168]

        arenaC = sb("arenaC", [P, 3072])
        selector = arenaC[:, 0:PAIRS * P]
        shsg = arenaC[:, 0:1024].rearrange("p (a n) -> p a n", n=N)
        v9 = arenaC[:, 0:2048].rearrange("p (c g w) -> p c g w", c=C, w=VW)
        shgu = arenaC[:, 1024:1024 + 2 * I].rearrange("p (k n) -> p k n", k=2)
        osb = arenaC[:, 2048:3072].rearrange("p (t n) -> p t n", n=N)

        ksB = sb("ksB", [P, PAIRS, 32])
        dsb, rr = arenaC[:, 1536:2048], arenaC[:, 2048:2560]
        mid = sb("mid", [P, N], BF16)
        rd3 = sb("rd3", [P, N], BF16)
        zt = sb("zt", [P, CPB, D])

        xb = sb("xb", [P, DEPTH, D])
        xbT = [sb(f"xbT{l}", [P, 2, P]) for l in range(2)]
        xbT_low = sb("xbT_low", [P, 2, P])
        sg = sb("sg", [P, 2, I])
        act = sb("act", [P, 2, I])
        aT = sb("aT", [P, 2, I])
        yb = sb("yb", [P, DEPTH, D])

        st = sb("st", [P, C, 6])
        mv = sb("mv", [P, C, 2])
        nv = sb("nv", [P, 80])
        ny = sb("ny", [P, 80])
        nt = sb("nt", [P, 80])
        lg = sb("lg", [P, C, E])
        oh = [sb(f"oh{i}", [P, C, E]) for i in range(2)]
        ohb = sb("ohb", [P, C, E], BF16)
        ra = sb("ra", [P, C, E])
        rb = sb("rb", [P, C, E])
        tot = sb("tot", [P, C, E])
        pos = sb("pos", [P, C, E])
        top = [sb(f"top{i}", [P, C]) for i in range(2)]
        first = sb("first", [P, C])
        rsum = sb("rsum", [P, CPB * HPG])
        wide = sb("wide", [P, NB1 * E])
        nblk = sb("nblk", [P, E])
        bend = [sb(f"bend{i}", [P, E]) for i in range(2)]
        slotf = sb("slotf", [P, C])
        bef = sb("bef", [1, NB1])
        score = sb("score", [P, C])
        wts = [sb(f"wts{i}", [P, C]) for i in range(2)]
        slot = [sb(f"slot{i}", [P, C], I32) for i in range(3)]
        bexp = [sb(f"bexp{i}", [1, n], I32) for i, n in enumerate((NB0, NB1))]

        ps = ctx.enter_context(nc.psum_tensor("ps", [P, 8, 512], F32))

        def bank(i):
            return ps[:, i, :]

        def pair_banks(n):
            return ps[:, 2 * (n % 2):2 * (n % 2) + 2, :]

        NB = (NB0, NB1)
        xs_dr = [nc.dram_tensor(f"sorted_x{l}", [NB[l] * P, D], F32, kind="Internal").ap() for l in range(2)]
        y_dr = [nc.dram_tensor(f"sorted_y{l}", [NB[l] * P, D], F32, kind="Internal").ap() for l in range(2)]

        x_in = [sem(f"x_in{b}") for b in range(B)]
        const_in = sem("const_in")
        rope_in = sem("rope_in")
        sel_in = sem("sel_in")
        gate_in = sem("gate_in")
        wvf_in = sem("wvf_in")
        wk_in = sem("wk_in")
        high_set = sem("high_set")
        low_set = sem("low_set")
        xnT_split = sem("xnT_split")
        experts_high = sem("experts_high")
        experts_low = sem("experts_low")
        experts_set = sem("experts_set")
        wq_in = sem("wq_in")
        affine_in = sem("affine_in")
        experts_in = [sem(f"experts_in{l}") for l in range(2)]
        shared_in = sem("shared_in")
        layer1_in = sem("layer1_in")
        zeroed = [sem(f"zeroed{l}") for l in range(2)]
        zero_set = sem("zero_set")
        pool_set = sem("pool_set")
        chain = sem("chain")
        casts = sem("casts")
        xn_done = [sem(f"xn_done{l}") for l in range(2)]
        xnT_ps = sem("xnT_ps")
        xnT_done = sem("xnT_done")
        logits = sem("logits")
        onehot = [sem(f"onehot{l}") for l in range(2)]
        ranks, ranks_out = sem("ranks"), sem("ranks_out")
        gate_split = sem("gate_split")
        lg_out = sem("lg_out")
        routed = [sem(f"routed{l}") for l in range(2)]
        top_set = sem("top_set")
        score_set = sem("score_set")
        xs_set = sem("xs_set")
        scattered = [sem(f"scattered{l}") for l in range(2)]
        gathered = [[sem(f"gathered0_{b}") for b in range(B)],
                    [sem(f"gathered1_{k}") for k in range(2)]]
        unit_ps = sem("unit_ps")
        unit_out = sem("unit_out")
        xk_ps, xk_out = sem("xk_ps"), sem("xk_out")
        xkT_ps, xkT_out = sem("xkT_ps"), sem("xkT_out")
        den_ps, rd3_set = sem("den_ps"), sem("rd3_set")
        kvw_ps, kvw_out = sem("kvw_ps"), sem("kvw_out")
        bc_ps, qs_set = sem("bc_ps"), sem("qs_set")
        y_ps, y_out = sem("y_ps"), sem("y_out")
        sh_sig, sh_m, sh_act = sem("sh_sig"), sem("sh_m"), sem("sh_act")
        shy_ps, shy_out = sem("shy_ps"), sem("shy_out")
        blk = [{n: sem(f"b{l}_{n}") for n in ("xT", "xbT", "xl", "gu", "sg", "m", "act", "aTp", "aT", "y", "yb")}
               | {n: [sem(f"b{l}_{n}{r}") for r in range(DEPTH)] for n in ("ld", "st")} for l in range(2)]
        piece_ps, piece_out = sem("piece_ps"), sem("piece_out")
        packed = sem("packed")
        s_ps, p_set, pv_done = sem("s_ps"), sem("p_set"), sem("pv_done")
        o_out = sem("o_out")
        ot_ps, ao_set = sem("ot_ps"), sem("ao_set")
        aoT_ps, aoT_out = sem("aoT_ps"), sem("aoT_out")
        wo_ps, wo_out = sem("wo_ps"), sem("wo_out")
        fin, stored = sem("fin"), sem("stored")

        TILES = [
            [(0, 0, 0, 0), (1, 0, 1, 0)],
            [(2, 0, 0, 0), (3, 0, 1, 0)],
            [(0, 1, 0, 0), (0, 3, 0, 384), (1, 1, 1, 0), (1, 3, 1, 384)],
            [(2, 1, 0, 0), (2, 3, 0, 384), (3, 1, 1, 0), (3, 3, 1, 384)],
            [(0, 2, 0, 0), (2, 2, 0, 256), (1, 2, 1, 0), (3, 2, 1, 256)],
        ]
        NT = len(TILES)
        GROUPS = B * G1
        PV_STEPS = [(0, 1, 0, 0, N // 2), (0, 1, 0, N // 2, N), (2, 3, 1, P, N), (2, 3, 3, 3 * P, N), (4, 4, 2, 2 * P, N)]
        PV_DONE = [2, 2, 4, 4, 5]
        FIRST = [("x", 0), ("qkv", 0, 0), ("qkv", 0, 1)] + [("tr", 0, j) for j in range(6)]
        BEHIND = {
            (0, 1): ("x", 1), (0, 2): ("qkv", 1, 0), (0, 3): ("qkv", 1, 1), (1, 2): ("x", 2), (1, 3): ("x", 3),
            (1, 4): ("logits",), (2, 1): ("tr", 1, 0), (2, 2): ("tr", 1, 1), (2, 3): ("ranks",), (2, 4): ("tr", 1, 2),
            (3, 0): ("tr", 1, 3), (3, 2): ("tr", 1, 4), (3, 3): ("tr", 1, 5), (3, 4): ("qkv", 2, 0),
            (4, 0): ("qkv", 2, 1), (6, 0): ("qkv", 3, 0), (6, 1): ("tr", 2, 0), (6, 2): ("qkv", 3, 1),
            (6, 3): ("tr", 2, 1), (6, 4): ("tr", 2, 2), (7, 0): ("tr", 2, 3), (7, 2): ("tr", 2, 4), (7, 3): ("tr", 2, 5),
            (8, 1): ("tr", 3, 0), (8, 4): ("tr", 3, 1), (9, 2): ("tr", 3, 2), (10, 0): ("tr", 3, 3),
            (10, 3): ("tr", 3, 4), (11, 1): ("tr", 3, 5),
        }
        PIECES = FIRST + [BEHIND[at] for at in sorted(BEHIND)]
        PACK = {(0, 4): (1, 0), (1, 0): (1, 1), (1, 1): (1, 2), (1, 2): (1, 3),
                (4, 0): (2, 0), (4, 4): (2, 1), (5, 0): (2, 2), (5, 1): (2, 3),
                (6, 2): (3, 0), (6, 4): (3, 1), (7, 0): (3, 2), (7, 4): (3, 3)}
        BLOCKS_AFTER = 2 * G1

        def piece_bank(n):
            return 7 if n > len(FIRST) or n % 2 else 6

        def piece_no(*piece):
            return PIECES.index(piece) + 1

        SHARED_UNITS = 2 + 8 * B

        BLOCKS0_AHEAD = B - 1
        SHARED_AHEAD = 2

        def block_dmas(sp, l):
            s, n = blk[l], NB[l]

            def load(it, r):
                t = it * DEPTH + r
                sp.dma_start(xb[:, r % DEPTH, :], xs_dr[l][bass.ts(t, P), :]).then_inc(s["ld"][r % DEPTH], 16)

            def store(it, r):
                t = it * DEPTH + r
                sp.wait_ge(s["yb"], t + 3)
                sp.dma_start(y_dr[l][bass.ts(t, P), :], yb[:, r % DEPTH, :]).then_inc(s["st"][r % DEPTH], 16)

            for q in s["st"]:
                sp.sem_inc(q, 16)
            sp.wait_ge(scattered[l], 16 * C * (l + 1))
            for t in range(DEPTH):
                load(0, t)
            for k in range(3):
                sp.wait_ge(s["xT"], k + 1)
                load(1, k)
            with sp.Fori(0, (n - 7) // DEPTH) as it:
                for r in range(DEPTH):
                    sp.wait_ge(s["xT"], it * DEPTH + (4 + r))
                    load(it, 7 + r)
                    store(it, r)
            for t in range(n - 7, n):
                store(0, t)
            for r, q in enumerate(s["st"]):
                sp.wait_ge(q, 16 * (1 + len(range(r, n, DEPTH))))

        def o_evac(sc, gi):
            sc.wait_ge(pv_done, (gi + 1) * NT)
            if gi >= 2:
                sc.wait_ge(ot_ps, gi - 1)
            nc.scalar.activation(osb[:, gi % 2, :], bank(4 + gi % 2), ACT.Copy).then_inc(o_out, 1)

        def ao_evac(sc, b):
            sc.wait_ge(aoT_ps, b + 1)
            if b >= 1:
                sc.wait_ge(wo_ps, b)
            nc.scalar.activation(aoT, bank(6), ACT.Copy).then_inc(aoT_out, 1)

        def block_acts(sc, l):
            s, n = blk[l], NB[l]

            def x_evac(it, r):
                sc.wait_ge(s["xT"], it * DEPTH + (r + 1))
                dst = xbT[l][:, r % 2, :]
                nc.scalar.activation(dst.bitcast(F32R) if l else dst, bank(r % 2)[:, 0:P], ACT.Copy).then_inc(s["xbT"], 1)

            def sigmoid(it, r):
                sc.wait_ge(s["gu"], it * DEPTH + (r + 1))
                nc.scalar.activation(sg[:, r % 2, :], bank(2 + r % 2)[:, 0:I], ACT.Sigmoid).then_inc(s["sg"], 1)

            def a_evac(it, r):
                sc.wait_ge(s["aTp"], it * DEPTH + (r + 1))
                nc.scalar.activation(aT[:, r % 2, :], bank(4 + r % 2)[:, 0:I], ACT.Copy).then_inc(s["aT"], 1)

            sc.sem_inc(s["aT"], 1)
            x_evac(0, 0)
            x_evac(0, 1)
            sigmoid(0, 0)
            x_evac(0, 2)
            sigmoid(0, 1)
            a_evac(0, 0)
            with sc.Fori(0, (n - 3) // DEPTH) as it:
                for r in range(DEPTH):
                    t = it * DEPTH + (2 + r)
                    sc.wait_ge(s["gu"], t)
                    x_evac(it, 3 + r)
                    sc.wait_ge(s["act"], t - 1)
                    sigmoid(it, 2 + r)
                    sc.wait_ge(s["y"], t - 1)
                    a_evac(it, 1 + r)
            t = n - 1
            sc.wait_ge(s["act"], t - 1)
            sigmoid(0, t)
            sc.wait_ge(s["y"], t - 1)
            a_evac(0, t - 1)
            sc.wait_ge(s["y"], t)
            a_evac(0, t)

        def block_matmuls(pe, l):
            s, n = blk[l], NB[l]

            at = {}

            def find_experts(t0):
                _, values = nc.values_load_multi_w_load_instructions(
                    bexp[l][0:1, t0:min(t0 + 4, n)], engines=(mybir.EngineType.PE,), min_val=0, max_val=(E - 1) * EW[l],
                    skip_runtime_bounds_check_because="route() counts at most E - 1 experts")
                for k, value in enumerate(values):
                    at[t0 + k] = value

            read = s["xl"] if l else s["xbT"]

            def x_transpose(t):
                pe.wait_ge(s["ld"][t % DEPTH], 16 * (t // DEPTH + 1))
                if t >= 2:
                    pe.wait_ge(read, t - 1)
                nc.tensor.transpose(bank(t % 2)[:, 0:P], xb[:, t % DEPTH, :], ident).then_inc(s["xT"], 1)

            def gate_up(t):
                pe.wait_ge(read, t + 1)
                if t >= 2:
                    pe.wait_ge(s["act"], t - 1)
                if l == 0:
                    nc.tensor.matmul(bank(2 + t % 2), xbT[0][:, t % 2, :], experts[:, bass.ds(at[t], GU)],
                                     start=True, stop=True).then_inc(s["gu"], 1)
                    return
                for x_part, w, first, last in ((xbT[1], high, True, False), (xbT[1], low, False, False),
                                               (xbT_low, high, False, True)):
                    out = nc.tensor.matmul(bank(2 + t % 2), x_part[:, t % 2, :].bitcast(F32R),
                                           w[:].bitcast(F32R)[:, bass.ds(at[t], GU)], start=first, stop=last)
                out.then_inc(s["gu"], 1)

            def a_transposes(t):
                pe.wait_ge(s["act"], t + 1)
                if t >= 2:
                    pe.wait_ge(s["aT"], t)
                for a in range(2):
                    last = nc.tensor.transpose(bank(4 + t % 2)[:, a * P:(a + 1) * P], act[:, t % 2, a * P:(a + 1) * P], ident)
                last.then_inc(s["aTp"], 1)

            def down(t):
                pe.wait_ge(s["aT"], t + 2)
                pe.wait_ge(s["yb"], t + 1)
                down0 = (GU, 0)[l]
                for a in range(2):
                    last = nc.tensor.matmul(bank(6 + t % 2)[:, 0:D], aT[:, t % 2, a * P:(a + 1) * P],
                                            experts[:, bass.ds(at[t] + (down0 + a * D), D)],
                                            start=(a == 0), stop=(a == 1))
                last.then_inc(s["y"], 1)

            if l == 0:
                pe.wait_ge(experts_in[0], 16)
            else:
                pe.wait_ge(experts_set, 1)
            pe.wait_ge(routed[l], 1)
            pe.sem_inc(s["y"], 1)
            find_experts(0)
            x_transpose(0)
            for t in range(n + 2):
                if t % 4 == 3 and t + 1 < n:
                    find_experts(t + 1)
                if t + 1 < n:
                    x_transpose(t + 1)
                if t < n:
                    gate_up(t)
                if t >= 2:
                    down(t - 2)
                if 1 <= t <= n:
                    a_transposes(t - 1)

        def shared_add(v, b):
            v.wait_ge(shy_ps, b + 1)
            xb4 = x[:, b * CPB:(b + 1) * CPB, :]
            nc.vector.tensor_tensor(xb4, xb4, bank(5 - b % 2).rearrange("p (c d) -> p c d", c=CPB),
                                    ALU.add).then_inc(shy_out, 1)

        def block_vectors(v, l):
            s, n = blk[l], NB[l]
            V = nc.vector

            def x_low(it, r):
                v.wait_ge(s["xbT"], it * DEPTH + (r + 1))
                V.tensor_tensor(xbT_low[:, r % 2, :].bitcast(F32R), bank(r % 2)[:, 0:P], xbT[1][:, r % 2, :],
                                ALU.subtract).then_inc(s["xl"], 1)

            def activate(it, r):
                t = it * DEPTH + r
                v.wait_ge(s["sg"], t + 1)
                gu = bank(2 + r % 2)
                V.tensor_tensor(act[:, r % 2, :], sg[:, r % 2, :], gu[:, 0:I], ALU.mult).then_inc(s["m"], 1)
                v.wait_ge(s["m"], t + 1)
                V.tensor_tensor(act[:, r % 2, :], act[:, r % 2, :], gu[:, I:2 * I], ALU.mult).then_inc(s["act"], 1)

            def take_y(it, r):
                t = it * DEPTH + r
                v.wait_ge(s["y"], t + 2)
                v.wait_ge(s["st"][r % DEPTH], (it + r // DEPTH + 1) * 16)
                V.tensor_copy(yb[:, r % DEPTH, :], bank(6 + r % 2)[:, 0:D]).then_inc(s["yb"], 1)

            if l == 1:
                x_low(0, 0)
                x_low(0, 1)
            activate(0, 0)
            if l == 1:
                x_low(0, 2)
            activate(0, 1)
            with v.Fori(0, (n - 3) // DEPTH) as it:
                for r in range(DEPTH):
                    if l == 1:
                        x_low(it, 3 + r)
                    v.wait_ge(s["aTp"], it * DEPTH + (1 + r))
                    activate(it, 2 + r)
                    take_y(it, r)
            v.wait_ge(s["aTp"], n - 2)
            activate(0, n - 1)
            for t in range(n - 3, n):
                take_y(0, t)

        blkctx = ctx.enter_context(nc.Block())

        @blkctx.sync
        def _(sp):
            for b in range(B):
                sp.dma_start(x[:, b * CPB:(b + 1) * CPB, :],
                             x_d[b].rearrange("(c p) d -> p c d", p=P)).then_inc(x_in[b], 16)
                if b == 1:
                    sp.dma_start(wk, wk_d).then_inc(wk_in, 16)
            sp.dma_start(wq, wq_d).then_inc(wq_in, 16)
            sp.wait_ge(zero_set, 1)
            for l in range(2):
                sp.dma_start(xs_dr[l].rearrange("(n p) d -> p n d", p=P),
                             zero[:, :].rearrange("p (a d) -> p a d", a=1).broadcast_to([P, NB[l], D])
                             ).then_inc(zeroed[l], 16)
            sp.dma_start(experts[:], experts0_d).then_inc(experts_in[0], 16)
            sp.dma_start(shgu[:, 0, :], shg_d).then_inc(shared_in, 16)
            sp.dma_start(shgu[:, 1, :], shu_d).then_inc(shared_in, 16)
            sp.dma_start(shdn[:], shd_d.rearrange("(a p) d -> p a d", p=P)).then_inc(shared_in, 16)
            sp.dma_start(wqkv[:], wqkv_d).then_inc(layer1_in, 16)
            sp.dma_start(wo[:], wo_d).then_inc(layer1_in, 16)
            sp.dma_start(wg1[:], wgT_d).then_inc(layer1_in, 16)
            block_dmas(sp, 0)
            sp.wait_ge(blk[0]["y"], NB0 + 1)
            for b in range(B):
                sp.wait_ge(gathered[0][b], 16 * CPB)
            sp.dma_start(experts[:], experts1_d).then_inc(experts_in[1], 16)
            block_dmas(sp, 1)
            for b in range(B):
                sp.wait_ge(fin, b + 1)
                sp.dma_start(out_d[b].rearrange("(c p) d -> p c d", p=P),
                             x[:, b * CPB:(b + 1) * CPB, :]).then_inc(stored, 16)
            sp.wait_ge(stored, 16 * B)

        @blkctx.gpsimd
        def _(pool):
            nc.gpsimd.memset(zero[:], 0.0).then_inc(zero_set, 1)
            nc.gpsimd.memset(xn[:, :, D:D + 1], 1.0).then_inc(pool_set, 1)
            nc.gpsimd.memset(ksB[:], 0.0).then_inc(pool_set, 1)
            nc.gpsimd.memset(onesb[:], 1.0).then_inc(pool_set, 1)

            def split_projection(n, w, w_high, w_low, loaded, count):
                pool.wait_ge(loaded, count)
                if n == 2:
                    pool.wait_ge(unit_ps, 2 + 8 * (B - 1) + CPB)
                    nc.gpsimd.tensor_copy(w_high.bitcast(F32R), w).then_inc(high_set, 1)
                pool.wait_ge(high_set, n + 1)
                nc.gpsimd.tensor_tensor(w_low.bitcast(F32R), w, w_high, ALU.subtract).then_inc(low_set, 1)

            split_projection(0, wk, wk_high, wk_low, wk_in, 16)
            split_projection(1, wq, wq_high, wq_low, wq_in, 16)

            def split_experts():
                quarter = E * GU // 4
                for i in range(4):
                    cols = slice(i * quarter, (i + 1) * quarter)
                    nc.gpsimd.tensor_copy(high[:, cols].bitcast(F32R), experts[:, cols]).then_inc(experts_high, 1)
                    pool.wait_ge(experts_high, i + 1)
                    nc.gpsimd.tensor_tensor(low[:, cols].bitcast(F32R), experts[:, cols], high[:, cols],
                                            ALU.subtract).then_inc(experts_low, 1)
                pool.wait_ge(experts_low, 4)
                downs = experts[:, E * GU:].rearrange("p (e d) -> p e d", e=E)
                places = experts[:, 0:E * GU].rearrange("p (e n) -> p e n", e=E)[:, :, 0:2 * D]
                nc.gpsimd.tensor_copy(places, downs).then_inc(experts_set, 1)

            def scatter(l, k, src):
                for c in range(C):
                    pool.indirect_dma_start(
                        out=xs_dr[l][:, :], out_offset=bass.IndirectOffsetOnAxis(slot[l + k][:, c:c + 1], 0),
                        in_=src(c), in_offset=None).then_inc(scattered[l], 16)

            def gather(l, k, dst, chunks=range(C)):
                for c in chunks:
                    pool.indirect_dma_start(
                        out=dst(c), out_offset=None, in_=y_dr[l][:, :],
                        in_offset=bass.IndirectOffsetOnAxis(slot[l + k][:, c:c + 1], 0)
                        ).then_inc(gathered[l][k if l else c // CPB], 16)

            def stored_blocks(l):
                for r, q in enumerate(blk[l]["st"]):
                    pool.wait_ge(q, 16 * (1 + len(range(r, NB[l], DEPTH))))

            pool.wait_ge(zeroed[0], 16)
            pool.wait_ge(routed[0], 1)
            pool.wait_ge(xs_set, 1)
            scatter(0, 0, lambda c: xs[:, c, :])
            split_projection(2, shgu, shgu_high, shgu_low, shared_in, 48)
            pool.wait_ge(y_ps, BLOCKS0_AHEAD)
            pool.wait_ge(scattered[0], 16 * C)
            for b in range(B):
                if b >= 1:
                    if b == 1:
                        stored_blocks(0)
                    gather(0, 0, lambda c: xs[:, c, :], range((b - 1) * CPB, b * CPB))
                for a in range(2):
                    i = 2 * b + a
                    pool.wait_ge(sh_sig, i + 1)
                    pool.wait_ge(unit_out, SHARED_UNITS + i + 1)
                    nc.gpsimd.tensor_tensor(shact[:, b, a, :], shsg[:, a, :], shgus[:, a, 0, :], ALU.mult).then_inc(sh_m, 1)
                    pool.wait_ge(sh_m, i + 1)
                    nc.gpsimd.tensor_tensor(shact[:, b, a, :], shact[:, b, a, :], shgus[:, a, 1, :],
                                            ALU.mult).then_inc(sh_act, 1)
            gather(0, 0, lambda c: xs[:, c, :], range((B - 1) * CPB, C))
            pool.wait_ge(sh_act, 2 * B)
            nc.gpsimd.memset(v9[:, :, :, HD:VW], 0.0).then_inc(pool_set, 1)
            pool.wait_ge(pool_set, 4)
            nc.gpsimd.memset(v9[:, :, :, HD:HD + 1], 1.0).then_inc(pool_set, 1)
            pool.wait_ge(experts_in[1], 16)
            split_experts()
            pool.wait_ge(zeroed[1], 16)
            pool.wait_ge(routed[1], 1)
            for k in range(2):
                scatter(1, k, lambda c: xn[:, c, 0:D])
            stored_blocks(1)
            gather(1, 0, lambda c: xs[:, c, :])
            gather(1, 1, lambda c: yg2[:, c, :])

        @blkctx.scalar
        def _(sc):
            sc.dma_start(const[:, 0:K_CC], const_d[:, 0:K_CC]).then_inc(const_in, 16)
            sc.dma_start(gate[:], gate_d).then_inc(gate_in, 16)
            sc.dma_start(wvT, wvT_d.rearrange("(u q) d -> q u d", q=P)).then_inc(wvf_in, 16)
            sc.dma_start(wfc, wfc_d.rearrange("(u q) d -> q u d", q=P)).then_inc(wvf_in, 16)
            sc.dma_start(gamma[:], gamma_d.rearrange("(a d) -> a d", a=1).broadcast_to([P, D])).then_inc(affine_in, 16)
            sc.dma_start(beta[:], beta_d.rearrange("(a d) -> a d", a=1).broadcast_to([P, D])).then_inc(affine_in, 16)
            sc.dma_start(selector, const_d[:, K_SEL:K_END]).then_inc(sel_in, 16)
            sc.dma_start(const[:, K_CC:K_SEL], const_d[:, K_CC:K_SEL]).then_inc(rope_in, 16)

            def take_piece(piece):
                if piece[0] not in ("x", "tr"):
                    return
                sc.wait_ge(piece_ps, piece_no(*piece))
                b = piece[1]
                if piece[0] == "x":
                    nc.scalar.activation(xnT1[:, b * N:(b + 1) * N], bank(piece_bank(piece_no(*piece))),
                                         ACT.Copy).then_inc(piece_out, 1)
                    return
                j = piece[2]
                if j == 0 and b >= 2:
                    sc.wait_ge(s_ps, (b - 1) * G1 * NT)
                src = bank(piece_bank(piece_no(*piece))).bitcast(BF16)
                if j < CPB:
                    nc.scalar.activation(qT[:, b % 2, :, j * P:(j + 1) * P],
                                         src.rearrange("p (u n) -> p u n", n=P), ACT.Copy).then_inc(piece_out, 1)
                else:
                    k = 2 * (j - CPB)
                    nc.scalar.activation(kT[:, b % 2, :, k * P:(k + 2) * P].rearrange("p g (k n) -> p k g n", k=2),
                                         src.rearrange("p (k g n) -> p k g n", k=2, g=G1), ACT.Copy).then_inc(piece_out, 1)

            unit_n = [0]

            def unit(dst, fn):
                n = unit_n[0]
                unit_n[0] += 1
                sc.wait_ge(unit_ps, n + 1)
                nc.scalar.activation(dst, pair_banks(n), fn).then_inc(unit_out, 1)

            def proj_unit(b, i):
                if i < CPB:
                    unit(Ks[:, i, :].rearrange("p (a n) -> p a n", a=2), ACT.Sigmoid)
                else:
                    u = 2 * (i - CPB)
                    unit(QT[:, b % 2, u:u + 2, :], ACT.Sigmoid)

            def xnT_evac(b):
                sc.wait_ge(xnT_ps, b + 1)
                nc.scalar.activation(xnT[:, b * N:(b + 1) * N].bitcast(F32R), bank(4 + b % 2), ACT.Copy).then_inc(xnT_done, 1)

            sc.wait_ge(wk_in, 16)
            nc.scalar.activation(wk_high.bitcast(F32R), wk, ACT.Copy).then_inc(high_set, 1)
            xnT_evac(0)
            sc.wait_ge(wq_in, 16)
            nc.scalar.activation(wq_high.bitcast(F32R), wq, ACT.Copy).then_inc(high_set, 1)
            unit(wvf[:, 0].rearrange("p (a u) d -> p a (u d)", a=2), ACT.Copy)
            unit(wvf[:, 1].rearrange("p (a u) d -> p a (u d)", a=2), ACT.Copy)
            for i in range(8):
                proj_unit(0, i)
                if i % 2 == 1 and i >= 3:
                    xnT_evac(i // 2)
            def shared_unit(i):
                sc.wait_ge(unit_ps, SHARED_UNITS + i + 1)
                if i >= 2:
                    sc.wait_ge(sh_act, i - 1)
                banks = pair_banks(SHARED_UNITS + i)
                nc.scalar.activation(shsg[:, i % 2, :], banks[:, 0, :], ACT.Sigmoid).then_inc(sh_sig, 1)
                nc.scalar.activation(shgus[:, i % 2], banks, ACT.Copy).then_inc(unit_out, 1)

            for b in range(B):
                more = b + 1 < B
                if b == BLOCKS0_AHEAD:
                    for i in range(SHARED_AHEAD):
                        shared_unit(i)
                    block_acts(sc, 0)
                if b == 1:
                    sc.wait_ge(top_set, 1)
                    nc.scalar.activation(score[:], top[0][:], ACT.Sigmoid).then_inc(score_set, 1)

                def units(lo, hi):
                    for i in range(lo, hi):
                        if not more:
                            if i + SHARED_AHEAD < 2 * B:
                                shared_unit(i + SHARED_AHEAD)
                        else:
                            if i == 0:
                                sc.wait_ge(xk_ps, b + 1)
                            if i == CPB and b >= 1:
                                sc.wait_ge(y_ps, b)
                            proj_unit(b + 1, i)

                units(0, 2)
                sc.wait_ge(xkT_ps, b + 1)
                if b >= 1:
                    sc.wait_ge(kvw_ps, b)
                nc.scalar.activation(xkT.rearrange("p (a n) -> p a n", a=2), ps[:, 4:6, :], ACT.Copy).then_inc(xkT_out, 1)
                units(2, 3)
                sc.wait_ge(kvw_ps, b + 1)
                if b >= 1:
                    sc.wait_ge(y_ps, b)
                nc.scalar.activation(kvw.rearrange("p (a u) d -> p a (u d)", a=2), ps[:, 4:6, :], ACT.Copy).then_inc(kvw_out, 1)
                units(3, 8)

            sc.wait_ge(y_ps, B)
            for piece in FIRST:
                if piece == ("tr", 0, 0):
                    sc.wait_ge(shy_ps, B)
                take_piece(piece)

            for gi in range(GROUPS):
                b, g = divmod(gi, G1)
                if gi == BLOCKS_AFTER:
                    block_acts(sc, 1)
                for t in range(NT):
                    n = gi * NT + t
                    if gi >= 1 and t == 2 and gi != BLOCKS_AFTER:
                        o_evac(sc, gi - 1)
                    sc.wait_ge(s_ps, n + 1)
                    if n >= 4:
                        sc.wait_ge(pv_done, (n - 4) // NT * NT + PV_DONE[(n - 4) % NT])
                    nc.scalar.activation(pT[:, n % 4, :].rearrange("p (a n) -> p a n", a=2), pair_banks(n),
                                         ACT.Exp, scale=float(1.0 / np.sqrt(np.float32(HD)))).then_inc(p_set, 1)
                    if b >= 1 and g == 1 and t == 1:
                        ao_evac(sc, b - 1)
                    before = divmod(n - 1, NT)
                    if before in BEHIND and t > 0:
                        take_piece(BEHIND[before])
                if (gi, NT - 1) in BEHIND:
                    take_piece(BEHIND[gi, NT - 1])
                if gi == G1 - 1:
                    sc.wait_ge(top_set, 2)
                    nc.scalar.activation(wts[1][:], wts[1][:], ACT.Exp).then_inc(score_set, 1)
                if gi + 1 in (BLOCKS_AFTER, GROUPS):
                    o_evac(sc, gi)
            ao_evac(sc, B - 1)

        @blkctx.tensor
        def _(pe):
            def split_product(dst, a, b):
                (ah, al), (bh, bl) = a, b
                for lhs, rhs, first, last in ((ah, bh, True, False), (ah, bl, False, False), (al, bh, False, True)):
                    out = nc.tensor.matmul(dst, lhs.bitcast(F32R), rhs.bitcast(F32R), start=first, stop=last)
                return out

            def count_ranks():
                rhs = ohb[:].rearrange("p c e -> p (c e)")
                nc.tensor.matmul(bank(7)[:, 0:C * E], trib[:], rhs, start=True, stop=True)
                return nc.tensor.matmul(bank(7)[:, C * E:2 * C * E], onesb[:], rhs, start=True, stop=True)

            unit_n = [0]

            def unit_begin():
                n = unit_n[0]
                if n >= 2:
                    pe.wait_ge(unit_out, n - 1)
                unit_n[0] += 1
                return pair_banks(n)

            def shared_unit(i):
                b, a = divmod(i, 2)
                dst = unit_begin()
                for k in range(2):
                    last = split_product(dst[:, k, :], [w[:, k, a * P:(a + 1) * P] for w in (shgu_high, shgu_low)],
                                         [w[:, b * N:(b + 1) * N] for w in (xnT, xnT_low)])
                last.then_inc(unit_ps, 1)

            def proj_unit(b, i):
                dst = unit_begin()
                if i < CPB:
                    c = b * CPB + i
                    for a in range(2):
                        last = split_product(dst[:, a, :], [w[:, c * P:(c + 1) * P] for w in (xnT, xnT_low)],
                                             [w[:, a * 512:(a + 1) * 512] for w in (wk_high, wk_low)])
                else:
                    for a in range(2):
                        u = 2 * (i - CPB) + a
                        last = split_product(dst[:, a, :], [w[:, u * P:(u + 1) * P] for w in (wq_high, wq_low)],
                                             [w[:, b * N:(b + 1) * N] for w in (xnT, xnT_low)])
                last.then_inc(unit_ps, 1)

            pe.wait_ge(const_in, 16)
            def x_transposes(b):
                pe.wait_ge(xn_done[0], b + 1)
                if b >= 2:
                    pe.wait_ge(xnT_split, b - 1)
                for i in range(CPB):
                    last = nc.tensor.transpose(bank(4 + b % 2)[:, i * P:(i + 1) * P], xn[:, b * CPB + i, 0:D], ident)
                last.then_inc(xnT_ps, 1)

            def logits0(b):
                pe.wait_ge(xnT_split, b + 1)
                for c in range(b * CPB, (b + 1) * CPB):
                    both = bank(6)[:, c * 2 * E:(c + 1) * 2 * E]
                    nc.tensor.matmul(both, xnT[:, c * P:(c + 1) * P].bitcast(F32R), gate_parts[:].bitcast(F32R),
                                     start=True, stop=False)
                    last = nc.tensor.matmul(both[:, 0:E], xnT_low[:, c * P:(c + 1) * P].bitcast(F32R),
                                            gate_parts[:, 0:E].bitcast(F32R), start=False, stop=True)
                last.then_inc(logits, 1)

            x_transposes(0)
            pe.wait_ge(wvf_in, 32)
            for par in range(2):
                dst = unit_begin()
                rows = slice(DK * par, DK * par + DK)
                for u in range(PAIRS):
                    last = nc.tensor.matmul(dst[:, u // 4, (u % 4) * D:(u % 4 + 1) * D], wvT[rows, u, :], wfc[rows, u, :],
                                            start=True, stop=True)
                last.then_inc(unit_ps, 1)
            pe.wait_ge(gate_split, 1)
            logits0(0)
            pe.wait_ge(low_set, 1)
            for i in range(8):
                if i == CPB:
                    pe.wait_ge(low_set, 2)
                proj_unit(0, i)
                if i % 2 == 1 and i >= 3:
                    x_transposes(i // 2)
                if i % 2 == 0 and i >= 4:
                    logits0(i // 2 - 1)
            logits0(B - 1)
            pe.wait_ge(pool_set, 3)
            def shared_down(b):
                pe.wait_ge(sh_act, 2 * b + 2)
                if b == 1:
                    pe.wait_ge(y_out, B)
                if b >= 2:
                    pe.wait_ge(shy_out, b - 1)
                for i in range(CPB):
                    for a in range(2):
                        last = nc.tensor.matmul(bank(5 - b % 2)[:, i * D:(i + 1) * D], shact[:, b, a, i * P:(i + 1) * P],
                                                shdn[:, a, :], start=(a == 0), stop=(a == 1))
                last.then_inc(shy_ps, 1)

            for b in range(B):
                more = b + 1 < B

                def units(lo, hi):
                    for i in range(lo, hi):
                        if more:
                            proj_unit(b + 1, i)
                        elif i + SHARED_AHEAD < 2 * B:
                            shared_unit(i + SHARED_AHEAD)

                if b == BLOCKS0_AHEAD:
                    pe.wait_ge(low_set, 3)
                    for i in range(SHARED_AHEAD):
                        shared_unit(i)
                    pe.wait_ge(unit_out, SHARED_UNITS + SHARED_AHEAD)
                    pe.wait_ge(y_out, b)
                    pe.wait_ge(kvw_out, b)
                    pe.wait_ge(qs_set, 8 * b)
                    block_matmuls(pe, 0)
                    for name, count in (("xbT", NB0), ("act", NB0), ("aT", NB0 + 1), ("yb", NB0 + 2)):
                        pe.wait_ge(blk[0][name], count)
                pe.wait_ge(unit_out, 2 + 8 * b + CPB)
                if b >= 1:
                    pe.wait_ge(qs_set, 8 * b)
                    if b == 1:
                        pe.wait_ge(onehot[0], 1)
                        count_ranks().then_inc(ranks, 1)
                else:
                    pe.wait_ge(lg_out, 1)
                    pe.wait_ge(xnT_split, B)
                for u in reversed(range(PAIRS)):
                    if u == 2 and b >= 1:
                        pe.wait_ge(y_out, b)
                    dst = ps[:, 4 + u // 3, (u % 3) * (D + 1):(u % 3 + 1) * (D + 1)]
                    for i in range(CPB):
                        last = nc.tensor.matmul(dst, Ks[:, i, u * P:(u + 1) * P], xn[:, b * CPB + i, :],
                                                start=(i == 0), stop=(i == CPB - 1))
                last.then_inc(xk_ps, 1)
                units(0, 2)
                pe.wait_ge(xk_out, b + 1)
                pe.wait_ge(unit_out, 2 + 8 * b + 8)
                if b == 1:
                    pe.wait_ge(ranks_out, 1)
                for u in range(PAIRS):
                    rows = slice(32 * (u % 4), 32 * (u % 4) + 32)
                    last = nc.tensor.matmul(bank(7)[rows, :], ksB[:, u, :], QT[:, b % 2, u, :],
                                            start=(u < 4), stop=(u >= 4))
                last.then_inc(den_ps, 1)
                for u in range(PAIRS):
                    last = nc.tensor.transpose(ps[:, 4 + u // 4, (u % 4) * P:(u % 4 + 1) * P], xk[:, u, :], ident)
                last.then_inc(xkT_ps, 1)
                units(2, 3)
                if b == 0:
                    pe.wait_ge(casts, 1)
                pe.wait_ge(xkT_out, b + 1)
                for h in range(H0):
                    u, par = divmod(h, 2)
                    last = nc.tensor.matmul(ps[DK * par:DK * par + DK, 4 + u // 4, (u % 4) * D:(u % 4 + 1) * D],
                                            xkT[:, h * DK:(h + 1) * DK], wvf[:, par, u, :], start=True, stop=True)
                last.then_inc(kvw_ps, 1)
                units(3, 5)
                pe.wait_ge(rd3_set, b + 1)
                for u in range(PAIRS):
                    if u >= 2:
                        pe.wait_ge(qs_set, 8 * b + u - 1)
                    nc.tensor.matmul(bank(6 + u % 2), selb[:, u, :], rd3[:], start=True, stop=True).then_inc(bc_ps, 1)
                    if u in (1, 4):
                        units(5 + u // 4, 6 + u // 4)
                units(7, 8)
                pe.wait_ge(kvw_out, b + 1)
                if not more:
                    shared_down(0)
                pe.wait_ge(qs_set, 8 * (b + 1))
                for i in range(CPB):
                    for u in range(PAIRS):
                        last = nc.tensor.matmul(bank(4)[:, i * D:(i + 1) * D], QT[:, b % 2, u, i * P:(i + 1) * P],
                                                kvw[:, u, :], start=(u == 0), stop=(u == PAIRS - 1))
                last.then_inc(y_ps, 1)

            pe.wait_ge(layer1_in, 48)
            def fill_piece(piece):
                n = piece_no(*piece)
                before = n - 1 if n > len(FIRST) else n - 2
                if before > 0:
                    pe.wait_ge(piece_out, before)
                dst = bank(piece_bank(n))
                if piece[0] == "x":
                    b = piece[1]
                    pe.wait_ge(xn_done[1], b + 1)
                    for i in range(CPB):
                        last = nc.tensor.transpose(dst[:, i * P:(i + 1) * P], xn[:, b * CPB + i, 0:D], ident)
                elif piece[0] == "logits":
                    for c in range(C):
                        last = nc.tensor.matmul(dst[:, c * E:(c + 1) * E], xnT1[:, c * P:(c + 1) * P], wg1[:],
                                                start=True, stop=True)
                elif piece[0] == "ranks":
                    pe.wait_ge(onehot[1], 1)
                    last = count_ranks()
                elif piece[0] == "qkv":
                    _, b, i = piece
                    pe.wait_ge(piece_out, piece_no("x", b))
                    for k in range(2):
                        c = b * CPB + 2 * i + k
                        last = nc.tensor.matmul(dst[:, k * 192:(k + 1) * 192], xnT1[:, c * P:(c + 1) * P], wqkv[:],
                                                start=True, stop=True)
                else:
                    _, b, j = piece
                    if j in (0, CPB):
                        pe.wait_ge(packed, 2 * b + 1 + (j == CPB))
                    dst = dst.bitcast(BF16)
                    if j < CPB:
                        for u in range(H1 // 2):
                            two = qpack[:, j * H1 + 2 * u:j * H1 + 2 * u + 2].rearrange("p h t d -> p (h t d)")
                            last = nc.tensor.transpose(dst[:, u * P:(u + 1) * P], two, identb[:])
                    else:
                        for k in range(2):
                            for g in range(G1):
                                two = kpack[:, (2 * (j - CPB) + k) * G1 + g].rearrange("p r t d -> p (r t d)")
                                last = nc.tensor.transpose(dst[:, (k * G1 + g) * P:(k * G1 + g + 1) * P], two, identb[:])
                last.then_inc(piece_ps, 1)

            def score_tile(n):
                gi, t = divmod(n, NT)
                b, g = divmod(gi, G1)
                if t == 0 and g == 0:
                    pe.wait_ge(piece_out, piece_no("tr", b, 5))
                if n >= 2:
                    pe.wait_ge(p_set, n - 1)
                for hh, kc, bk, col in TILES[t]:
                    h = g * HPG + hh
                    rows = slice(64 * (h % 2), 64 * (h % 2) + 64)
                    w = N - kc * P
                    dst = pair_banks(n)[:, bk, :]
                    nc.tensor.matmul(dst[:, col:col + w], kT[rows, b % 2, g, kc * P:(kc + 1) * P],
                                     qT[rows, b % 2, h // 2, kc * P:N], start=True, stop=False)
                    last = nc.tensor.matmul(dst[:, col:col + P], identb[:], maskb[:], start=False, stop=True)
                last.then_inc(s_ps, 1)

            def pv_step(gi, k):
                b, g = divmod(gi, G1)
                t0, t2, kc, q0, q1 = PV_STEPS[k]
                if k == 0 and gi >= 2:
                    pe.wait_ge(o_out, gi - 1)
                pe.wait_ge(p_set, gi * NT + t2 + 1)
                for hh in range(HPG):
                    t = t2 if hh >= 2 else t0
                    for head, key, bk, col in TILES[t]:
                        if (head, key) == (hh, kc):
                            c0 = bk * 512 + col + q0 - kc * P
                    last = nc.tensor.matmul(bank(4 + gi % 2)[VW * hh:VW * hh + VW, q0:q1], v9[:, b * CPB + kc, g, :],
                                            pT[:, (gi * NT + t) % 4, c0:c0 + q1 - q0],
                                            start=(k == 0), stop=(k == len(PV_STEPS) - 1))
                last.then_inc(pv_done, 1)

            def o_transposes(gi):
                pe.wait_ge(o_out, gi + 1)
                if gi % G1 == 0 and gi >= G1:
                    pe.wait_ge(wo_out, gi // G1)
                elif gi >= 1:
                    pe.wait_ge(ao_set, gi)
                for i in range(CPB):
                    last = nc.tensor.transpose(bank(6)[:, i * P:(i + 1) * P], osb[:, gi % 2, i * P:(i + 1) * P], ident)
                last.then_inc(ot_ps, 1)

            def ao_transposes(b):
                pe.wait_ge(ao_set, (b + 1) * G1)
                for i in range(CPB):
                    last = nc.tensor.transpose(bank(6)[:, i * P:(i + 1) * P], ao[:, i, :], ident)
                last.then_inc(aoT_ps, 1)

            def wo_matmuls(b):
                pe.wait_ge(aoT_out, b + 1)
                for i in range(CPB):
                    last = nc.tensor.matmul(bank(6)[:, i * D:(i + 1) * D], aoT[:, i * P:(i + 1) * P], wo[:],
                                            start=True, stop=True)
                last.then_inc(wo_ps, 1)

            fill_piece(FIRST[0])
            shared_down(1)
            fill_piece(FIRST[1])
            fill_piece(FIRST[2])
            shared_down(2)
            shared_down(3)
            for piece in FIRST[3:]:
                fill_piece(piece)
            pe.wait_ge(shy_out, B)
            pe.wait_ge(pool_set, 5)
            score_tile(0)
            for gi in range(GROUPS):
                b, g = divmod(gi, G1)
                for t in range(NT):
                    n = gi * NT + t
                    stop = gi + 1 in (BLOCKS_AFTER, GROUPS) and t == NT - 1
                    if t == 3:
                        pv_step(gi, 1)
                    if t == 0 and gi not in (0, BLOCKS_AFTER):
                        pv_step(gi - 1, 3)
                    if not stop:
                        score_tile(n + 1)
                    if t == 0 and gi not in (0, BLOCKS_AFTER):
                        pv_step(gi - 1, 4)
                    if t == 2:
                        pv_step(gi, 0)
                    if t == 4:
                        pv_step(gi, 2)
                    if stop:
                        pv_step(gi, 3)
                        pv_step(gi, 4)
                    if gi >= 1 and t == 3:
                        o_transposes(gi - 1)
                    if g == 1 and b >= 1 and t == 0:
                        ao_transposes(b - 1)
                    if g == 1 and b >= 1 and t == 2:
                        wo_matmuls(b - 1)
                    if (gi, t) in BEHIND:
                        fill_piece(BEHIND[gi, t])
                if gi + 1 == BLOCKS_AFTER:
                    pe.wait_ge(p_set, BLOCKS_AFTER * NT)
                    pe.wait_ge(o_out, BLOCKS_AFTER)
                    pe.wait_ge(ao_set, BLOCKS_AFTER - 1)
                    pe.wait_ge(piece_out, piece_no("tr", BLOCKS_AFTER // G1, 5))
                    block_matmuls(pe, 1)
                    pe.wait_ge(blk[1]["xl"], NB1)
                    pe.wait_ge(blk[1]["act"], NB1)
                    pe.wait_ge(blk[1]["aT"], NB1 + 1)
                    pe.wait_ge(blk[1]["yb"], NB1 + 2)
                    score_tile(n + 1)
            o_transposes(GROUPS - 1)
            ao_transposes(B - 1)
            wo_matmuls(B - 1)

        @blkctx.vector
        def _(v):
            count = [0]

            def tick(ins):
                count[0] += 1
                ins.then_inc(chain, 1)

            def sync():
                v.wait_ge(chain, count[0])

            def link(ins):
                tick(ins)
                sync()

            V = nc.vector

            def rsqrt(n):
                a, y, t = nv[:, 0:n], ny[:, 0:n], nt[:, 0:n]
                link(V.tensor_scalar(t.bitcast(I32), a.bitcast(I32), 1, None, ALU.logical_shift_right))
                link(V.tensor_scalar(y.bitcast(I32), t.bitcast(I32), -1.0, float(0x5f3759df), ALU.mult, ALU.add))
                for _ in range(3):
                    link(V.scalar_tensor_tensor(out=t, in0=y, scalar=-0.5, in1=a, op0=ALU.mult, op1=ALU.mult))
                    link(V.tensor_tensor(t, t, y, ALU.mult))
                    link(V.scalar_tensor_tensor(out=y, in0=t, scalar=1.5, in1=y, op0=ALU.add, op1=ALU.mult))

            def moments(src, n, at=0):
                for i in range(n):
                    tick(V.bn_stats(st[:, at + i, :], src(i)))
                sync()
                for i in range(n):
                    tick(V.bn_aggr(mv[:, at + i, :], st[:, at + i, :]))
                sync()

            def standardise(src, dst, n, at=0, done=None, times=1):
                for i in range(n):
                    last = V.tensor_scalar(dst(i), src(i), mv[:, at + i, 0:1], ny[:, at + i:at + i + 1],
                                           ALU.subtract, ALU.mult)
                    if done is not None and i == n - 1:
                        last.then_inc(done, times)
                    else:
                        tick(last)
                sync()

            def deviations(n):
                link(V.tensor_scalar(nv[:, 0:n], mv[:, 0:n, 1], LN_EPS, None, ALU.add))
                rsqrt(n)

            def normalise(src, dst, n, done=None, times=1, more=0):
                moments(src, n)
                deviations(n + more)
                standardise(src, dst, n, 0, done, times)

            CE = [P, C, E]

            def column(a):
                return a[:].rearrange("p (c o) -> p c o", o=1).broadcast_to(CE)

            rev = const[:, K_REV:K_REV + E].rearrange("p (o e) -> p o e", o=1).broadcast_to(CE)

            def best(src, k):
                link(V.tensor_reduce(top[k][:], src[:], AX.X, ALU.max))
                link(V.tensor_tensor(ra[:], src[:], column(top[k]), ALU.is_equal))
                link(V.tensor_tensor(ra[:], ra[:], rev, ALU.mult))
                link(V.tensor_reduce(first[:], ra[:], AX.X, ALU.max))
                link(V.tensor_tensor(oh[k][:], rev, column(first), ALU.is_equal))

            def choose(l):
                best(lg, 0)
                if l == 0:
                    V.tensor_copy(ohb[:], oh[0][:]).then_inc(onehot[0], 1)
                    V.tensor_copy(slotf[:], top[0][:]).then_inc(top_set, 1)
                else:
                    link(V.scalar_tensor_tensor(out=rb[:].rearrange("p c e -> p (c e)"), in0=oh[0][:].rearrange("p c e -> p (c e)"),
                                                scalar=-3e38, in1=lg[:].rearrange("p c e -> p (c e)"),
                                                op0=ALU.mult, op1=ALU.add))
                    best(rb, 1)
                    V.tensor_tensor(ohb[:], oh[0][:], oh[1][:], ALU.add).then_inc(onehot[1], 1)
                    V.tensor_tensor(wts[1][:], top[1][:], top[0][:], ALU.subtract).then_inc(top_set, 1)

            def take_ranks():
                tick(V.tensor_copy(tot[:].rearrange("p c e -> p (c e)"), bank(7)[:, C * E:2 * C * E]))
                return V.tensor_copy(pos[:].rearrange("p c e -> p (c e)"), bank(7)[:, 0:C * E])

            def place(l):
                choices = l + 1
                src, dst = tot, ra
                sh = 1
                while sh < C:
                    tick(V.tensor_copy(dst[:, 0:sh, :], src[:, 0:sh, :]))
                    link(V.tensor_tensor(dst[:, sh:C, :], src[:, sh:C, :], src[:, 0:C - sh, :], ALU.add))
                    src, dst = dst, (rb if dst is ra else ra)
                    sh *= 2
                cum, free = src, dst
                w16 = wide[:, 0:E * C].rearrange("p (e m) -> p e m", e=E)
                cnt = cum[:, C - 1, :].rearrange("p (e o) -> p e o", o=1).broadcast_to([P, E, C])
                m128 = const[:, K_M128:K_M128 + C].rearrange("p (o m) -> p o m", o=1).broadcast_to([P, E, C])
                link(V.tensor_tensor(w16, cnt, m128, ALU.is_gt))
                link(V.tensor_reduce(nblk[:], w16, AX.X, ALU.add))
                a, c = nblk, bend[0]
                for sh in (1, 2, 4):
                    tick(V.tensor_copy(c[:, 0:sh], a[:, 0:sh]))
                    link(V.tensor_tensor(c[:, sh:E], a[:, sh:E], a[:, 0:E - sh], ALU.add))
                    a, c = c, (bend[1] if c is bend[0] else bend[0])
                ends, starts = a, c
                link(V.tensor_tensor(starts[:], ends[:], nblk[:], ALU.subtract))
                link(V.tensor_scalar(starts[:], starts[:], float(P), None, ALU.mult))
                link(V.tensor_tensor(free[:], cum[:], tot[:], ALU.subtract))
                link(V.tensor_tensor(free[:], free[:], starts[:].rearrange("p (o e) -> p o e", o=1).broadcast_to(CE), ALU.add))
                link(V.tensor_tensor(pos[:], pos[:], free[:], ALU.add))
                nb = NB[l]
                wj = wide[0:1, 0:nb * (E - 1)].rearrange("p (j e) -> p j e", j=nb)
                jj = const[0:1, K_J:K_J + nb].rearrange("p (j o) -> p j o", o=1).broadcast_to([1, nb, E - 1])
                en = ends[0:1, 0:E - 1].rearrange("p (o e) -> p o e", o=1).broadcast_to([1, nb, E - 1])
                link(V.tensor_tensor(wj, jj, en, ALU.is_ge))
                link(V.tensor_reduce(bef[:, 0:nb], wj, AX.X, ALU.add))
                link(V.tensor_scalar(bexp[l][:], bef[:, 0:nb], float(EW[l]), None, ALU.mult))
                if l == 0:
                    v.wait_ge(score_set, 1)
                for k in range(choices):
                    link(V.tensor_tensor(ra[:], oh[k][:], pos[:], ALU.mult))
                    link(V.tensor_reduce(first[:], ra[:], AX.X, ALU.add))
                    last = V.tensor_copy(slot[l + k][:], first[:])
                    if k < choices - 1:
                        link(last)
                last.then_inc(routed[l], 1)

            for l in range(2):
                v.sem_inc(blk[l]["yb"], 2)

            def split_xnT(b):
                v.wait_ge(xnT_done, b + 1)
                cols = slice(b * N, (b + 1) * N)
                V.tensor_tensor(xnT_low[:, cols].bitcast(F32R), bank(4 + b % 2), xnT[:, cols], ALU.subtract).then_inc(xnT_split, 1)

            for b in range(B):
                v.wait_ge(x_in[b], 16)
                normalise(lambda i: x[:, b * CPB + i, :], lambda i: xn[:, b * CPB + i, 0:D], CPB, xn_done[0])
                if b == 0:
                    v.wait_ge(gate_in, 16)
                    link(V.tensor_copy(gate_parts[:, 0:E].bitcast(F32R), gate[:]))
                    V.tensor_tensor(gate_parts[:, E:2 * E].bitcast(F32R), gate[:], gate_parts[:, 0:E],
                                    ALU.subtract).then_inc(gate_split, 1)
                if b == 1:
                    split_xnT(0)
            v.wait_ge(const_in, 16)
            tick(V.tensor_copy(identb[:], ident))
            tick(V.tensor_copy(trib[:], const[:, K_TRI:K_TRI + P]))
            tick(V.tensor_copy(maskb[:], const[:, K_MASK:K_MASK + P]))
            v.wait_ge(sel_in, 16)
            V.tensor_copy(selb[:].rearrange("p u d -> p (u d)"), selector).then_inc(casts, 1)
            for b in range(1, B):
                split_xnT(b)
            v.wait_ge(logits, B)
            halves = bank(6)[:, 0:2 * C * E].rearrange("p (c k e) -> p c k e", k=2, e=E)
            link(V.tensor_copy(lg[:], halves[:, :, 0, :]))
            V.tensor_tensor(lg[:], lg[:], halves[:, :, 1, :], ALU.add).then_inc(lg_out, 1)

            def layer_norm1(b, m, more=0):
                v.wait_ge(shy_out, b + m)
                for q in range(b, b + m):
                    v.wait_ge(gathered[0][q], 16 * CPB)
                xm = x[:, b * CPB:(b + m) * CPB, :]
                link(V.tensor_tensor(xm, xm, xs[:, b * CPB:(b + m) * CPB, :], ALU.add))
                normalise(lambda i: x[:, b * CPB + i, :], lambda i: xn[:, b * CPB + i, 0:D], m * CPB, xn_done[1], m,
                          more)

            def chunk_of_zt(i):
                return zt[:, i, :]

            def finish0(b):
                v.wait_ge(y_out, b + 1)
                if b < B - 1:
                    normalise(chunk_of_zt, chunk_of_zt, CPB)
                else:
                    standardise(chunk_of_zt, chunk_of_zt, CPB, CPB)
                if b == 0:
                    v.wait_ge(affine_in, 32)
                g4 = gamma[:].rearrange("p (o d) -> p o d", o=1).broadcast_to([P, CPB, D])
                b4 = beta[:].rearrange("p (o d) -> p o d", o=1).broadcast_to([P, CPB, D])
                xb4 = x[:, b * CPB:(b + 1) * CPB, :]
                link(V.tensor_tensor(zt[:], zt[:], g4, ALU.mult))
                link(V.tensor_tensor(xb4, xb4, b4, ALU.add))
                link(V.tensor_tensor(xb4, xb4, zt[:], ALU.add))

            v.wait_ge(pool_set, 2)
            for b in range(B):
                if b == 1:
                    v.wait_ge(ranks, 1)
                    take_ranks().then_inc(ranks_out, 1)
                    v.wait_ge(ranks_out, 1)
                v.wait_ge(xk_ps, b + 1)
                if b >= 1:
                    v.wait_ge(den_ps, b)
                    v.wait_ge(xkT_ps, b)
                for k in range(3):
                    u0, m = 3 * k, min(3, PAIRS - 3 * k)
                    src = bank(4 + k)[:, 0:m * (D + 1)].rearrange("p (u n) -> p u n", u=m)
                    for par in range(2):
                        rows = slice(DK * par, DK * par + DK)
                        for first4 in (True, False):
                            us = [u for u in range(u0, u0 + m) if (u < 4) == first4]
                            if us:
                                c0 = den_row(us[0], par, 0) % 32
                                sums = src[rows, us[0] - u0:us[-1] - u0 + 1, D:D + 1].broadcast_to([DK, len(us), 3])
                                tick(V.tensor_copy(ksB[rows, us[0]:us[-1] + 1, c0:c0 + 9:4], sums))
                    last = V.tensor_copy(xk[:, u0:u0 + m, :], src[:, :, 0:D])
                    if k < 2:
                        tick(last)
                last.then_inc(xk_out, 1)
                sync()
                v.wait_ge(den_ps, b + 1)
                link(V.tensor_scalar(dsb, bank(7), DEN_EPS, None, ALU.add))
                link(V.reciprocal(rr, dsb))
                part = const[:, K_PART:K_PART + 2]
                link(V.tensor_copy(mid[:], rr))
                link(V.scalar_tensor_tensor(out=dsb, in0=mid[:], scalar=part[:, 0:1], in1=rr,
                                            op0=ALU.mult, op1=ALU.add))
                link(V.tensor_copy(mid[:], dsb))
                link(V.scalar_tensor_tensor(out=rr, in0=mid[:], scalar=part[:, 1:2], in1=dsb,
                                            op0=ALU.mult, op1=ALU.add))
                if b >= 1:
                    v.wait_ge(bc_ps, 8 * b)
                V.tensor_copy(rd3[:], rr).then_inc(rd3_set, 1)
                for u in range(PAIRS):
                    v.wait_ge(bc_ps, 8 * b + u + 1)
                    V.tensor_tensor(QT[:, b % 2, u, :], QT[:, b % 2, u, :], bank(6 + u % 2), ALU.mult).then_inc(qs_set, 1)
                if b == 0:
                    v.wait_ge(lg_out, 1)
                    choose(0)
                if b == 1:
                    place(0)
                    V.tensor_tensor(xs[:], xn[:, :, 0:D], score[:].rearrange("p (c o) -> p c o", o=1).broadcast_to([P, C, D]),
                                    ALU.mult).then_inc(xs_set, 1)
                if b == B - 1:
                    shared_add(v, 0)
                    layer_norm1(0, 1)
                v.wait_ge(y_ps, b + 1)
                V.tensor_tensor(zt[:], bank(4).rearrange("p (c d) -> p c d", c=CPB),
                                xn[:, b * CPB:(b + 1) * CPB, 0:D], ALU.add).then_inc(y_out, 1)
                if b + 1 == BLOCKS0_AHEAD:
                    block_vectors(v, 0)
                if b < B - 1:
                    finish0(b)
                else:
                    v.wait_ge(y_out, B)
                    moments(chunk_of_zt, CPB, CPB)

            def take_qkv(b, i):
                src = bank(piece_bank(piece_no("qkv", b, i)))[:, 0:2 * 192].rearrange("p (c n) -> p c n", c=2)
                tick(V.tensor_copy(qk[:, i * 256:(i + 1) * 256].rearrange("p (c n) -> p c n", c=2), src[:, :, 0:128]))
                tick(V.tensor_copy(qk[:, 512 + i * 64:512 + (i + 1) * 64].rearrange("p (c n) -> p c n", c=2),
                                   src[:, :, 128:160]))
                c0 = b * CPB + 2 * i
                for k in range(2):
                    last = V.tensor_copy(v9[:, c0 + k, :, 0:HD], src[:, k, 160:192].rearrange("p (g d) -> p g d", g=G1))
                    if k == 0:
                        tick(last)
                last.then_inc(piece_out, 1)

            def heads(a):
                return a.rearrange("p (h d) -> p h d", d=HD)

            nn, nq = CPB * NQK, CPB * H1

            def pack_norm(b):
                sync()
                link(V.tensor_tensor(tA, qk, qk, ALU.mult))
                link(V.tensor_reduce(nv[:, 0:nn], heads(tA), AX.X, ALU.add))
                rsqrt(nn)
                link(V.tensor_tensor(nt[:, 0:nn], nv[:, 0:nn], ny[:, 0:nn], ALU.mult))
                link(V.tensor_scalar(nt[:, 0:nn], nt[:, 0:nn], NORM_EPS, None, ALU.add))
                link(V.reciprocal(ny[:, 0:nn], nt[:, 0:nn]))
                link(V.tensor_tensor(heads(qk), heads(qk),
                                     ny[:, 0:nn].rearrange("p (h o) -> p h o", o=1).broadcast_to([P, nn, HD]), ALU.mult))

            def pack_rotate(b):
                if b == 0:
                    v.wait_ge(rope_in, 16)
                cc, ss = const[:, K_CC:K_CC + nn * HD], const[:, K_SS:K_SS + nn * HD]
                hf = HD // 2
                tick(V.tensor_tensor(tA, qk, cc, ALU.mult))
                tick(V.tensor_tensor(heads(tB)[:, :, 0:hf], heads(qk)[:, :, hf:HD], heads(ss)[:, :, 0:hf], ALU.mult))
                link(V.tensor_tensor(heads(tB)[:, :, hf:HD], heads(qk)[:, :, 0:hf], heads(ss)[:, :, hf:HD], ALU.mult))
                link(V.tensor_tensor(tA, tA, tB, ALU.add))

            def pack_split(b):
                link(V.tensor_copy(s1, tA))
                link(V.tensor_tensor(tB, tA, s1, ALU.subtract))
                link(V.tensor_copy(s2, tB))
                link(V.tensor_tensor(tA, tB, s2, ALU.subtract))
                link(V.tensor_copy(s3, tA))

            def pack_lay(b):
                if b >= 1:
                    v.wait_ge(piece_ps, piece_no("tr", b - 1, 5))
                for part, t0, t1 in ((s1, 0, 3), (s2, 3, 6), (s3, 6, 8)):
                    src = part[:, 0:nq * HD].rearrange("p (h o d) -> p h o d", o=1, d=HD).broadcast_to([P, nq, t1 - t0, HD])
                    last = V.tensor_copy(qpack[:, :, t0:t1, :], src)
                    if part is not s3:
                        tick(last)
                last.then_inc(packed, 1)
                for j, part in enumerate((s1, s2, s3)):
                    src = part[:, nq * HD:].rearrange("p (h o d) -> p h o d", o=1, d=HD)
                    m = len(range(j, TERMS, 3))
                    tick(V.tensor_copy(kpack[:, :, 0, j:TERMS:3, :], src.broadcast_to([P, CPB * G1, m, HD])))
                sync()
                V.tensor_copy(kpack[:, :, 1].rearrange("p h t d -> p h (t d)"),
                              kpack[:, :, 0].rearrange("p h t d -> p h (t d)")).then_inc(packed, 1)

            def take_piece(piece):
                if piece[0] in ("x", "tr"):
                    return
                v.wait_ge(piece_ps, piece_no(*piece))
                if piece[0] == "logits":
                    V.tensor_copy(lg[:].rearrange("p c e -> p (c e)"), bank(7)[:, 0:C * E]).then_inc(piece_out, 1)
                    v.wait_ge(piece_out, piece_no(*piece))
                    choose(1)
                elif piece[0] == "ranks":
                    take_ranks().then_inc(piece_out, 1)
                    v.wait_ge(piece_out, piece_no(*piece))
                    sync()
                else:
                    take_qkv(piece[1], piece[2])

            pack_steps = (pack_norm, pack_rotate, pack_split, pack_lay)

            def divide(gi):
                b, g = divmod(gi, G1)
                v.wait_ge(ot_ps, gi + 1)
                if g == 0 and b >= 1:
                    v.wait_ge(aoT_ps, b)
                src = bank(6).rearrange("p (c h w) -> p c h w", c=CPB, w=VW)
                rs = rsum[:].rearrange("p (c h) -> p c h", c=CPB)
                link(V.reciprocal(rs, src[:, :, :, HD]))
                dst = ao.rearrange("p c (h d) -> p c h d", d=HD)[:, :, g * HPG:(g + 1) * HPG, :]
                V.tensor_tensor(dst, src[:, :, :, 0:HD],
                                rsum[:].rearrange("p (c h o) -> p c h o", c=CPB, o=1).broadcast_to([P, CPB, HPG, HD]),
                                ALU.mult).then_inc(ao_set, 1)

            def wo_add(b):
                v.wait_ge(wo_ps, b + 1)
                xb4 = x[:, b * CPB:(b + 1) * CPB, :]
                return V.tensor_tensor(xb4, xb4, bank(6).rearrange("p (c d) -> p c d", c=CPB), ALU.add)

            def add_experts():
                v.wait_ge(score_set, 2)
                link(V.tensor_scalar(slotf[:], wts[1][:], 1.0, None, ALU.add))
                link(V.reciprocal(wts[0][:], slotf[:]))
                link(V.tensor_tensor(wts[1][:], wts[1][:], wts[0][:], ALU.mult))
                v.wait_ge(wo_out, B - 1)
                for k, src in enumerate((xs, yg2)):
                    v.wait_ge(gathered[1][k], 16 * C)
                    for c in range(C):
                        last = V.scalar_tensor_tensor(out=x[:, c, :], in0=src[:, c, :], scalar=wts[k][:, c:c + 1],
                                                      in1=x[:, c, :], op0=ALU.mult, op1=ALU.add)
                        if k == 1 and c % CPB == CPB - 1 and c < C - 1:
                            last.then_inc(fin, 1)
                        else:
                            tick(last)
                    sync()

            v.wait_ge(sh_act, 2 * B)
            for piece in FIRST:
                take_piece(piece)
            shared_add(v, 1)
            for step in pack_steps:
                step(0)
            shared_add(v, 2)
            shared_add(v, 3)
            layer_norm1(1, 1, CPB)
            finish0(B - 1)
            layer_norm1(2, 2)
            for gi in range(GROUPS):
                b, g = divmod(gi, G1)
                if gi == BLOCKS_AFTER:
                    block_vectors(v, 1)
                if gi == GROUPS - 2:
                    add_experts()
                for t in range(NT):
                    if gi >= 1 and t == 3:
                        divide(gi - 1)
                    if g == 1 and b >= 1 and t == 2:
                        wo_add(b - 1).then_inc(wo_out, 1)
                    if (gi, t) in BEHIND:
                        take_piece(BEHIND[gi, t])
                    if (gi, t) in PACK:
                        q, step = PACK[gi, t]
                        pack_steps[step](q)
                    if (gi, t) == (2, 4):
                        place(1)
            divide(GROUPS - 1)
            wo_add(B - 1).then_inc(fin, 1)

_INS = ["x", "wq", "wk", "wvT", "wfc", "gamma", "beta", "gate", "shg", "shu", "shd", "experts0",
        "wqkv", "wo", "wgT", "experts1", "const"]


def expert_columns(gate, up, down):
    return np.concatenate([gate.transpose(1, 0, 2), up.transpose(1, 0, 2)], 2), down.reshape(E, 2, P, D).transpose(2, 0, 1, 3).reshape(P, E, 2 * D)


def kernel(L0_attn_inputs, L0_attn_W_Q, L0_attn_W_K, L0_attn_W_V, L0_attn_W_fc, L0_attn_gamma, L0_attn_beta,
           L0_ffn_gate_w, L0_ffn_sh_gate, L0_ffn_sh_up, L0_ffn_sh_down, L0_ffn_rt_gate, L0_ffn_rt_up, L0_ffn_rt_down,
           L1_attn_w_qkv, L1_attn_w_o, L1_ffn_Wg, L1_ffn_W1, L1_ffn_W2, L1_ffn_W3):
    import concourse.bacc as bacc
    from concourse.bass_utils import run_bass_kernel_spmd

    t, a = np.ascontiguousarray, np.asarray
    values = [
        t(L0_attn_inputs), t(L0_attn_W_Q), t(L0_attn_W_K), t(np.asarray(L0_attn_W_V).T), t(L0_attn_W_fc),
        t(L0_attn_gamma), t(L0_attn_beta), t(L0_ffn_gate_w), t(L0_ffn_sh_gate), t(L0_ffn_sh_up), t(L0_ffn_sh_down),
        t(np.concatenate(expert_columns(a(L0_ffn_rt_gate), a(L0_ffn_rt_up), a(L0_ffn_rt_down)), 2).reshape(P, -1)), t(L1_attn_w_qkv), t(L1_attn_w_o),
        t(a(L1_ffn_Wg).T),
        t(np.concatenate([w.reshape(P, -1) for w in
                          expert_columns(*(a(w).transpose(0, 2, 1) for w in (L1_ffn_W1, L1_ffn_W2, L1_ffn_W3)))], 1)),
        constants(),
    ]
    nc = bacc.Bacc("TRN2", target_bir_lowering=False, num_devices=1)
    arrays, args = {}, []
    for name, a in zip(_INS, values):
        arrays[f"in_{name}"] = a
        args.append(nc.dram_tensor(f"in_{name}", a.shape, mybir.dt.from_np(a.dtype), kind="ExternalInput").ap())
    args.append(nc.dram_tensor("out_x", (B, N, D), F32, kind="ExternalOutput").ap())
    build(nc, *args)
    r = run_bass_kernel_spmd(nc, [arrays], core_ids=[0])
    return r.results[0]["out_x"]
```
